# Optimizing a Trainium2 kernel written in Bass

```python
import numpy as np
import jax
import jax.numpy as jnp

def _softmax(x, axis=-1):
    return jax.nn.softmax(x, axis=axis)

def _gelu(x):
    return jax.nn.gelu(x, approximate=True)

def _silu(x):
    return jax.nn.silu(x)

def _sigmoid(x):
    return jax.nn.sigmoid(x)

def _layernorm(x, axis=-1, eps=1e-05):
    m = jnp.mean(x, axis=axis, keepdims=True)
    v = jnp.var(x, axis=axis, keepdims=True)
    return (x - m) / jnp.sqrt(v + eps)

def _scatter_add(tgt, idx, src, axis=0):
    return tgt.at[idx].add(src)

def _segment_sum(src, seg, n):
    return jax.ops.segment_sum(src, seg, n)
kernel_name = 'mk_adj_ffn_d2_adj_r2_054f98'

def setup_inputs(seed: int=0):
    np.random.seed(seed)
    _w = jnp.asarray

    def _rec_inputs():
        import jax
        import jax.numpy as jnp
        _gk = jax.random.key(seed)
        x = 7.22e-05 + 1 * jax.random.normal(jax.random.fold_in(_gk, 1), (64, 128, 128), jnp.float32)
        _a = jax.random.bernoulli(jax.random.fold_in(_gk, 2), 0.125, (64, 128, 128))
        _a = jnp.logical_or(_a, jnp.swapaxes(_a, -1, -2))
        _a = jnp.logical_or(_a, jnp.eye(128, dtype=bool))
        adj = _a.astype(jnp.int32)
        return (x, adj)
    x, adj = _rec_inputs()

    def _L0_gnn_setup():
        import jax, jax.numpy as jnp
        import numpy as np
        NEG_INF = -1000000000.0
        LEAKY_ALPHA = 0.2
        key = jax.random.key(seed)
        k1, k2, k3, k4 = jax.random.split(key, 4)
        B, N, Din, Dout = (16, 1024, 128, 128)
        h = jax.random.normal(k1, (B, N, Din), dtype=jnp.float32)
        adj = jax.random.randint(k2, (B, N, N), 0, 2, dtype=jnp.int32)
        W = jax.random.normal(k3, (Din, Dout), dtype=jnp.float32) * (1.0 / np.sqrt(Din))
        a = jax.random.normal(k4, (2 * Dout,), dtype=jnp.float32) * (1.0 / np.sqrt(2 * Dout))
        return {'h': h, 'adj': adj, 'W': W, 'a': a}
    _L0_gnn_all = _L0_gnn_setup()
    _L0_gnn_in = {k: v for k, v in _L0_gnn_all.items() if k in ('W', 'a')}
    del _L0_gnn_all

    def _L0_ffn_setup():
        import jax, jax.numpy as jnp
        import numpy as np
        E, D, H, TOP_K = (6, 128, 128, 2)
        ROUTER_H = D // 2
        key = jax.random.key(seed)
        ks = jax.random.split(key, 12)
        s = 1.0 / np.sqrt(D)
        sh = 1.0 / np.sqrt(H)
        sr = 1.0 / np.sqrt(ROUTER_H)
        return {'features': jax.random.normal(ks[0], (8, 2048, D), dtype=jnp.float32), 'router_w1': jax.random.uniform(ks[1], (D, ROUTER_H), jnp.float32, -s, s), 'router_b1': jnp.zeros((ROUTER_H,), jnp.float32), 'router_w2': jax.random.uniform(ks[2], (ROUTER_H, E), jnp.float32, -sr, sr), 'router_b2': jnp.zeros((E,), jnp.float32), 'expert_w1': jax.random.uniform(ks[3], (E, D, H), jnp.float32, -s, s), 'expert_b1': jnp.zeros((E, H), jnp.float32), 'expert_w2': jax.random.uniform(ks[4], (E, H, H), jnp.float32, -sh, sh), 'expert_b2': jnp.zeros((E, H), jnp.float32), 'expert_w3': jax.random.uniform(ks[5], (E, H, D), jnp.float32, -sh, sh), 'expert_b3': jnp.zeros((E, D), jnp.float32)}
    _L0_ffn_all = _L0_ffn_setup()
    _L0_ffn_in = {k: v for k, v in _L0_ffn_all.items() if k in ('router_w1', 'router_b1', 'router_w2', 'router_b2', 'expert_w1', 'expert_b1', 'expert_w2', 'expert_b2', 'expert_w3', 'expert_b3')}
    del _L0_ffn_all

    def _L1_gnn_setup():
        import jax, jax.numpy as jnp
        import numpy as np
        NEG_BIG = -9000000000000000.0
        key = jax.random.key(seed)
        k1, k2, k3, k4 = jax.random.split(key, 4)
        B, N, FIN, FOUT = (8, 1024, 128, 128)
        inp = jax.random.normal(k1, (B, N, FIN), dtype=jnp.float32)
        adj = jax.random.randint(k2, (B, N, N), 0, 2, dtype=jnp.int32)
        W = jax.random.normal(k3, (FIN, FOUT), dtype=jnp.float32) * (1.414 / np.sqrt(FIN))
        a = jax.random.normal(k4, (2 * FOUT, 1), dtype=jnp.float32) * 0.1
        return {'input': inp, 'adj': adj, 'W': W, 'a': a}
    _L1_gnn_all = _L1_gnn_setup()
    _L1_gnn_in = {k: v for k, v in _L1_gnn_all.items() if k in ('W', 'a')}
    del _L1_gnn_all

    def _L1_ffn_setup():
        import math
        import jax, jax.numpy as jnp
        import numpy as np
        CAPACITY_FACTOR = 1.25
        TOP_K = 2
        LN_EPS = 1e-05

        def _layer_norm(x, gamma, beta):
            mu = jnp.mean(x, axis=-1, keepdims=True)
            var = jnp.var(x, axis=-1, keepdims=True)
            return (x - mu) * jax.lax.rsqrt(var + LN_EPS) * gamma + beta
        key = jax.random.key(seed)
        ks = jax.random.split(key, 4)
        B, S, D, F, E = (8, 2048, 128, 256, 8)
        x = jax.random.normal(ks[0], (B, S, D), dtype=jnp.float32)
        Wr = jax.random.normal(ks[1], (D, E), dtype=jnp.float32) / np.sqrt(D)
        br = jnp.zeros((E,), jnp.float32)
        W1 = jax.random.normal(ks[2], (E, D, F), dtype=jnp.float32) / np.sqrt(D)
        b1 = jnp.zeros((E, F), jnp.float32)
        W2 = jax.random.normal(ks[3], (E, F, D), dtype=jnp.float32) / np.sqrt(F)
        b2 = jnp.zeros((E, D), jnp.float32)
        gamma = jnp.ones((D,), jnp.float32)
        beta = jnp.zeros((D,), jnp.float32)
        return {'x': x, 'Wr': Wr, 'br': br, 'W1': W1, 'b1': b1, 'W2': W2, 'b2': b2, 'gamma': gamma, 'beta': beta}
    _L1_ffn_all = _L1_ffn_setup()
    _L1_ffn_in = {k: v for k, v in _L1_ffn_all.items() if k in ('Wr', 'br', 'W1', 'b1', 'W2', 'b2', 'gamma', 'beta')}
    del _L1_ffn_all
    return {'x': x, 'adj': adj, 'L0_gnn_W': _L0_gnn_in['W'], 'L0_gnn_a': _L0_gnn_in['a'], 'L0_ffn_router_w1': _L0_ffn_in['router_w1'], 'L0_ffn_router_b1': _L0_ffn_in['router_b1'], 'L0_ffn_router_w2': _L0_ffn_in['router_w2'], 'L0_ffn_router_b2': _L0_ffn_in['router_b2'], 'L0_ffn_expert_w1': _L0_ffn_in['expert_w1'], 'L0_ffn_expert_b1': _L0_ffn_in['expert_b1'], 'L0_ffn_expert_w2': _L0_ffn_in['expert_w2'], 'L0_ffn_expert_b2': _L0_ffn_in['expert_b2'], 'L0_ffn_expert_w3': _L0_ffn_in['expert_w3'], 'L0_ffn_expert_b3': _L0_ffn_in['expert_b3'], 'L1_gnn_W': _L1_gnn_in['W'], 'L1_gnn_a': _L1_gnn_in['a'], 'L1_ffn_Wr': _L1_ffn_in['Wr'], 'L1_ffn_br': _L1_ffn_in['br'], 'L1_ffn_W1': _L1_ffn_in['W1'], 'L1_ffn_b1': _L1_ffn_in['b1'], 'L1_ffn_W2': _L1_ffn_in['W2'], 'L1_ffn_b2': _L1_ffn_in['b2'], 'L1_ffn_gamma': _L1_ffn_in['gamma'], 'L1_ffn_beta': _L1_ffn_in['beta']}

def reference(x, adj, L0_gnn_W, L0_gnn_a, L0_ffn_router_w1, L0_ffn_router_b1, L0_ffn_router_w2, L0_ffn_router_b2, L0_ffn_expert_w1, L0_ffn_expert_b1, L0_ffn_expert_w2, L0_ffn_expert_b2, L0_ffn_expert_w3, L0_ffn_expert_b3, L1_gnn_W, L1_gnn_a, L1_ffn_Wr, L1_ffn_br, L1_ffn_W1, L1_ffn_b1, L1_ffn_W2, L1_ffn_b2, L1_ffn_gamma, L1_ffn_beta):
    import jax
    import jax.numpy as jnp

    def _L0_gnn_ref(h, adj, W, a):
        import jax, jax.numpy as jnp
        import numpy as np
        NEG_INF = -1000000000.0
        LEAKY_ALPHA = 0.2
        Wh = jnp.einsum('bnd,de->bne', h, W)
        Dout = Wh.shape[-1]
        a1, a2 = (a[:Dout], a[Dout:])
        f_i = Wh @ a1
        f_j = Wh @ a2
        e = f_i[:, :, None] + f_j[:, None, :]
        e = jax.nn.leaky_relu(e, negative_slope=LEAKY_ALPHA)
        e = jnp.where(adj > 0, e, NEG_INF)
        alpha = jax.nn.softmax(e, axis=-1)
        out = jnp.einsum('bij,bjd->bid', alpha, Wh)
        return jax.nn.elu(out)

    def _L0_ffn_ref(features, router_w1, router_b1, router_w2, router_b2, expert_w1, expert_b1, expert_w2, expert_b2, expert_w3, expert_b3):
        import jax, jax.numpy as jnp
        import numpy as np
        E, D, H, TOP_K = (6, 128, 128, 2)
        ROUTER_H = D // 2
        rh = jax.nn.relu(features @ router_w1 + router_b1)
        expert_logits = jax.nn.softmax(rh @ router_w2 + router_b2, axis=-1)
        top_w, top_i = jax.lax.top_k(expert_logits, TOP_K)
        routing_weights = jax.nn.softmax(top_w, axis=-1)
        h1 = jax.nn.relu(jnp.einsum('bsd,edh->bseh', features, expert_w1) + expert_b1)
        h2 = jax.nn.relu(jnp.einsum('bseh,ehf->bsef', h1, expert_w2) + expert_b2)
        expert_out = jnp.einsum('bsef,efo->bseo', h2, expert_w3) + expert_b3
        sel = jnp.take_along_axis(expert_out, top_i[:, :, :, None], axis=2)
        combined = jnp.sum(sel * routing_weights[..., None], axis=2)
        return combined

    def _L1_gnn_ref(input, adj, W, a):
        import jax, jax.numpy as jnp
        import numpy as np
        NEG_BIG = -9000000000000000.0
        alpha = 0.2
        h = jnp.matmul(input, W)
        F = h.shape[-1]
        a1, a2 = (a[:F, 0], a[F:, 0])
        s1 = jnp.einsum('bnf,f->bn', h, a1)
        s2 = jnp.einsum('bnf,f->bn', h, a2)
        e = s1[:, :, None] + s2[:, None, :]
        e = jax.nn.leaky_relu(e, negative_slope=alpha)
        e = jnp.where(adj > 0, e, NEG_BIG)
        attention = jax.nn.softmax(e, axis=2)
        h_prime = jnp.matmul(attention, h)
        return jax.nn.elu(h_prime)

    def _L1_ffn_ref(x, Wr, br, W1, b1, W2, b2, gamma, beta):
        import math
        import jax, jax.numpy as jnp
        import numpy as np
        CAPACITY_FACTOR = 1.25
        TOP_K = 2
        LN_EPS = 1e-05

        def _layer_norm(x, gamma, beta):
            mu = jnp.mean(x, axis=-1, keepdims=True)
            var = jnp.var(x, axis=-1, keepdims=True)
            return (x - mu) * jax.lax.rsqrt(var + LN_EPS) * gamma + beta
        B, S, D = x.shape
        E = Wr.shape[1]
        N = B * S
        K = TOP_K
        logits = jnp.mean(x, axis=1) @ Wr + br
        routing_weights = jax.nn.softmax(logits, axis=-1)
        capacity = float(math.ceil(N * CAPACITY_FACTOR / E))
        expected_loads = routing_weights.sum(axis=0) * (N / B)
        scale = jnp.where(expected_loads > capacity, capacity / expected_loads, 1.0)
        routing_weights = jax.nn.softmax(routing_weights * scale, axis=-1)
        rw_tok = jnp.broadcast_to(routing_weights[:, None, :], (B, S, E)).reshape(N, E)
        top_w, top_i = jax.lax.top_k(rw_tok, K)
        top_w = jax.nn.softmax(top_w, axis=-1)
        xf = x.reshape(N, D)
        h = jax.nn.gelu(jnp.einsum('nd,edf->enf', xf, W1) + b1[:, None, :], approximate=False)
        y = jnp.einsum('enf,efd->end', h, W2) + b2[:, None, :]
        w_dense = jnp.zeros((N, E), x.dtype).at[jnp.arange(N)[:, None], top_i].add(top_w)
        out = jnp.einsum('ne,end->nd', w_dense, y).reshape(B, S, D)
        out = _layer_norm(out + x, gamma, beta)
        return out
    x = x + _L0_gnn_ref(_layernorm(x, axis=-1), adj, L0_gnn_W, L0_gnn_a)
    x = x + _L0_ffn_ref(_layernorm(x, axis=-1), L0_ffn_router_w1, L0_ffn_router_b1, L0_ffn_router_w2, L0_ffn_router_b2, L0_ffn_expert_w1, L0_ffn_expert_b1, L0_ffn_expert_w2, L0_ffn_expert_b2, L0_ffn_expert_w3, L0_ffn_expert_b3)
    x = x + _L1_gnn_ref(_layernorm(x, axis=-1), adj, L1_gnn_W, L1_gnn_a)
    x = x + _L1_ffn_ref(_layernorm(x, axis=-1), L1_ffn_Wr, L1_ffn_br, L1_ffn_W1, L1_ffn_b1, L1_ffn_W2, L1_ffn_b2, L1_ffn_gamma, L1_ffn_beta)
    return x

_drawn_inputs = setup_inputs


def setup_inputs(seed=0):
    import zlib

    import numpy as np

    out = dict(_drawn_inputs(seed))
    spreads = {'L0_ffn_router_b1': (0.0, 0.1),
     'L0_ffn_router_b2': (0.0, 0.1),
     'L0_ffn_expert_b1': (0.0, 0.1),
     'L0_ffn_expert_b2': (0.0, 0.1),
     'L0_ffn_expert_b3': (0.0, 0.1),
     'L1_ffn_br': (0.0, 0.1),
     'L1_ffn_b1': (0.0, 0.371),
     'L1_ffn_b2': (0.0, 0.1),
     'L1_ffn_gamma': (1.0, 0.2),
     'L1_ffn_beta': (0.0, 0.1)}
    factors = {}
    for name, (base, spread) in spreads.items():
        noise = np.random.default_rng([zlib.crc32(name.encode()), seed]).standard_normal(out[name].shape)
        drawn = base * np.exp(spread * noise) if base else spread * noise
        out[name] = jnp.asarray(drawn.astype(out[name].dtype))
    for name, factor in factors.items():
        out[name] = (out[name] * factor).astype(out[name].dtype)
    return out
```

```python
import concourse.bass as bass
from concourse import mybir

F32 = mybir.dt.float32
F32R = mybir.dt.float32r
BF16 = mybir.dt.bfloat16
I32 = mybir.dt.int32
U32 = mybir.dt.uint32
ALU = mybir.AluOpType
ACT = mybir.ActivationFunctionType
AX = mybir.AxisListType.X

P = 128
NG = 64
GG = 4
N = NG // GG
GW = GG * P
E0 = 6
RH = 64
E1 = 8
FF = 256
FC = FF // P
SLOPE = 0.2
EPS = 1e-5
MASKED = -5.0e9
CAPACITY = float(-(-NG * P * 5 // (4 * E1)))
SLOTS = 6
ROUTE = 20
LEAD = {"attn0": 2, "route": 1, "experts": 0, "attn1": -1, "pool": -2}


def need(eng, sem, value):
    if not isinstance(value, int) or value > 0:
        eng.wait_ge(sem, value)


def settle(eng, sem, value=1):
    eng.wait_ge(sem, value)


def cols(g):
    return bass.ds(g * GW, GW)


def tiles(ap):
    return ap.rearrange("p (t d) -> p t d", t=GG)


def per_tile(ap):
    return ap.unsqueeze(2).broadcast_to([P, GG, P])


def norm_stage(nc, name):
    st = {}
    st["stats"] = nc.alloc_sbuf_tensor(name + "_stats", [P, GG, 6], F32)
    st["turn"] = nc.alloc_sbuf_tensor(name + "_turn", [P, 1], F32)
    st["mv"] = nc.alloc_sbuf_tensor(name + "_mean_var", [P, GG, 2], F32)
    st["vare"] = nc.alloc_sbuf_tensor(name + "_var_eps", [P, GG], F32)
    st["rstd"] = nc.alloc_sbuf_tensor(name + "_rstd", [P, GG], F32)
    st["stats_ready"] = nc.alloc_semaphore(name + "_stats_ready")
    st["var_ready"] = nc.alloc_semaphore(name + "_var_ready")
    st["vare_ready"] = nc.alloc_semaphore(name + "_vare_ready")
    st["rstd_ready"] = nc.alloc_semaphore(name + "_rstd_ready")
    st["xn_ready"] = nc.alloc_semaphore(name + "_xn_ready")
    return st


def norm_measure(st, v, src, g):
    for t in range(GG):
        last = v.bn_stats(st["stats"][:, t, :], src(t))
    last.then_inc(st["stats_ready"], 1)
    v.wait_ge(st["stats_ready"], g + 1)
    need(v, st["rstd_ready"], g)
    v.tensor_copy(st["turn"][:, :], st["stats"][:, GG - 1, 0:1])
    for t in range(GG):
        last = v.bn_aggr(st["mv"][:, t, :], st["stats"][:, t, :])
    last.then_inc(st["var_ready"], 1)


def norm_root(st, p, eps, minus_half, g):
    p.wait_ge(st["var_ready"], g + 1)
    p.tensor_tensor(st["vare"][:, :], st["mv"][:, :, 1], eps[:, :], ALU.add).then_inc(st["vare_ready"], 1)
    p.wait_ge(st["vare_ready"], g + 1)
    need(p, st["xn_ready"], g)
    p.tensor_tensor(st["rstd"][:, :], st["vare"][:, :], minus_half[:, :], ALU.pow).then_inc(st["rstd_ready"], 1)


def norm_apply(st, v, dst, src, g):
    v.wait_ge(st["rstd_ready"], g + 1)
    for t in range(GG):
        last = v.tensor_scalar(dst(t), src(t), st["mv"][:, t, 0:1], st["rstd"][:, t:t + 1],
                               ALU.subtract, ALU.mult)
    last.then_inc(st["xn_ready"], 1)


def attn_stage(nc, name, bank):
    st = {}
    def sb(what, cols=GW, dt=F32):
        return nc.alloc_sbuf_tensor(name + "_" + what, [P, cols], dt)

    def sem(what):
        return nc.alloc_semaphore(name + "_" + what)

    st["norm"] = norm_stage(nc, name)
    st["bank"] = bank
    st["w"] = sb("w", P)
    st["wT"] = sb("wT", P)
    st["a"] = sb("a", 2)
    st["wa"] = sb("wa", 2)
    st["wa2"] = sb("wa2", P)
    st["xn"] = sb("xn")
    st["xnT"] = sb("xnT")
    st["wh"] = sb("wh")
    st["z"] = sb("z")
    st["lk"] = sb("lk")
    st["pr"] = sb("pr")
    st["prT"] = sb("prT")
    st["fi"] = sb("fi", GG)
    st["mx"] = sb("mx", GG)
    st["nt"] = sb("nt", GG)
    st["nm"] = sb("nm", GG)
    st["sums"] = sb("sums", GG)
    st["rsum"] = sb("rsum", GG)
    st["xnT_done"] = sem("xnT_done")
    st["xnT_ready"] = sem("xnT_ready")
    st["wh_done"] = sem("wh_done")
    st["wh_ready"] = sem("wh_ready")
    st["fi_done"] = sem("fi_done")
    st["fi_ready"] = sem("fi_ready")
    st["z_done"] = sem("z_done")
    st["mx_ready"] = sem("mx_ready")
    st["z_ready"] = sem("z_ready")
    st["nt_ready"] = sem("nt_ready")
    st["nm_ready"] = sem("nm_ready")
    st["lk_ready"] = sem("lk_ready")
    st["pr_ready"] = sem("pr_ready")
    st["prT_done"] = sem("prT_done")
    st["prT_ready"] = sem("prT_ready")
    st["rsum_ready"] = sem("rsum_ready")
    st["agg_done"] = sem("agg_done")
    st["y_ready"] = sem("y_ready")
    st["ymin_ready"] = sem("ymin_ready")
    st["yexp_ready"] = sem("yexp_ready")
    st["elu_ready"] = sem("elu_ready")
    st["x_ready"] = sem("x_ready")
    return st


def attn_pe_transpose_xn(st, pe, ident, g):
    pe.wait_ge(st["norm"]["xn_ready"], g + 1)
    need(pe, st["y_ready"], g)
    for t in range(GG):
        last = pe.transpose(st["bank"][:, t * P:(t + 1) * P], st["xn"][:, t * P:(t + 1) * P], ident[:, :])
    last.then_inc(st["xnT_done"], 1)


def attn_pe_project(st, pe, small, g):
    pe.wait_ge(st["xnT_ready"], g + 1)
    for t in range(GG):
        last = pe.matmul(st["bank"][:, t * P:(t + 1) * P], st["xnT"][:, t * P:(t + 1) * P], st["w"][:, :],
                         start=True, stop=True)
    last.then_inc(st["wh_done"], 1)
    for t in range(GG):
        last = pe.matmul(small[:, t:t + 1], st["xnT"][:, t * P:(t + 1) * P], st["wa"][:, 0:1],
                         start=True, stop=True)
    last.then_inc(st["fi_done"], 1)


def attn_pe_scores(st, pe, identb, mask, g):
    pe.wait_ge(st["wh_ready"], g + 1)
    pe.matmul(st["bank"][:, :], st["wa2"][:, :], st["xnT"][:, :], start=True, stop=False)
    pe.matmul(st["bank"][:, :], identb[:, :], mask[:, cols(g)], start=False, stop=True).then_inc(st["z_done"], 1)


def attn_pe_transpose_probs(st, pe, ident, g):
    pe.wait_ge(st["pr_ready"], g + 1)
    pe.wait_ge(st["z_ready"], g + 1)
    for t in range(GG):
        last = pe.transpose(st["bank"][:, t * P:(t + 1) * P], st["pr"][:, t * P:(t + 1) * P], ident[:, :])
    last.then_inc(st["prT_done"], 1)


def attn_pe_aggregate(st, pe, g):
    pe.wait_ge(st["prT_ready"], g + 1)
    for t in range(GG):
        s = slice(t * P, (t + 1) * P)
        last = pe.matmul(st["bank"][:, s], st["prT"][:, s], st["wh"][:, s], start=True, stop=True)
    last.then_inc(st["agg_done"], 1)

def attn_act_xnT(st, a, g):
    a.wait_ge(st["xnT_done"], g + 1)
    need(a, st["z_done"], g)
    a.activation(st["xnT"][:, :], st["bank"][:, :], ACT.Copy).then_inc(st["xnT_ready"], 1)


def attn_act_wh(st, a, g):
    a.wait_ge(st["wh_done"], g + 1)
    need(a, st["agg_done"], g)
    a.activation(st["wh"][:, :], st["bank"][:, :], ACT.Copy).then_inc(st["wh_ready"], 1)


def attn_act_exp(st, a, g):
    a.wait_ge(st["lk_ready"], g + 1)
    a.wait_ge(st["nm_ready"], g + 1)
    need(a, st["elu_ready"], g)
    for t in range(GG):
        s = slice(t * P, (t + 1) * P)
        last = a.activation(st["pr"][:, s], st["lk"][:, s], ACT.Exp, bias=st["nm"][:, t:t + 1],
                            accum_out=st["sums"][:, t:t + 1])
    last.then_inc(st["pr_ready"], 1)


def attn_act_prT(st, a, g):
    a.wait_ge(st["prT_done"], g + 1)
    need(a, st["x_ready"], g)
    a.activation(st["prT"][:, :], st["bank"][:, :], ACT.Copy).then_inc(st["prT_ready"], 1)


def attn_act_elu(st, a, g):
    a.wait_ge(st["ymin_ready"], g + 1)
    a.activation(st["pr"][:, :], st["lk"][:, :], ACT.Exp).then_inc(st["yexp_ready"], 1)

def attn_dve_fi(st, v, small, g):
    v.wait_ge(st["fi_done"], g + 1)
    v.tensor_copy(st["fi"][:, :], small[:, 0:GG]).then_inc(st["fi_ready"], 1)


def attn_dve_scores(st, v, g):
    v.wait_ge(st["z_done"], g + 1)
    v.wait_ge(st["fi_ready"], g + 1)
    v.tensor_reduce(st["mx"][:, :], tiles(st["bank"][:, :]), AX, ALU.max).then_inc(st["mx_ready"], 1)
    v.tensor_tensor(tiles(st["z"][:, :]), tiles(st["bank"][:, :]), per_tile(st["fi"][:, :]), ALU.add)\
        .then_inc(st["z_ready"], 1)
    v.wait_ge(st["mx_ready"], g + 1)
    v.scalar_tensor_tensor(st["nt"][:, :], st["mx"][:, :], -1.0, st["fi"][:, :], ALU.mult, ALU.subtract)\
        .then_inc(st["nt_ready"], 1)
    v.wait_ge(st["z_ready"], g + 1)
    v.scalar_tensor_tensor(st["lk"][:, :], st["z"][:, :], SLOPE, st["z"][:, :], ALU.mult, ALU.max)\
        .then_inc(st["lk_ready"], 1)
    v.wait_ge(st["nt_ready"], g + 1)
    v.scalar_tensor_tensor(st["nm"][:, :], st["nt"][:, :], SLOPE, st["nt"][:, :], ALU.mult, ALU.min)\
        .then_inc(st["nm_ready"], 1)


def attn_dve_rsum(st, v, g):
    v.wait_ge(st["pr_ready"], g + 1)
    v.reciprocal(st["rsum"][:, :], st["sums"][:, :]).then_inc(st["rsum_ready"], 1)


def attn_dve_y(st, v, g):
    v.wait_ge(st["agg_done"], g + 1)
    v.wait_ge(st["rsum_ready"], g + 1)
    v.tensor_tensor(tiles(st["z"][:, :]), tiles(st["bank"][:, :]), per_tile(st["rsum"][:, :]), ALU.mult)\
        .then_inc(st["y_ready"], 1)
    v.wait_ge(st["y_ready"], g + 1)
    v.tensor_scalar(st["lk"][:, :], st["z"][:, :], 0.0, None, ALU.min).then_inc(st["ymin_ready"], 1)


def attn_dve_elu(st, v, g):
    v.wait_ge(st["yexp_ready"], g + 1)
    v.scalar_tensor_tensor(st["prT"][:, :], st["pr"][:, :], -1.0, st["z"][:, :], ALU.add, ALU.max)\
        .then_inc(st["elu_ready"], 1)

def attn_pool_residual(st, p, x, g):
    p.wait_ge(st["elu_ready"], g + 1)
    p.tensor_tensor(x[:, cols(g)], x[:, cols(g)], st["prT"][:, :], ALU.add).then_inc(st["x_ready"], 1)


def build(nc, A, out):
    def sb(name, shape, dt=F32):
        return nc.alloc_sbuf_tensor(name, shape, dt)

    def sem(name):
        return nc.alloc_semaphore(name)

    bank = [nc.alloc_psum_tensor("bank%d" % b, [P, GW], F32) for b in range(8)]
    b_h2, b_h1, b_out, b_wts, b_at0, b_small, b_at1, b_misc = bank

    const_ready = sem("const_ready")

    x = sb("x", [P, NG * P])
    mean3 = sb("mean3", [P, NG])
    rstd3 = sb("rstd3", [P, NG])
    xnT3 = sb("xnT3", [P, NG * P])
    mask = sb("mask", [P, NG * P], BF16)
    adj_in = sb("adj_in", [P, 2, GW], I32)
    ident = sb("ident", [P, P])
    identb = sb("identb", [P, P], BF16)
    ones = sb("ones", [P, P])
    minus_half = sb("minus_half", [P, GG])
    eps = sb("eps", [P, GG])
    lower = sb("lower", [P, E0, E0])
    upper = sb("upper", [P, E0, E0])
    pick = sb("pick", [3 * E0, E0, P], BF16)

    at0 = attn_stage(nc, "at0", b_at0)
    at1 = attn_stage(nc, "at1", b_at1)
    rn = norm_stage(nc, "route")
    pn = norm_stage(nc, "pool")
    r_xn = sb("r_xn", [P, GW])
    p_xn = sb("p_xn", [P, GW])
    xnTh = sb("xnTh", [P, 2, GW], F32R)
    xnTl = sb("xnTl", [P, 2, GW], F32R)
    rw1h = sb("rw1h", [P, RH], F32R)
    rw1l = sb("rw1l", [P, RH], F32R)
    rb1 = sb("rb1", [RH, 1])
    rh = sb("rh", [RH + 1, GW])
    rw2 = sb("rw2", [RH + 1, E0])
    w1h = sb("w1h", [P, E0 * P], F32R)
    w1l = sb("w1l", [P, E0 * P], F32R)
    w2 = sb("w2", [P, E0, P])
    w3 = sb("w3", [P, E0, P])
    b1 = sb("b1", [P, E0])
    b2 = sb("b2", [P, E0])
    b3 = sb("b3", [3 * E0, P])
    b3r = sb("b3r", [3 * E0, 2, P])
    b3p = sb("b3p", [3 * E0, 3, P], BF16)
    h1 = sb("h1", [P, 2, GW])
    h2 = sb("h2", [P, 2, GW])
    h2w = sb("h2w", [P, 2, GW])
    lg = sb("lg", [P, GG, E0])
    lgmx = sb("lgmx", [P, GG])
    lgd = sb("lgd", [P, GG, E0])
    pe0 = sb("pe0", [P, GG, E0])
    psum_ = sb("p_sum", [P, GG])
    prc = sb("p_rcp", [P, GG])
    prob = sb("prob", [P, GG, E0])
    ge = sb("ge", [P, GG, E0, E0])
    gt = sb("gt", [P, GG, E0, E0])
    rank = sb("rank", [P, GG * E0])
    pd = sb("pd", [P, GG, E0])
    pq = sb("pq", [P, GG, E0])
    pqs = sb("pqs", [P, GG, E0])
    qsum = sb("qsum", [P, GG])
    qrc = sb("qrc", [P, GG])
    wgt = sb("wgt", [P, GG, E0])
    wr1 = sb("wr1", [P, GG, E0])
    wparts = sb("wparts", [P, GG, 3, E0], BF16)
    wpT = sb("wpT", [3 * E0, 2, GW], BF16)

    W1 = sb("W1", [P, E1, FF + FC])
    W2 = sb("W2", [P, E1, FF])
    msum = sb("msum", [P, NG])
    wr = sb("wr", [P, E1])
    br = sb("br", [NG, E1])
    B2 = sb("B2", [E1, P])
    gamma = sb("gamma", [P, P])
    beta = sb("beta", [P, P])
    iota8 = sb("iota8", [NG, E1])
    hd = sb("hd", [NG, 12, E1])
    top8 = sb("top8", [NG, 8])
    top8i = sb("top8i", [NG, 8], U32)
    pairs = sb("pairs", [NG, 4])
    diag = sb("diag", [NG, 4, NG])
    gw = sb("gw", [P, 2 * NG])
    gidx = sb("gidx", [P, 2 * NG], I32)
    wdT = sb("wdT", [E1, NG])
    bias2 = sb("bias2", [NG, P])
    fn = norm_stage(nc, "final")

    bias2_dram = nc.dram_tensor("bias2_scratch", (NG, P), F32).ap()

    w1c = [sb("w1c%d" % j, [P, 2, FF + FC]) for j in range(2)]
    w2c = [at0["wh"], at0["z"]]
    hid = [at0["lk"], at0["pr"]]
    b2b = [at0["prT"], at0["xn"]]
    res = at1["xn"]
    xb = [at1["xnT"], at1["wh"]]
    sm = [at1["z"], at1["lk"]]
    fin = [at1["pr"], at1["prT"]]

    x_loaded = sem("x_loaded")
    adj_loaded = sem("adj_loaded")
    small_loaded = sem("small_loaded")
    early_loaded = sem("early_loaded")
    late_loaded = sem("late_loaded")
    const_step = sem("const_step")
    wT_done = sem("wT_done")
    wT_ready = sem("wT_ready")
    wa_done = sem("wa_done")
    wa_ready = sem("wa_ready")
    split_step = sem("split_step")
    mask_ready = sem("mask_ready")
    r_xnT_done = sem("r_xnT_done")
    xnTh_ready = sem("xnTh_ready")
    xnTl_ready = sem("xnTl_ready")
    rh_done = sem("rh_done")
    rh_ready = sem("rh_ready")
    lg_done = sem("lg_done")
    lg_ready = sem("lg_ready")
    route_step = sem("route_step")
    pe0_ready = sem("pe0_ready")
    pq_ready = sem("pq_ready")
    wpT_done = sem("wpT_done")
    wpT_ready = sem("wpT_ready")
    l1_done = sem("l1_done")
    l2_done = sem("l2_done")
    l3_done = sem("l3_done")
    h1_ready = sem("h1_ready")
    h2_ready = sem("h2_ready")
    wb_done = sem("wb_done")
    h2w_ready = sem("h2w_ready")
    x_experts_ready = sem("x_experts_ready")
    p_xnT_done = sem("p_xnT_done")
    xnT3_ready = sem("xnT3_ready")
    msum_ready = sem("msum_ready")
    moments_ready = sem("moments_ready")
    res_normed = sem("res_normed")

    head_pe = sem("head_pe")
    head_act = sem("head_act")
    head_dve = sem("head_dve")
    gw_ready = sem("gw_ready")
    gidx_ready = sem("gidx_ready")
    bias2_stored = sem("bias2_stored")
    b2b_loaded = sem("b2b_loaded")
    w1c_ready = sem("w1c_ready")
    w2c_ready = sem("w2c_ready")
    up_done = sem("up_done")
    gelu_ready = sem("gelu_ready")
    down_done = sem("down_done")
    res_ready = sem("res_ready")
    xb_ready = sem("xb_ready")
    sum_ready = sem("sum_ready")
    scaled_ready = sem("scaled_ready")
    fin_ready = sem("fin_ready")
    stored = sem("stored")

    EARLY = 16 * 6
    SMALL = 16 * 10
    LATE = 16 * 10

    def rounds(eng, body):
        for i in range(-2, 3):
            body(i, i)
        with eng.Fori(3, N - 4, 2) as i:
            body(i, 3)
            body(i + 1, 4)
        for i in range(N - 3, N + 2):
            body(i, i)

    def live(stage, i0, shift=0):
        return 0 <= i0 + LEAD[stage] + shift < N

    def newest(i, i0, stage):
        lead = LEAD[stage] + 1
        if isinstance(i, int):
            return max(0, min(i + lead, N))
        return i + lead

    with nc.Block() as block:

        @block.sync
        def _(sp):
            xg = A["x"].rearrange("(g t) p d -> g p t d", t=GG)
            ag = A["adj"].rearrange("(g t) p d -> g p t d", t=GG)

            def load(g, par):
                settle(sp, const_ready)
                need(sp, x_loaded, 16 * g)
                sp.dma_start(tiles(x[:, cols(g)]), xg[g] if isinstance(g, int) else
                             xg[bass.ds(g, 1)].rearrange("a p t d -> p (a t) d")).then_inc(x_loaded, 16)
                settle(sp, const_ready)
                need(sp, adj_loaded, 16 * g)
                need(sp, mask_ready, g - 1)
                sp.dma_start(tiles(adj_in[:, par, :]), ag[g] if isinstance(g, int) else
                             ag[bass.ds(g, 1)].rearrange("a p t d -> p (a t) d")).then_inc(adj_loaded, 16)

            load(0, 0)
            sp.dma_start(at0["w"][:, :], A["L0_gnn_W"]).then_inc(early_loaded, 16)
            sp.dma_start(at1["w"][:, :], A["L1_gnn_W"]).then_inc(early_loaded, 16)
            load(1, 1)
            with sp.Fori(2, N - 1, 2) as g:
                load(g, 0)
                load(g + 1, 1)

            sp.wait_ge(head_dve, 31)
            sp.dma_start(bias2_dram, bias2[:, :]).then_inc(bias2_stored, 16)
            sp.wait_ge(bias2_stored, 16)
            b2g = bias2_dram.rearrange("(g t) d -> g (t d)", t=GG)
            outg = out.rearrange("(g t) p d -> g p t d", t=GG)

            def load_bias(g, par):
                settle(sp, const_ready)
                need(sp, res_ready, g - 1)
                need(sp, b2b_loaded, 16 * g)
                row = b2g[g] if isinstance(g, int) else b2g[bass.ds(g, 1)].rearrange("a d -> (a d)")
                sp.dma_start(b2b[par][:, :], row.partition_broadcast(P)).then_inc(b2b_loaded, 16)

            def store(g, par):
                settle(sp, const_ready)
                sp.wait_ge(fin_ready, g + 1)
                need(sp, stored, 16 * g)
                dst = outg[g] if isinstance(g, int) else outg[bass.ds(g, 1)].rearrange("a p t d -> p (a t) d")
                sp.dma_start(dst, tiles(fin[par][:, :])).then_inc(stored, 16)

            load_bias(0, 0)
            load_bias(1, 1)
            for g in range(2, 4):
                store(g - 2, g % 2)
                load_bias(g, g % 2)
            with sp.Fori(4, N - 1, 2) as g:
                store(g - 2, 0)
                load_bias(g, 0)
                store(g - 1, 1)
                load_bias(g + 1, 1)
            store(N - 2, 0)
            store(N - 1, 1)
            sp.wait_ge(stored, 16 * N)

        @block.gpsimd
        def _(p):
            p.memset(minus_half[:, :], -0.5).then_inc(const_ready, 1)
            p.memset(eps[:, :], EPS).then_inc(const_ready, 1)
            p.memset(ones[:, :], 1.0).then_inc(const_ready, 1)
            p.memset(ident[:, :], 0.0).then_inc(const_step, 1)
            p.memset(identb[:, :], 0.0).then_inc(const_step, 1)
            p.memset(lower[:, :, :], 1.0).then_inc(const_step, 1)
            p.memset(upper[:, :, :], 1.0).then_inc(const_step, 1)
            p.memset(pick[:, :, :], 0.0).then_inc(const_step, 1)
            p.iota(iota8[:, :], pattern=[[1, E1]], base=0, channel_multiplier=0,
                   allow_small_or_imprecise_dtypes=True).then_inc(const_ready, 1)
            p.wait_ge(const_step, 5)
            for m in (ident, identb):
                p.affine_select(out=m[:, :], in_=m[:, :], compare_op=ALU.not_equal, fill=1.0, base=0,
                                pattern=[[-1, P]], channel_multiplier=1).then_inc(const_ready, 1)
            p.affine_select(out=lower[:, :, :], in_=lower[:, :, :], compare_op=ALU.is_gt, fill=0.0, base=0,
                            pattern=[[1, E0], [-1, E0]], channel_multiplier=0).then_inc(const_ready, 1)
            p.affine_select(out=upper[:, :, :], in_=upper[:, :, :], compare_op=ALU.is_gt, fill=0.0, base=0,
                            pattern=[[-1, E0], [1, E0]], channel_multiplier=0).then_inc(const_ready, 1)
            for q in range(3):
                p.wait_ge(const_step, 5 + q)
                p.affine_select(out=pick[:, :, :], in_=pick[:, :, :], compare_op=ALU.not_equal, fill=1.0,
                                base=-q * E0, pattern=[[-1, E0], [0, P]], channel_multiplier=1)\
                    .then_inc(const_step, 1)
            p.wait_ge(const_ready, 8)
            w2d = A["L1_ffn_W2"].rearrange("e (c f) d -> f e c d", c=FC)
            p.dma_start(W1[:, :, 0:FF], A["L1_ffn_W1"].rearrange("e d f -> d e f")).then_inc(late_loaded, 16)
            for c in range(FC):
                p.dma_start(W2[:, :, c * P:(c + 1) * P], w2d[:, :, c, :]).then_inc(late_loaded, 16)
            with nc.allow_non_contiguous_dma(reason="bias columns, once"):
                for c in range(FC):
                    p.dma_start(W1[:, :, FF + c], A["L1_ffn_b1"][:, c * P:(c + 1) * P].rearrange("e p -> p e"))\
                        .then_inc(late_loaded, 16)
            p.dma_start(wr[:, :], A["L1_ffn_Wr"]).then_inc(late_loaded, 16)
            p.dma_start(br[:, :], A["L1_ffn_br"].partition_broadcast(NG)).then_inc(late_loaded, 16)
            p.dma_start(B2[:, :], A["L1_ffn_b2"]).then_inc(late_loaded, 16)
            p.dma_start(gamma[:, :], A["L1_ffn_gamma"].partition_broadcast(P)).then_inc(late_loaded, 16)
            p.dma_start(beta[:, :], A["L1_ffn_beta"].partition_broadcast(P)).then_inc(late_loaded, 16)

            def body(i, i0):
                if live("attn0", i0):
                    norm_root(at0["norm"], p, eps, minus_half, i + 2)
                if live("attn0", i0, -1):
                    attn_pool_residual(at0, p, x, i + 1)
                if live("attn1", i0):
                    norm_root(at1["norm"], p, eps, minus_half, i - 1)
                if live("route", i0):
                    norm_root(rn, p, eps, minus_half, i + 1)
                if live("attn1", i0, -1):
                    attn_pool_residual(at1, p, x, i - 2)
                if live("pool", i0):
                    g = i - 2
                    norm_root(pn, p, eps, minus_half, g)
                    p.wait_ge(pn["rstd_ready"], g + 1)
                    p.tensor_copy(mean3[:, bass.ds(g * GG, GG)], pn["mv"][:, :, 0])
                    p.tensor_copy(rstd3[:, bass.ds(g * GG, GG)], pn["rstd"][:, :]).then_inc(moments_ready, 1)

            rounds(p, body)

            p.wait_ge(late_loaded, LATE)
            p.wait_ge(gidx_ready, 1)

            def choose_w1(m, par):
                need(p, gelu_ready, m - 1)
                for k in range(2):
                    e = p.value_load(gidx[0:1, bass.ds(m + k * NG, 1)], min_val=0, max_val=E1 - 1)
                    last = p.tensor_copy(w1c[par][:, k, :], W1[:, bass.ds(e, 1), :].rearrange("p a f -> p (a f)"))
                last.then_inc(w1c_ready, 1)

            def group(g, g0, par):
                for t in range(GG):
                    choose_w1(GG * g + t, t % 2)
                    if t == 1 and g0 > 0:
                        norm_root(fn, p, eps, minus_half, g - 1)
                    if t == 2:
                        p.wait_ge(b2b_loaded, 16 * g + 16)
                        p.wait_ge(res_normed, g + 1)
                        p.tensor_tensor(res[:, :], res[:, :], b2b[par][:, :], ALU.add).then_inc(res_ready, 1)
                    if t == 0:
                        need(p, fin_ready, g - 1)
                        p.tensor_tensor(tiles(xb[par][:, :]), tiles(x[:, cols(g)]),
                                        beta[:, :].unsqueeze(1).broadcast_to([P, GG, P]), ALU.add)\
                            .then_inc(xb_ready, 1)
                    if t == 3 and g0 > 0:
                        finish(g - 1, 1 - par)

            def finish(g, par):
                p.wait_ge(fn["xn_ready"], g + 1)
                p.tensor_tensor(tiles(sm[par][:, :]), tiles(sm[par][:, :]),
                                gamma[:, :].unsqueeze(1).broadcast_to([P, GG, P]), ALU.mult)\
                    .then_inc(scaled_ready, 1)
                p.wait_ge(scaled_ready, g + 1)
                p.wait_ge(xb_ready, g + 1)
                need(p, stored, 16 * (g - 1))
                p.tensor_tensor(fin[par][:, :], sm[par][:, :], xb[par][:, :], ALU.add).then_inc(fin_ready, 1)

            for g in range(4):
                group(g, g, g % 2)
            with p.Fori(4, N - 1, 2) as g:
                group(g, 4, 0)
                group(g + 1, 5, 1)
            norm_root(fn, p, eps, minus_half, N - 1)
            finish(N - 1, 1)

        @block.scalar
        def _(a):
            with nc.allow_non_contiguous_dma(reason="bias columns, once"):
                a.dma_start(at0["a"][:, :], A["L0_gnn_a"].rearrange("(t p) -> p t", p=P)).then_inc(early_loaded, 16)
                a.dma_start(at1["a"][:, :], A["L1_gnn_a"].rearrange("(t p) a -> p (t a)", p=P))\
                    .then_inc(early_loaded, 16)
                a.dma_start(h1[:, :, :].rearrange("p a f -> p (a f)")[:, 0:E0 * P],
                            A["L0_ffn_expert_w1"].rearrange("e d h -> d e h")).then_inc(early_loaded, 16)
                a.dma_start(h2[:, 0, 0:RH], A["L0_ffn_router_w1"]).then_inc(early_loaded, 16)
                a.dma_start(rb1[:, :], A["L0_ffn_router_b1"].unsqueeze(1)).then_inc(small_loaded, 16)
                a.dma_start(rw2[0:RH, :], A["L0_ffn_router_w2"]).then_inc(small_loaded, 16)
                a.dma_start(rw2[RH:RH + 1, :], A["L0_ffn_router_b2"].unsqueeze(0)).then_inc(small_loaded, 16)
                a.dma_start(b1[:, :], A["L0_ffn_expert_b1"].rearrange("e p -> p e")).then_inc(small_loaded, 16)
                a.dma_start(b2[:, :], A["L0_ffn_expert_b2"].rearrange("e p -> p e")).then_inc(small_loaded, 16)
                for q in range(3):
                    a.dma_start(b3[q * E0:(q + 1) * E0, :], A["L0_ffn_expert_b3"]).then_inc(small_loaded, 16)
                a.dma_start(w2[:, :, :], A["L0_ffn_expert_w2"].rearrange("e d h -> d e h"))\
                    .then_inc(small_loaded, 16)
                a.dma_start(w3[:, :, :], A["L0_ffn_expert_w3"].rearrange("e d h -> d e h"))\
                    .then_inc(small_loaded, 16)

            def relu2(n, e):
                a.wait_ge(l2_done, n + 1)
                need(a, h2w_ready, n - 1)
                a.activation(h2[:, e % 2, :], b_h2[:, :], ACT.Relu, bias=b2[:, e:e + 1]).then_inc(h2_ready, 1)

            def relu1(n, e):
                a.wait_ge(l1_done, n + 1)
                a.activation(h1[:, e % 2, :], b_h1[:, :], ACT.Relu, bias=b1[:, e:e + 1]).then_inc(h1_ready, 1)

            a.wait_ge(small_loaded, SMALL)
            a.wait_ge(split_step, 9)

            def body(i, i0):
                run = live("experts", i0)
                for s in range(SLOTS):
                    n = i * E0 + s
                    if run:
                        relu2(n, s)
                    if s == 0 and live("attn1", i0, -1):
                        attn_act_prT(at1, a, i - 2)
                    if run and s < SLOTS - 1:
                        relu1(n + 1, s + 1)
                    if s == SLOTS - 1 and live("experts", i0, 1):
                        relu1(n + 1, 0)
                    if s == 0 and live("attn0", i0, -1):
                        attn_act_elu(at0, a, i + 1)
                    if s == 1 and live("attn0", i0):
                        attn_act_xnT(at0, a, i + 2)
                    if s == 1 and live("attn1", i0, -1):
                        attn_act_elu(at1, a, i - 2)
                    if s == 2:
                        if live("attn1", i0):
                            attn_act_xnT(at1, a, i - 1)
                        if live("route", i0):
                            g = i + 1
                            a.wait_ge(r_xnT_done, g + 1)
                            need(a, l1_done, (g - 1) * E0)
                            a.activation(xnTh[:, (i0 + 1) % 2, :], b_misc[:, :], ACT.Copy)\
                                .then_inc(xnTh_ready, 1)
                        if live("attn0", i0):
                            attn_act_wh(at0, a, i + 2)
                    if s == 3:
                        if live("route", i0):
                            g = i + 1
                            a.wait_ge(rh_done, g + 1)
                            need(a, lg_done, g)
                            a.activation(rh[0:RH, :], b_misc[0:RH, :], ACT.Relu, bias=rb1[:, :])\
                                .then_inc(rh_ready, 1)
                        if live("attn1", i0):
                            attn_act_wh(at1, a, i - 1)
                    if s == 4:
                        if live("attn0", i0):
                            attn_act_exp(at0, a, i + 2)
                        if live("route", i0):
                            g = i + 1
                            a.wait_ge(route_step, ROUTE * g + 2)
                            a.activation(pe0[:, :, :], lgd[:, :, :], ACT.Exp).then_inc(pe0_ready, 1)
                    if s == 5:
                        if live("attn0", i0):
                            attn_act_prT(at0, a, i + 2)
                        if live("attn1", i0):
                            attn_act_exp(at1, a, i - 1)
                        if live("pool", i0):
                            g = i - 2
                            a.wait_ge(p_xnT_done, g + 1)
                            a.activation(xnT3[:, cols(g)], b_misc[:, :], ACT.Copy).then_inc(xnT3_ready, 1)
                        if live("route", i0):
                            g = i + 1
                            a.wait_ge(route_step, ROUTE * g + 12)
                            a.activation(pq[:, :, :], pd[:, :, :], ACT.Exp).then_inc(pq_ready, 1)

            rounds(a, body)

            for at, dst, src in ((3, hd[:, 3, :], hd[:, 1, :]), (12, hd[:, 8, :], hd[:, 7, :]),
                                 (19, hd[:, 11, 0:2], hd[:, 10, 0:2])):
                a.wait_ge(head_dve, at)
                a.activation(dst, src, ACT.Exp).then_inc(head_act, 1)

            def gelus(m, par):
                a.wait_ge(up_done, m + 1)
                need(a, down_done, m - 1)
                for k in range(2):
                    for c in range(FC):
                        s = slice((FC * k + c) * P, (FC * k + c + 1) * P)
                        last = a.activation(hid[par][:, s], bank[par][:, s], ACT.Gelu,
                                            bias=w1c[par][:, k, FF + c:FF + c + 1])
                last.then_inc(gelu_ready, 1)

            for m in range(4):
                gelus(m, m % 2)
            with a.Fori(4, NG - 1, 2) as m:
                gelus(m, 0)
                gelus(m + 1, 1)

        @block.vector
        def _(v):
            v.wait_ge(early_loaded, EARLY)
            raw = h1[:, :, :].rearrange("p a f -> p (a f)")[:, 0:E0 * P]
            v.tensor_copy(w1h[:, :], raw).then_inc(split_step, 1)
            v.tensor_copy(rw1h[:, :], h2[:, 0, 0:RH]).then_inc(split_step, 1)
            v.wait_ge(split_step, 2)
            v.tensor_tensor(w1l[:, :], raw, w1h[:, :].bitcast(F32), ALU.subtract).then_inc(split_step, 1)
            v.tensor_tensor(rw1l[:, :], h2[:, 0, 0:RH], rw1h[:, :].bitcast(F32), ALU.subtract)\
                .then_inc(split_step, 1)
            for j, at in enumerate((at0, at1)):
                v.wait_ge(wT_done, j + 1)
                v.tensor_copy(at["wT"][:, :], at["bank"][:, 0:P]).then_inc(wT_ready, 1)
            for j, at in enumerate((at0, at1)):
                v.wait_ge(wa_done, 2)
                v.tensor_copy(at["wa"][:, :], b_misc[:, 2 * j:2 * j + 2]).then_inc(wa_ready, 1)
            v.wait_ge(wa_ready, 2)
            v.wait_ge(const_ready, 8)
            for at in (at0, at1):
                v.tensor_scalar(at["wa2"][:, :], ones[:, :], at["wa"][:, 1:2], None, ALU.mult).then_inc(wa_ready, 1)
            v.wait_ge(small_loaded, SMALL)
            v.tensor_copy(b3p[:, 0, :], b3[:, :]).then_inc(split_step, 1)
            v.wait_ge(split_step, 5)
            v.tensor_tensor(b3r[:, 0, :], b3[:, :], b3p[:, 0, :], ALU.subtract).then_inc(split_step, 1)
            v.wait_ge(split_step, 6)
            v.tensor_copy(b3p[:, 1, :], b3r[:, 0, :]).then_inc(split_step, 1)
            v.wait_ge(split_step, 7)
            v.tensor_tensor(b3p[:, 2, :], b3r[:, 0, :], b3p[:, 1, :], ALU.subtract).then_inc(split_step, 1)
            v.memset(rh[RH:RH + 1, :], 1.0).then_inc(split_step, 1)

            def x_tile(g):
                return lambda t: x[:, bass.ds(g * GW + t * P, P)]

            def buf_tile(buf):
                return lambda t: buf[:, t * P:(t + 1) * P]

            def make_mask(g, par):
                v.wait_ge(adj_loaded, 16 * g + 16)
                v.tensor_scalar(mask[:, cols(g)], adj_in[:, par, :], 0.0, MASKED, ALU.is_le, ALU.mult)\
                    .then_inc(mask_ready, 1)

            def weigh(n, e):
                v.wait_ge(h2_ready, n + 1)
                v.wait_ge(wb_done, n + 1)
                need(v, l3_done, n - 1)
                v.tensor_tensor(h2w[:, e % 2, :], h2[:, e % 2, :], b_wts[:, :], ALU.mult).then_inc(h2w_ready, 1)

            def route_first(g):
                base = ROUTE * g
                v.wait_ge(lg_done, g + 1)
                v.tensor_copy(lg[:, :, :], b_misc[:, 0:GG * E0].rearrange("p (t e) -> p t e", t=GG))\
                    .then_inc(lg_ready, 1)
                v.wait_ge(lg_ready, g + 1)
                v.tensor_reduce(lgmx[:, :], lg[:, :, :], AX, ALU.max).then_inc(route_step, 1)
                v.wait_ge(route_step, base + 1)
                v.tensor_tensor(lgd[:, :, :], lg[:, :, :], lgmx[:, :].unsqueeze(2).broadcast_to([P, GG, E0]),
                                ALU.subtract).then_inc(route_step, 1)

            def route_rank(g):
                base = ROUTE * g
                v.wait_ge(pe0_ready, g + 1)
                v.tensor_reduce(psum_[:, :], pe0[:, :, :], AX, ALU.add).then_inc(route_step, 1)
                v.wait_ge(route_step, base + 3)
                v.reciprocal(prc[:, :], psum_[:, :]).then_inc(route_step, 1)
                v.wait_ge(route_step, base + 4)
                v.tensor_tensor(prob[:, :, :], pe0[:, :, :], prc[:, :].unsqueeze(2).broadcast_to([P, GG, E0]),
                                ALU.mult).then_inc(route_step, 1)
                v.wait_ge(route_step, base + 5)
                mine = prob[:, :, :].unsqueeze(3).broadcast_to([P, GG, E0, E0])
                other = prob[:, :, :].unsqueeze(2).broadcast_to([P, GG, E0, E0])
                v.tensor_tensor(ge[:, :, :, :], other, mine, ALU.is_ge).then_inc(route_step, 1)
                v.tensor_tensor(gt[:, :, :, :], other, mine, ALU.is_gt).then_inc(route_step, 1)
                lo = lower[:, :, :].rearrange("p a b -> p (a b)").unsqueeze(1).broadcast_to([P, GG, E0 * E0])
                up = upper[:, :, :].rearrange("p a b -> p (a b)").unsqueeze(1).broadcast_to([P, GG, E0 * E0])
                ge3 = ge[:, :, :, :].rearrange("p t a b -> p t (a b)")
                gt3 = gt[:, :, :, :].rearrange("p t a b -> p t (a b)")
                v.wait_ge(route_step, base + 6)
                v.tensor_tensor(ge3, ge3, lo, ALU.mult).then_inc(route_step, 1)
                v.wait_ge(route_step, base + 7)
                v.tensor_tensor(gt3, gt3, up, ALU.mult).then_inc(route_step, 1)
                v.wait_ge(route_step, base + 9)
                v.tensor_tensor(ge3, ge3, gt3, ALU.add).then_inc(route_step, 1)
                v.wait_ge(route_step, base + 10)
                v.tensor_reduce(rank[:, :], ge[:, :, :, :].rearrange("p t a b -> p (t a) b"), AX, ALU.add)\
                    .then_inc(route_step, 1)
                v.tensor_tensor(pd[:, :, :], prob[:, :, :], prc[:, :].unsqueeze(2).broadcast_to([P, GG, E0]),
                                ALU.subtract).then_inc(route_step, 1)

            def route_weights(g):
                base = ROUTE * g
                v.wait_ge(pq_ready, g + 1)
                v.wait_ge(route_step, base + 12)
                v.scalar_tensor_tensor(pqs[:, :, :].rearrange("p t e -> p (t e)"), rank[:, :], 2.0,
                                       pq[:, :, :].rearrange("p t e -> p (t e)"), ALU.is_lt, ALU.mult)\
                    .then_inc(route_step, 1)
                v.wait_ge(route_step, base + 13)
                v.tensor_reduce(qsum[:, :], pqs[:, :, :], AX, ALU.add).then_inc(route_step, 1)
                v.wait_ge(route_step, base + 14)
                v.reciprocal(qrc[:, :], qsum[:, :]).then_inc(route_step, 1)
                v.wait_ge(route_step, base + 15)
                v.tensor_tensor(wgt[:, :, :], pqs[:, :, :], qrc[:, :].unsqueeze(2).broadcast_to([P, GG, E0]),
                                ALU.mult).then_inc(route_step, 1)
                v.wait_ge(route_step, base + 16)
                need(v, wpT_done, g)
                v.tensor_copy(wparts[:, :, 0, :], wgt[:, :, :]).then_inc(route_step, 1)
                v.wait_ge(route_step, base + 17)
                v.tensor_tensor(wr1[:, :, :], wgt[:, :, :], wparts[:, :, 0, :], ALU.subtract)\
                    .then_inc(route_step, 1)
                v.wait_ge(route_step, base + 18)
                v.tensor_copy(wparts[:, :, 1, :], wr1[:, :, :]).then_inc(route_step, 1)
                v.wait_ge(route_step, base + 19)
                v.tensor_tensor(wparts[:, :, 2, :], wr1[:, :, :], wparts[:, :, 1, :], ALU.subtract)\
                    .then_inc(route_step, 1)

            def body(i, i0):
                run = live("experts", i0)
                for s in range(SLOTS):
                    n = i * E0 + s
                    if s == 0:
                        if run:
                            v.wait_ge(wpT_done, i + 1)
                            need(v, wb_done, (i - 1) * E0)
                            v.tensor_copy(wpT[:, i0 % 2, :], b_misc[0:3 * E0, 0:GW // 2].bitcast(BF16))\
                                .then_inc(wpT_ready, 1)
                        if live("experts", i0, -1):
                            g = i - 1
                            v.wait_ge(l3_done, i * E0)
                            v.tensor_tensor(x[:, cols(g)], b_out[:, :], x[:, cols(g)], ALU.add)\
                                .then_inc(x_experts_ready, 1)
                        if live("attn0", i0, -1):
                            attn_dve_y(at0, v, i + 1)
                        if live("attn0", i0):
                            settle(v, const_ready)
                            v.wait_ge(x_loaded, 16 * (i + 2) + 16)
                            norm_measure(at0["norm"], v, x_tile(i + 2), i + 2)
                            make_mask(i + 2, i0 % 2)
                            need(v, at0["xnT_done"], i + 2)
                            norm_apply(at0["norm"], v, buf_tile(at0["xn"]), x_tile(i + 2), i + 2)
                        if run:
                            weigh(n, s)
                        if live("attn0", i0, -1):
                            attn_dve_elu(at0, v, i + 1)
                    if s == 1:
                        if live("attn1", i0):
                            settle(v, const_ready)
                            v.wait_ge(x_experts_ready, i)
                            norm_measure(at1["norm"], v, x_tile(i - 1), i - 1)
                        if live("attn1", i0, -1):
                            attn_dve_y(at1, v, i - 2)
                        if live("route", i0):
                            settle(v, const_ready)
                            v.wait_ge(at0["x_ready"], i + 2)
                            norm_measure(rn, v, x_tile(i + 1), i + 1)
                        if live("attn1", i0):
                            need(v, at1["xnT_done"], i - 1)
                            norm_apply(at1["norm"], v, buf_tile(at1["xn"]), x_tile(i - 1), i - 1)
                        if live("route", i0):
                            need(v, r_xnT_done, i + 1)
                            norm_apply(rn, v, buf_tile(r_xn), x_tile(i + 1), i + 1)
                        if run:
                            weigh(n, s)
                        if live("attn1", i0, -1):
                            attn_dve_elu(at1, v, i - 2)
                    if s == 2:
                        if live("attn0", i0):
                            attn_dve_fi(at0, v, b_small, i + 2)
                        if live("route", i0):
                            g = i + 1
                            par = (i0 + 1) % 2
                            v.wait_ge(xnTh_ready, g + 1)
                            v.tensor_tensor(xnTl[:, par, :], b_misc[:, :], xnTh[:, par, :].bitcast(F32),
                                            ALU.subtract).then_inc(xnTl_ready, 1)
                        if run:
                            weigh(n, s)
                        if live("pool", i0):
                            settle(v, const_ready)
                            v.wait_ge(at1["x_ready"], i - 1)
                            need(v, moments_ready, i - 2)
                            norm_measure(pn, v, x_tile(i - 2), i - 2)
                    if s == 3:
                        if live("attn1", i0):
                            attn_dve_fi(at1, v, b_small, i - 1)
                        if live("attn0", i0):
                            attn_dve_scores(at0, v, i + 2)
                        if run:
                            weigh(n, s)
                        if live("pool", i0):
                            need(v, p_xnT_done, i - 2)
                            norm_apply(pn, v, buf_tile(p_xn), x_tile(i - 2), i - 2)
                    if s == 4:
                        if live("route", i0):
                            route_first(i + 1)
                        if live("attn1", i0):
                            attn_dve_scores(at1, v, i - 1)
                        if run:
                            weigh(n, s)
                        if live("route", i0):
                            route_rank(i + 1)
                        if live("attn0", i0):
                            attn_dve_rsum(at0, v, i + 2)
                    if s == 5:
                        if run:
                            weigh(n, s)
                        if live("pool", i0):
                            g = i - 2
                            v.wait_ge(xnT3_ready, g + 1)
                            v.tensor_reduce(msum[:, bass.ds(g * GG, GG)], tiles(b_misc[:, :]), AX, ALU.add)\
                                .then_inc(msum_ready, 1)
                        if live("route", i0):
                            route_weights(i + 1)
                        if live("attn1", i0):
                            attn_dve_rsum(at1, v, i - 1)

            rounds(v, body)

            count = [0]

            def step(ins):
                count[0] += 1
                ins.then_inc(head_dve, 1)
                v.wait_ge(head_dve, count[0])

            def h(j, w=E1):
                return hd[:, j, 0:w]

            def softmax(src, e, j):
                step(v.tensor_reduce(h(j, 1), src, AX, ALU.max))
                step(v.tensor_scalar(e, src, h(j, 1), None, ALU.subtract))

            def softmax_end(e, dst, j, nth):
                v.wait_ge(head_act, nth)
                step(v.tensor_reduce(h(j, 1), e, AX, ALU.add))
                step(v.reciprocal(h(j, 1), h(j, 1)))
                step(v.tensor_scalar(dst, e, h(j, 1), None, ALU.mult))

            v.wait_ge(late_loaded, LATE)
            v.wait_ge(head_pe, 1)
            step(v.scalar_tensor_tensor(h(0), b_misc[0:NG, 0:E1], 1.0 / P, br[:, :], ALU.mult, ALU.add))
            softmax(h(0), h(1), 2)
            softmax_end(h(3), h(4), 2, 1)
            v.wait_ge(head_pe, 2)
            step(v.tensor_scalar(h(5), b_misc[0:NG, 0:E1], float(P), None, ALU.mult))
            step(v.reciprocal(h(5), h(5)))
            step(v.tensor_scalar(h(5), h(5), CAPACITY, 1.0, ALU.mult, ALU.min))
            step(v.tensor_tensor(h(6), h(4), h(5), ALU.mult))
            softmax(h(6), h(7), 2)
            softmax_end(h(8), h(9), 2, 2)
            step(v.max(top8[:, :], h(9)))
            step(v.max_index(top8i[:, :], top8[:, :], h(9)))
            step(v.tensor_copy(pairs[:, 2:4], top8i[:, 0:2]))
            step(v.tensor_scalar(h(10, 2), top8[:, 0:2], top8[:, 0:1], None, ALU.subtract))
            softmax_end(h(11, 2), pairs[:, 0:2], 2, 3)
            step(v.tensor_scalar(h(0), iota8[:, :], pairs[:, 2:3], pairs[:, 0:1], ALU.is_equal, ALU.mult))
            step(v.tensor_scalar(h(1), iota8[:, :], pairs[:, 3:4], pairs[:, 1:2], ALU.is_equal, ALU.mult))
            step(v.tensor_tensor(h(2), h(0), h(1), ALU.add))
            for q in range(4):
                step(v.tensor_scalar(diag[:, q, :], ident[0:NG, 0:NG], pairs[:, q:q + 1], None, ALU.mult))
            v.wait_ge(head_pe, 3)
            v.tensor_copy(gidx[:, :], bank[0][:, 2 * NG:4 * NG]).then_inc(gidx_ready, 1)
            v.tensor_copy(gw[:, :], bank[0][:, 0:2 * NG]).then_inc(gw_ready, 1)
            v.wait_ge(head_pe, 4)
            step(v.tensor_copy(wdT[:, :], b_misc[0:E1, 0:NG]))
            v.wait_ge(head_pe, 5)
            step(v.tensor_copy(bias2[:, :], b_misc[0:NG, 0:P]))
            v.wait_ge(gidx_ready, 1)
            v.wait_ge(gw_ready, 1)

            def choose_w2(m, par):
                need(v, down_done, m - 1)
                for k in range(2):
                    e = v.value_load(gidx[0:1, bass.ds(m + k * NG, 1)], min_val=0, max_val=E1 - 1)
                    last = v.tensor_scalar(w2c[par][:, k * FF:(k + 1) * FF],
                                           W2[:, bass.ds(e, 1), :].rearrange("p a f -> p (a f)"),
                                           gw[:, bass.ds(m + k * NG, 1)], None, ALU.mult)
                last.then_inc(w2c_ready, 1)

            def tail_sum(g, par):
                v.wait_ge(down_done, GG * g + GG)
                v.wait_ge(res_ready, g + 1)
                need(v, scaled_ready, g - 1)
                need(v, fin_ready, g - 1)
                v.tensor_tensor(sm[par][:, :], bank[2 + par][:, :], res[:, :], ALU.add).then_inc(sum_ready, 1)
                settle(v, const_ready)
                v.wait_ge(sum_ready, g + 1)
                norm_measure(fn, v, buf_tile(sm[par]), g)

            def group(g, g0, par):
                for t in range(GG):
                    choose_w2(GG * g + t, t % 2)
                    if t == 1 and g0 > 0:
                        tail_sum(g - 1, 1 - par)
                    if t == 2 and g0 > 0:
                        norm_apply(fn, v, buf_tile(sm[1 - par]), buf_tile(sm[1 - par]), g - 1)
                    if t == 1:
                        for q in range(GG):
                            m = bass.ds(g * GG + q, 1)
                            last = v.tensor_scalar(res[:, q * P:(q + 1) * P], x_tile(g)(q), mean3[:, m], rstd3[:, m],
                                                   ALU.subtract, ALU.mult)
                        last.then_inc(res_normed, 1)

            for g in range(4):
                group(g, g, g % 2)
            with v.Fori(4, N - 1, 2) as g:
                group(g, 4, 0)
                group(g + 1, 5, 1)
            tail_sum(N - 1, 1)
            norm_apply(fn, v, buf_tile(sm[1]), buf_tile(sm[1]), N - 1)

        @block.tensor
        def _(pe):
            pe.wait_ge(early_loaded, EARLY)
            pe.wait_ge(const_ready, 8)
            for at in (at0, at1):
                pe.transpose(at["bank"][:, 0:P], at["w"][:, :], ident[:, :]).then_inc(wT_done, 1)
            pe.wait_ge(wT_ready, 2)
            for j, at in enumerate((at0, at1)):
                pe.matmul(b_misc[:, 2 * j:2 * j + 2], at["wT"][:, :], at["a"][:, :], start=True, stop=True)\
                    .then_inc(wa_done, 1)
            pe.wait_ge(wa_ready, 4)
            pe.wait_ge(small_loaded, SMALL)
            pe.wait_ge(split_step, 9)
            pe.wait_ge(const_step, 8)

            def layer1(n, g, par, e):
                ws = slice(e * P, (e + 1) * P)
                pe.matmul(b_h1[:, :], w1h[:, ws], xnTh[:, par, :], start=True, stop=False)
                pe.matmul(b_h1[:, :], w1l[:, ws], xnTh[:, par, :], start=False, stop=False)
                pe.matmul(b_h1[:, :], w1h[:, ws], xnTl[:, par, :], start=False, stop=True)\
                    .then_inc(l1_done, 1)

            def layer2(n, e):
                pe.wait_ge(h1_ready, n + 1)
                need(pe, h2_ready, n)
                pe.matmul(b_h2[:, :], w2[:, e, :], h1[:, e % 2, :], start=True, stop=True).then_inc(l2_done, 1)

            def spread_weights(n, par, e):
                need(pe, h2w_ready, n)
                pe.matmul(b_wts[:, :], pick[:, e, :], wpT[:, par, :], start=True, stop=True).then_inc(wb_done, 1)

            def bias3(g, par):
                need(pe, x_experts_ready, g)
                for t in range(GG):
                    s = slice(t * P, (t + 1) * P)
                    for q in range(3):
                        pe.matmul(b_out[:, s], wpT[:, par, s], b3p[:, q, :], start=(t == 0 and q == 0),
                                  stop=False, skip_group_check=True)

            def layer3(n, e):
                pe.wait_ge(h2w_ready, n + 1)
                for t in range(GG):
                    s = slice(t * P, (t + 1) * P)
                    last = pe.matmul(b_out[:, s], h2w[:, e % 2, s], w3[:, e, :], start=False,
                                     stop=(e == E0 - 1), skip_group_check=True)
                last.then_inc(l3_done, 1)

            def body(i, i0):
                run = live("experts", i0)
                par = i0 % 2
                for s in range(SLOTS):
                    n = i * E0 + s
                    if s == 0:
                        if live("experts", i0, -1):
                            layer3(n - 1, E0 - 1)
                        if run:
                            pe.wait_ge(route_step, ROUTE * (i + 1))
                            need(pe, msum_ready, newest(i - 1, i0 - 1, "pool"))
                            for t in range(GG):
                                last = pe.transpose(
                                    b_misc[:, :].bitcast(BF16)[0:3 * E0, t * P:(t + 1) * P],
                                    wparts[:, t, :, :].rearrange("p a e -> p (a e)"), identb[:, :])
                            last.then_inc(wpT_done, 1)
                            layer2(n, 0)
                            layer1(n + 1, i, par, 1)
                        if live("attn1", i0, -1):
                            attn_pe_aggregate(at1, pe, i - 2)
                        if live("attn0", i0):
                            attn_pe_transpose_xn(at0, pe, ident, i + 2)
                        if run:
                            pe.wait_ge(wpT_ready, i + 1)
                            spread_weights(n, par, 0)
                    else:
                        if run:
                            if s == 1:
                                bias3(i, par)
                            layer2(n, s)
                            if s < SLOTS - 1:
                                layer1(n + 1, i, par, s + 1)
                            spread_weights(n, par, s)
                            layer3(n - 1, s - 1)
                        if s == SLOTS - 1 and live("experts", i0, 1):
                            pe.wait_ge(xnTl_ready, i + 2)
                            layer1(n + 1, i + 1, 1 - par, 0)
                    if s == 1:
                        if live("attn0", i0):
                            need(pe, at1["fi_ready"], newest(i - 1, i0 - 1, "attn1"))
                            attn_pe_project(at0, pe, b_small, i + 2)
                        if live("attn1", i0):
                            attn_pe_transpose_xn(at1, pe, ident, i - 1)
                        if live("route", i0):
                            g = i + 1
                            pe.wait_ge(rn["xn_ready"], g + 1)
                            need(pe, wpT_ready, g)
                            need(pe, msum_ready, newest(i - 1, i0 - 1, "pool"))
                            for t in range(GG):
                                q = slice(t * P, (t + 1) * P)
                                last = pe.transpose(b_misc[:, q], r_xn[:, q], ident[:, :])
                            last.then_inc(r_xnT_done, 1)
                    if s == 2:
                        if live("attn0", i0):
                            pe.wait_ge(mask_ready, i + 3)
                            attn_pe_scores(at0, pe, identb, mask, i + 2)
                        if live("route", i0):
                            g = i + 1
                            pr = 1 - par
                            pe.wait_ge(xnTh_ready, g + 1)
                            pe.wait_ge(xnTl_ready, g + 1)
                            pe.matmul(b_misc[0:RH, :], rw1h[:, :], xnTh[:, pr, :], start=True, stop=False)
                            pe.matmul(b_misc[0:RH, :], rw1l[:, :], xnTh[:, pr, :], start=False, stop=False)
                            pe.matmul(b_misc[0:RH, :], rw1h[:, :], xnTl[:, pr, :], start=False, stop=True)\
                                .then_inc(rh_done, 1)
                        if live("attn1", i0):
                            need(pe, at0["fi_ready"], newest(i, i0, "attn0"))
                            attn_pe_project(at1, pe, b_small, i - 1)
                    if s == 3:
                        if live("route", i0):
                            g = i + 1
                            pe.wait_ge(rh_ready, g + 1)
                            for t in range(GG):
                                last = pe.matmul(b_misc[:, t * E0:(t + 1) * E0], rh[:, t * P:(t + 1) * P],
                                                 rw2[:, :], start=True, stop=True)
                            last.then_inc(lg_done, 1)
                        if live("attn1", i0):
                            attn_pe_scores(at1, pe, identb, mask, i - 1)
                    if s == 4:
                        if live("pool", i0):
                            g = i - 2
                            pe.wait_ge(pn["xn_ready"], g + 1)
                            need(pe, lg_ready, newest(i, i0, "route"))
                            need(pe, wpT_ready, newest(i, i0, "experts"))
                            need(pe, msum_ready, g)
                            for t in range(GG):
                                q = slice(t * P, (t + 1) * P)
                                last = pe.transpose(b_misc[:, q], p_xn[:, q], ident[:, :])
                            last.then_inc(p_xnT_done, 1)
                        if live("attn0", i0):
                            attn_pe_transpose_probs(at0, pe, ident, i + 2)
                    if s == 5:
                        if live("attn0", i0):
                            attn_pe_aggregate(at0, pe, i + 2)
                        if live("attn1", i0):
                            attn_pe_transpose_probs(at1, pe, ident, i - 1)

            rounds(pe, body)

            pe.wait_ge(late_loaded, LATE)
            pe.wait_ge(msum_ready, N)
            pe.matmul(b_misc[0:NG, 0:E1], msum[:, :], wr[:, :], start=True, stop=True).then_inc(head_pe, 1)
            pe.wait_ge(head_dve, 6)
            pe.matmul(b_misc[0:NG, 0:E1], ones[0:NG, 0:NG], hd[:, 4, :], start=True, stop=True)\
                .then_inc(head_pe, 1)
            pe.wait_ge(head_dve, 29)
            pe.matmul(bank[0][:, 0:4 * NG], ones[0:NG, :], diag[:, :, :].rearrange("p a b -> p (a b)"),
                      start=True, stop=True).then_inc(head_pe, 1)
            pe.transpose(b_misc[0:E1, 0:NG], hd[:, 2, :], ident[0:NG, 0:NG]).then_inc(head_pe, 1)
            pe.wait_ge(head_dve, 30)
            pe.matmul(b_misc[0:NG, 0:P], wdT[:, :], B2[:, :], start=True, stop=True).then_inc(head_pe, 1)
            pe.wait_ge(gw_ready, 1)

            def up(m, par):
                pe.wait_ge(w1c_ready, m + 1)
                need(pe, gelu_ready, m - 1)
                for k in range(2):
                    for c in range(FC):
                        j = FC * k + c
                        last = pe.matmul(bank[par][:, j * P:(j + 1) * P], w1c[par][:, k, c * P:(c + 1) * P],
                                         xnT3[:, bass.ds(m * P, P)], start=True, stop=True)
                last.then_inc(up_done, 1)

            def down(m, par, gpar, t):
                pe.wait_ge(gelu_ready, m + 1)
                pe.wait_ge(w2c_ready, m + 1)
                for j in range(2 * FC):
                    last = pe.matmul(bank[2 + gpar][:, t * P:(t + 1) * P], hid[par][:, j * P:(j + 1) * P],
                                     w2c[par][:, j * P:(j + 1) * P], start=(j == 0), stop=(j == 2 * FC - 1))
                last.then_inc(down_done, 1)

            def group(g, g0, gpar):
                for t in range(GG):
                    up(GG * g + t, t % 2)
                    if t == 0 and g0 > 0:
                        down(GG * g - 1, 1, 1 - gpar, GG - 1)
                    if t == 1:
                        need(pe, sum_ready, g - 1)
                    if t > 0:
                        down(GG * g + t - 1, (t - 1) % 2, gpar, t - 1)

            pe.wait_ge(xnT3_ready, N)
            for g in range(4):
                group(g, g, g % 2)
            with pe.Fori(4, N - 1, 2) as g:
                group(g, 4, 0)
                group(g + 1, 5, 1)
            down(NG - 1, 1, 1, GG - 1)


_INS = ["x", "adj", "L0_gnn_W", "L0_gnn_a", "L0_ffn_router_w1", "L0_ffn_router_b1", "L0_ffn_router_w2",
        "L0_ffn_router_b2", "L0_ffn_expert_w1", "L0_ffn_expert_b1", "L0_ffn_expert_w2", "L0_ffn_expert_b2",
        "L0_ffn_expert_w3", "L0_ffn_expert_b3", "L1_gnn_W", "L1_gnn_a", "L1_ffn_Wr", "L1_ffn_br",
        "L1_ffn_W1", "L1_ffn_b1", "L1_ffn_W2", "L1_ffn_b2", "L1_ffn_gamma", "L1_ffn_beta"]


def kernel(**inputs):
    import numpy as _np
    import concourse.bacc as _bacc
    from concourse.bass_utils import run_bass_kernel_spmd as _run

    nc = _bacc.Bacc("TRN2", target_bir_lowering=False, num_devices=1)
    arrays, args = {}, {}
    for name in _INS:
        a = _np.ascontiguousarray(inputs[name])
        arrays["in_" + name] = a
        args[name] = nc.dram_tensor("in_" + name, a.shape, mybir.dt.from_np(a.dtype), kind="ExternalInput").ap()
    out = nc.dram_tensor("out_0", (NG, P, P), F32, kind="ExternalOutput").ap()
    build(nc, args, out)
    r = _run(nc, [arrays], core_ids=[0])
    return r.results[0]["out_0"]
```

```python
import concourse.bass as bass
from concourse import mybir

F32 = mybir.dt.float32
F32R = mybir.dt.float32r
BF16 = mybir.dt.bfloat16
I32 = mybir.dt.int32
U32 = mybir.dt.uint32
ALU = mybir.AluOpType
ACT = mybir.ActivationFunctionType
AX = mybir.AxisListType.X

P = 128
NG = 64
GG = 4
N = NG // GG
GW = GG * P
E0 = 6
RH = 64
E1 = 8
FF = 256
FC = FF // P
SLOPE = 0.2
EPS = 1e-5
MASKED = -5.0e9
LIFT = 2.0 ** 120
JUST_BELOW = -1e-30
CAPACITY = float(-(-NG * P * 5 // (4 * E1)))
SLOTS = 6
ROUTE = 18
KW = 9 * E0
LEAD = {"norm0": 3, "attn0": 2, "route": 1, "experts": 0, "attn1": -1, "pool": -2}


def need(eng, sem, value):
    if not isinstance(value, int) or value > 0:
        eng.wait_ge(sem, value)


def settle(eng, sem, value=1):
    eng.wait_ge(sem, value)


def cols(g):
    return bass.ds(g * GW, GW)


def tiles(ap):
    return ap.rearrange("p (t d) -> p t d", t=GG)


def per_tile(ap):
    return ap.unsqueeze(2).broadcast_to([P, GG, P])


def norm_stage(nc, name):
    st = {}
    st["stats"] = nc.alloc_sbuf_tensor(name + "_stats", [P, GG, 6], F32)
    st["turn"] = nc.alloc_sbuf_tensor(name + "_turn", [P, 1], F32)
    st["mv"] = nc.alloc_sbuf_tensor(name + "_mean_var", [P, GG, 2], F32)
    st["vare"] = nc.alloc_sbuf_tensor(name + "_var_eps", [P, GG], F32)
    st["rstd"] = nc.alloc_sbuf_tensor(name + "_rstd", [P, GG], F32)
    st["stats_ready"] = nc.alloc_semaphore(name + "_stats_ready")
    st["var_ready"] = nc.alloc_semaphore(name + "_var_ready")
    st["vare_ready"] = nc.alloc_semaphore(name + "_vare_ready")
    st["shift"] = nc.alloc_sbuf_tensor(name + "_shift", [P, GG], F32)
    st["shift0"] = nc.alloc_sbuf_tensor(name + "_shift0", [P, GG], F32)
    st["rstd_ready"] = nc.alloc_semaphore(name + "_rstd_ready")
    st["shift_step"] = nc.alloc_semaphore(name + "_shift_step")
    st["xn_ready"] = nc.alloc_semaphore(name + "_xn_ready")
    return st


def norm_measure(st, v, src, g):
    for t in range(GG):
        last = v.bn_stats(st["stats"][:, t, :], src(t))
    last.then_inc(st["stats_ready"], 1)
    v.wait_ge(st["stats_ready"], g + 1)
    need(v, st["xn_ready"], g)
    v.tensor_copy(st["turn"][:, :], st["stats"][:, GG - 1, 0:1])
    for t in range(GG):
        last = v.bn_aggr(st["mv"][:, t, :], st["stats"][:, t, :])
    last.then_inc(st["var_ready"], 1)


def norm_root(st, p, eps, minus_half, g):
    p.wait_ge(st["var_ready"], g + 1)
    p.tensor_tensor(st["vare"][:, :], st["mv"][:, :, 1], eps[:, :], ALU.add).then_inc(st["vare_ready"], 1)
    p.wait_ge(st["vare_ready"], g + 1)
    need(p, st["xn_ready"], g)
    p.tensor_tensor(st["rstd"][:, :], st["vare"][:, :], minus_half[:, :], ALU.pow).then_inc(st["rstd_ready"], 1)


def norm_shift(st, p, minus_one, g):
    p.wait_ge(st["rstd_ready"], g + 1)
    p.tensor_tensor(st["shift0"][:, :], st["mv"][:, :, 0], st["rstd"][:, :], ALU.mult).then_inc(st["shift_step"], 1)
    p.wait_ge(st["shift_step"], 2 * g + 1)
    p.tensor_tensor(st["shift"][:, :], st["shift0"][:, :], minus_one[:, :], ALU.mult)\
        .then_inc(st["shift_step"], 1)


def norm_apply_act(st, a, dst, src, g):
    a.wait_ge(st["shift_step"], 2 * g + 2)
    for t in range(GG):
        last = a.activation(dst(t), src(t), ACT.Identity, bias=st["shift"][:, t:t + 1],
                            scale=st["rstd"][:, t:t + 1])
    last.then_inc(st["xn_ready"], 1)


def norm_apply(st, v, dst, src, g):
    v.wait_ge(st["rstd_ready"], g + 1)
    for t in range(GG):
        last = v.tensor_scalar(dst(t), src(t), st["mv"][:, t, 0:1], st["rstd"][:, t:t + 1],
                               ALU.subtract, ALU.mult)
    last.then_inc(st["xn_ready"], 1)


def attn_stage(nc, name, bank):
    st = {}
    def sb(what, cols=GW, dt=F32):
        return nc.alloc_sbuf_tensor(name + "_" + what, [P, cols], dt)

    def sem(what):
        return nc.alloc_semaphore(name + "_" + what)

    st["norm"] = norm_stage(nc, name)
    st["bank"] = bank
    st["w"] = sb("w", P)
    st["wT"] = sb("wT", P)
    st["a"] = sb("a", 2)
    st["wa"] = sb("wa", 2)
    st["wa2"] = sb("wa2", P)
    st["xn"] = sb("xn")
    st["xnT"] = sb("xnT")
    st["wh"] = sb("wh")
    st["z"] = sb("z")
    st["lk"] = sb("lk")
    st["pr"] = sb("pr")
    st["prT"] = sb("prT")
    st["fi"] = sb("fi", GG)
    st["mx"] = sb("mx", GG)
    st["nt"] = sb("nt", GG)
    st["nm"] = sb("nm", GG)
    st["sums"] = sb("sums", GG)
    st["rsum"] = sb("rsum", GG)
    st["xnT_done"] = sem("xnT_done")
    st["xnT_ready"] = sem("xnT_ready")
    st["wh_done"] = sem("wh_done")
    st["wh_ready"] = sem("wh_ready")
    st["fi_done"] = sem("fi_done")
    st["fi_ready"] = sem("fi_ready")
    st["z_done"] = sem("z_done")
    st["mx_ready"] = sem("mx_ready")
    st["z_ready"] = sem("z_ready")
    st["nt_ready"] = sem("nt_ready")
    st["nm_ready"] = sem("nm_ready")
    st["lk_ready"] = sem("lk_ready")
    st["pr_ready"] = sem("pr_ready")
    st["prT_done"] = sem("prT_done")
    st["prT_ready"] = sem("prT_ready")
    st["rsum_ready"] = sem("rsum_ready")
    st["agg_done"] = sem("agg_done")
    st["y_ready"] = sem("y_ready")
    st["yneg_ready"] = sem("yneg_ready")
    st["yexp_ready"] = sem("yexp_ready")
    st["elu_ready"] = sem("elu_ready")
    st["x_ready"] = sem("x_ready")
    return st


def attn_pe_transpose_xn(st, pe, ident, g):
    pe.wait_ge(st["norm"]["xn_ready"], g + 1)
    need(pe, st["y_ready"], g)
    for t in range(GG):
        last = pe.transpose(st["bank"][:, t * P:(t + 1) * P], st["xn"][:, t * P:(t + 1) * P], ident[:, :])
    last.then_inc(st["xnT_done"], 1)


def attn_pe_project(st, pe, small, g):
    pe.wait_ge(st["xnT_ready"], g + 1)
    for t in range(GG):
        last = pe.matmul(st["bank"][:, t * P:(t + 1) * P], st["xnT"][:, t * P:(t + 1) * P], st["w"][:, :],
                         start=True, stop=True)
    last.then_inc(st["wh_done"], 1)
    for t in range(GG):
        last = pe.matmul(small[:, t:t + 1], st["xnT"][:, t * P:(t + 1) * P], st["wa"][:, 0:1],
                         start=True, stop=True)
    last.then_inc(st["fi_done"], 1)


def attn_pe_scores(st, pe, identb, mask, g):
    pe.wait_ge(st["wh_ready"], g + 1)
    pe.matmul(st["bank"][:, :], st["wa2"][:, :], st["xnT"][:, :], start=True, stop=False)
    pe.matmul(st["bank"][:, :], identb[:, :], mask[:, cols(g)], start=False, stop=True).then_inc(st["z_done"], 1)


def attn_pe_transpose_probs(st, pe, ident, g):
    pe.wait_ge(st["pr_ready"], g + 1)
    pe.wait_ge(st["z_ready"], g + 1)
    for t in range(GG):
        last = pe.transpose(st["bank"][:, t * P:(t + 1) * P], st["pr"][:, t * P:(t + 1) * P], ident[:, :])
    last.then_inc(st["prT_done"], 1)


def attn_pe_aggregate(st, pe, g):
    pe.wait_ge(st["prT_ready"], g + 1)
    for t in range(GG):
        s = slice(t * P, (t + 1) * P)
        last = pe.matmul(st["bank"][:, s], st["prT"][:, s], st["wh"][:, s], start=True, stop=True)
    last.then_inc(st["agg_done"], 1)

def attn_act_xnT(st, a, g):
    a.wait_ge(st["xnT_done"], g + 1)
    need(a, st["z_done"], g)
    a.activation(st["xnT"][:, :], st["bank"][:, :], ACT.Copy).then_inc(st["xnT_ready"], 1)


def attn_act_wh(st, a, g):
    a.wait_ge(st["wh_done"], g + 1)
    need(a, st["agg_done"], g)
    a.activation(st["wh"][:, :], st["bank"][:, :], ACT.Copy).then_inc(st["wh_ready"], 1)


def attn_act_exp(st, a, g):
    a.wait_ge(st["lk_ready"], g + 1)
    a.wait_ge(st["nm_ready"], g + 1)
    need(a, st["elu_ready"], g)
    for t in range(GG):
        s = slice(t * P, (t + 1) * P)
        last = a.activation(st["pr"][:, s], st["lk"][:, s], ACT.Exp, bias=st["nm"][:, t:t + 1],
                            accum_out=st["sums"][:, t:t + 1])
    last.then_inc(st["pr_ready"], 1)


def attn_act_prT(st, a, g):
    a.wait_ge(st["prT_done"], g + 1)
    need(a, st["x_ready"], g)
    a.activation(st["prT"][:, :], st["bank"][:, :], ACT.Copy).then_inc(st["prT_ready"], 1)


def attn_act_elu(st, a, g):
    a.wait_ge(st["y_ready"], g + 1)
    a.activation(st["lk"][:, :], st["z"][:, :], ACT.Exp).then_inc(st["yexp_ready"], 1)
    a.wait_ge(st["yexp_ready"], g + 1)
    a.activation(st["pr"][:, :], st["lk"][:, :], ACT.Relu, bias=1.0, scale=-1.0).then_inc(st["yneg_ready"], 1)

def attn_dve_fi(st, v, small, g):
    v.wait_ge(st["fi_done"], g + 1)
    v.tensor_copy(st["fi"][:, :], small[:, 0:GG]).then_inc(st["fi_ready"], 1)


def attn_dve_scores(st, v, g):
    v.wait_ge(st["z_done"], g + 1)
    v.wait_ge(st["fi_ready"], g + 1)
    v.tensor_reduce(st["mx"][:, :], tiles(st["bank"][:, :]), AX, ALU.max).then_inc(st["mx_ready"], 1)
    v.tensor_tensor(tiles(st["z"][:, :]), tiles(st["bank"][:, :]), per_tile(st["fi"][:, :]), ALU.add)\
        .then_inc(st["z_ready"], 1)
    v.wait_ge(st["mx_ready"], g + 1)
    v.scalar_tensor_tensor(st["nt"][:, :], st["mx"][:, :], -1.0, st["fi"][:, :], ALU.mult, ALU.subtract)\
        .then_inc(st["nt_ready"], 1)
    v.wait_ge(st["z_ready"], g + 1)
    v.scalar_tensor_tensor(st["lk"][:, :], st["z"][:, :], SLOPE, st["z"][:, :], ALU.mult, ALU.max)\
        .then_inc(st["lk_ready"], 1)
    v.wait_ge(st["nt_ready"], g + 1)
    v.scalar_tensor_tensor(st["nm"][:, :], st["nt"][:, :], SLOPE, st["nt"][:, :], ALU.mult, ALU.min)\
        .then_inc(st["nm_ready"], 1)


def attn_dve_rsum(st, v, g):
    v.wait_ge(st["pr_ready"], g + 1)
    v.reciprocal(st["rsum"][:, :], st["sums"][:, :]).then_inc(st["rsum_ready"], 1)


def attn_dve_y(st, v, g):
    v.wait_ge(st["agg_done"], g + 1)
    v.wait_ge(st["rsum_ready"], g + 1)
    v.tensor_tensor(tiles(st["z"][:, :]), tiles(st["bank"][:, :]), per_tile(st["rsum"][:, :]), ALU.mult)\
        .then_inc(st["y_ready"], 1)


def attn_dve_elu(st, v, g):
    v.wait_ge(st["yneg_ready"], g + 1)
    v.scalar_tensor_tensor(st["prT"][:, :], st["pr"][:, :], -1.0, st["z"][:, :], ALU.mult, ALU.max)\
        .then_inc(st["elu_ready"], 1)

def attn_pool_residual(st, p, x, g):
    p.wait_ge(st["elu_ready"], g + 1)
    p.tensor_tensor(x[:, cols(g)], x[:, cols(g)], st["prT"][:, :], ALU.add).then_inc(st["x_ready"], 1)


def build(nc, A, out):
    def sb(name, shape, dt=F32):
        return nc.alloc_sbuf_tensor(name, shape, dt)

    def sem(name):
        return nc.alloc_semaphore(name)

    bank = [nc.alloc_psum_tensor("bank%d" % b, [P, GW], F32) for b in range(8)]
    b_h2, b_h1, b_out, b_wts, b_at0, b_small, b_at1, b_misc = bank

    const_ready = sem("const_ready")

    x = sb("x", [P, NG * P])
    shift3 = sb("shift3", [P, NG])
    rstd3 = sb("rstd3", [P, NG])
    xnT3 = sb("xnT3", [P, NG * P])
    mask = sb("mask", [P, NG * P], BF16)
    adj_in = sb("adj_in", [P, 2, GW], I32)
    ident = sb("ident", [P, P])
    identb = sb("identb", [P, P], BF16)
    ones = sb("ones", [P, P])
    minus_half = sb("minus_half", [P, GG])
    minus_one = sb("minus_one", [P, GG])
    eps = sb("eps", [P, GG])
    level = sb("level", [P, E0, E0])
    pick = sb("pick", [KW, E0, P], BF16)

    at0 = attn_stage(nc, "at0", b_at0)
    at1 = attn_stage(nc, "at1", b_at1)
    rn = norm_stage(nc, "route")
    pn = norm_stage(nc, "pool")
    r_xn = sb("r_xn", [P, GW])
    p_xn = sb("p_xn", [P, GW])
    xnTh = sb("xnTh", [P, 2, GW], F32R)
    xnTl = sb("xnTl", [P, 2, GW], F32R)
    rw1h = sb("rw1h", [P, RH], F32R)
    rw1l = sb("rw1l", [P, RH], F32R)
    rb1 = sb("rb1", [RH, 1])
    rh = sb("rh", [RH + 1, GW])
    rw2 = sb("rw2", [RH + 1, E0])
    w1h = sb("w1h", [P, E0 * P], F32R)
    w1l = sb("w1l", [P, E0 * P], F32R)
    rowpart = sb("rowpart", [KW, 3])
    w2 = sb("w2", [P, E0, P])
    w3 = sb("w3", [P, E0, P])
    b1 = sb("b1", [P, E0])
    b2 = sb("b2", [P, E0])
    b3 = sb("b3", [KW, P])
    b3r = sb("b3r", [KW, 2, P])
    b3a = sb("b3a", [KW, 3, P], BF16)
    b3p = sb("b3p", [KW, P], BF16)
    h1 = sb("h1", [P, 2, GW])
    h2 = sb("h2", [P, 2, GW])
    h2w = sb("h2w", [P, 2, GW])
    lg = sb("lg", [P, GG, E0])
    lgmx = sb("lgmx", [P, GG])
    lgd = sb("lgd", [P, GG, E0])
    pe0 = sb("pe0", [P, GG, E0])
    psum_ = sb("p_sum", [P, GG])
    prc = sb("p_rcp", [P, GG])
    prob = sb("prob", [P, GG, E0])
    lifted = sb("lifted", [P, GG, E0])
    over = sb("over", [P, GG, E0, E0])
    rank = sb("rank", [P, GG * E0])
    pd = sb("pd", [P, GG, E0])
    pq = sb("pq", [P, GG, E0])
    pqs = sb("pqs", [P, GG, E0])
    qsum = sb("qsum", [P, GG])
    qrc = sb("qrc", [P, GG])
    wgt = sb("wgt", [P, GG, E0])
    wr1 = sb("wr1", [P, GG, E0])
    wparts = sb("wparts", [P, GG, 3, 3, E0], BF16)
    wpT = sb("wpT", [KW, 2, GW], BF16)

    W1 = sb("W1", [P, E1, FF + FC])
    W2 = sb("W2", [P, E1, FF])
    msum = sb("msum", [P, NG])
    wr = sb("wr", [P, E1])
    br = sb("br", [NG, E1])
    B2 = sb("B2", [E1, P])
    gamma = sb("gamma", [P, P])
    beta = sb("beta", [P, P])
    iota8 = sb("iota8", [NG, E1])
    hd = sb("hd", [NG, 12, E1])
    top8 = sb("top8", [NG, 8])
    top8i = sb("top8i", [NG, 8], U32)
    pairs = sb("pairs", [NG, 4])
    diag = sb("diag", [NG, 4, NG])
    gw = sb("gw", [P, 2 * NG])
    gidx = sb("gidx", [P, 2 * NG], I32)
    wdT = sb("wdT", [E1, NG])
    bias2 = sb("bias2", [NG, P])
    fn = norm_stage(nc, "final")

    bias2_dram = nc.dram_tensor("bias2_scratch", (NG, P), F32).ap()

    def flat(buf):
        return buf[:, :, :].rearrange("p a f -> p (a f)")[:, 0:2 * (FF + FC)].rearrange("p (k f) -> p k f", k=2)

    w1c = [flat(h1), flat(h2), flat(h2w), sb("w1c", [P, 2, FF + FC])]
    w2c = [at0["wh"], at0["z"], at0["xnT"], r_xn]
    hid = [at0["lk"], at0["pr"]]
    b2b = [at0["prT"], at0["xn"]]
    res = at1["xn"]
    xb = [at1["xnT"], at1["wh"]]
    sm = [at1["z"], at1["lk"]]
    fin = [at1["pr"], at1["prT"]]

    x_loaded = sem("x_loaded")
    adj_loaded = sem("adj_loaded")
    small_loaded = sem("small_loaded")
    early_loaded = sem("early_loaded")
    late_loaded = sem("late_loaded")
    const_step = sem("const_step")
    wT_done = sem("wT_done")
    wT_ready = sem("wT_ready")
    wa_done = sem("wa_done")
    wa_ready = sem("wa_ready")
    split_step = sem("split_step")
    mask_ready = sem("mask_ready")
    r_xnT_done = sem("r_xnT_done")
    xnTh_ready = sem("xnTh_ready")
    xnTl_ready = sem("xnTl_ready")
    rh_done = sem("rh_done")
    rh_ready = sem("rh_ready")
    lg_done = sem("lg_done")
    lg_ready = sem("lg_ready")
    route_step = sem("route_step")
    pe0_ready = sem("pe0_ready")
    pq_ready = sem("pq_ready")
    wpT_done = sem("wpT_done")
    wpT_ready = sem("wpT_ready")
    l1_done = sem("l1_done")
    l2_done = sem("l2_done")
    l3_done = sem("l3_done")
    h1_ready = sem("h1_ready")
    h2_ready = sem("h2_ready")
    wb_done = sem("wb_done")
    h2w_ready = sem("h2w_ready")
    x_experts_ready = sem("x_experts_ready")
    p_xnT_done = sem("p_xnT_done")
    xnT3_ready = sem("xnT3_ready")
    msum_done = sem("msum_done")
    msum_ready = sem("msum_ready")
    moments_ready = sem("moments_ready")
    res_normed = sem("res_normed")

    head_pe = sem("head_pe")
    head_act = sem("head_act")
    head_dve = sem("head_dve")
    gw_ready = sem("gw_ready")
    gidx_ready = sem("gidx_ready")
    bias2_stored = sem("bias2_stored")
    b2b_loaded = sem("b2b_loaded")
    w1c_ready = sem("w1c_ready")
    w2c_ready = sem("w2c_ready")
    up_done = sem("up_done")
    gelu_ready = sem("gelu_ready")
    down_done = sem("down_done")
    res_ready = sem("res_ready")
    xb_ready = sem("xb_ready")
    sum_ready = sem("sum_ready")
    scaled_ready = sem("scaled_ready")
    fin_ready = sem("fin_ready")
    stored = sem("stored")

    EARLY = 16 * 6
    SMALL = 16 * 16
    LATE = 16 * 10

    def rounds(eng, body):
        for i in range(-3, 3):
            body(i, i)
        with eng.Fori(3, N - 4, 2) as i:
            body(i, 3)
            body(i + 1, 4)
        for i in range(N - 3, N + 2):
            body(i, i)

    def live(stage, i0, shift=0):
        return 0 <= i0 + LEAD[stage] + shift < N

    def newest(i, i0, stage):
        lead = LEAD[stage] + 1
        if isinstance(i, int):
            return max(0, min(i + lead, N))
        return i + lead

    with nc.Block() as block:

        @block.sync
        def _(sp):
            xg = A["x"].rearrange("(g t) p d -> g p t d", t=GG)
            ag = A["adj"].rearrange("(g t) p d -> g p t d", t=GG)

            def load(g, par):
                settle(sp, const_ready)
                need(sp, x_loaded, 16 * g)
                sp.dma_start(tiles(x[:, cols(g)]), xg[g] if isinstance(g, int) else
                             xg[bass.ds(g, 1)].rearrange("a p t d -> p (a t) d")).then_inc(x_loaded, 16)
                settle(sp, const_ready)
                need(sp, adj_loaded, 16 * g)
                need(sp, mask_ready, g - 1)
                sp.dma_start(tiles(adj_in[:, par, :]), ag[g] if isinstance(g, int) else
                             ag[bass.ds(g, 1)].rearrange("a p t d -> p (a t) d")).then_inc(adj_loaded, 16)

            load(0, 0)
            sp.dma_start(at0["w"][:, :], A["L0_gnn_W"]).then_inc(early_loaded, 16)
            sp.dma_start(at1["w"][:, :], A["L1_gnn_W"]).then_inc(early_loaded, 16)
            load(1, 1)
            with sp.Fori(2, N - 1, 2) as g:
                load(g, 0)
                load(g + 1, 1)

            sp.wait_ge(head_dve, 31)
            sp.dma_start(bias2_dram, bias2[:, :]).then_inc(bias2_stored, 16)
            sp.wait_ge(bias2_stored, 16)
            b2g = bias2_dram.rearrange("(g t) d -> g (t d)", t=GG)
            outg = out.rearrange("(g t) p d -> g p t d", t=GG)

            def load_bias(g, par):
                settle(sp, const_ready)
                need(sp, res_ready, g - 1)
                need(sp, b2b_loaded, 16 * g)
                row = b2g[g] if isinstance(g, int) else b2g[bass.ds(g, 1)].rearrange("a d -> (a d)")
                sp.dma_start(b2b[par][:, :], row.partition_broadcast(P)).then_inc(b2b_loaded, 16)

            def store(g, par):
                settle(sp, const_ready)
                sp.wait_ge(fin_ready, g + 1)
                need(sp, stored, 16 * g)
                dst = outg[g] if isinstance(g, int) else outg[bass.ds(g, 1)].rearrange("a p t d -> p (a t) d")
                sp.dma_start(dst, tiles(fin[par][:, :])).then_inc(stored, 16)

            load_bias(0, 0)
            load_bias(1, 1)
            for g in range(2, 4):
                store(g - 2, g % 2)
                load_bias(g, g % 2)
            with sp.Fori(4, N - 1, 2) as g:
                store(g - 2, 0)
                load_bias(g, 0)
                store(g - 1, 1)
                load_bias(g + 1, 1)
            store(N - 2, 0)
            store(N - 1, 1)
            sp.wait_ge(stored, 16 * N)

        @block.gpsimd
        def _(p):
            p.memset(minus_half[:, :], -0.5).then_inc(const_ready, 1)
            p.memset(eps[:, :], EPS).then_inc(const_ready, 1)
            p.memset(minus_one[:, :], -1.0).then_inc(const_ready, 1)
            p.memset(ones[:, :], 1.0).then_inc(const_ready, 1)
            p.memset(ident[:, :], 0.0).then_inc(const_step, 1)
            p.memset(identb[:, :], 0.0).then_inc(const_step, 1)
            p.memset(level[:, :, :], JUST_BELOW).then_inc(const_step, 1)
            p.memset(pick[:, :, :], 0.0).then_inc(const_step, 1)
            p.iota(iota8[:, :], pattern=[[1, E1]], base=0, channel_multiplier=0,
                   allow_small_or_imprecise_dtypes=True).then_inc(const_ready, 1)
            p.wait_ge(const_step, 4)
            for m in (ident, identb):
                p.affine_select(out=m[:, :], in_=m[:, :], compare_op=ALU.not_equal, fill=1.0, base=0,
                                pattern=[[-1, P]], channel_multiplier=1).then_inc(const_ready, 1)
            p.affine_select(out=level[:, :, :], in_=level[:, :, :], compare_op=ALU.is_gt, fill=0.0, base=0,
                            pattern=[[1, E0], [-1, E0]], channel_multiplier=0).then_inc(const_ready, 1)
            for q in range(3):
                p.wait_ge(const_step, 4 + q)
                p.affine_select(out=pick[:, :, :], in_=pick[:, :, :], compare_op=ALU.not_equal, fill=1.0,
                                base=-q * E0, pattern=[[-1, E0], [0, P]], channel_multiplier=1)\
                    .then_inc(const_step, 1)
            p.wait_ge(const_ready, 8)
            p.memset(rowpart[:, :], 1.0).then_inc(const_step, 1)
            p.wait_ge(const_step, 8)
            p.affine_select(out=rowpart[:, :], in_=rowpart[:, :], compare_op=ALU.is_ge, fill=0.0, base=0,
                            pattern=[[-3 * E0, 3]], channel_multiplier=1).then_inc(const_step, 1)
            p.wait_ge(const_step, 9)
            p.affine_select(out=rowpart[:, :], in_=rowpart[:, :], compare_op=ALU.is_ge, fill=0.0,
                            base=3 * E0 - 1, pattern=[[3 * E0, 3]], channel_multiplier=-1)\
                .then_inc(const_step, 1)
            w2d = A["L1_ffn_W2"].rearrange("e (c f) d -> f e c d", c=FC)
            p.dma_start(W1[:, :, 0:FF], A["L1_ffn_W1"].rearrange("e d f -> d e f")).then_inc(late_loaded, 16)
            for c in range(FC):
                p.dma_start(W2[:, :, c * P:(c + 1) * P], w2d[:, :, c, :]).then_inc(late_loaded, 16)
            with nc.allow_non_contiguous_dma(reason="bias columns, once"):
                for c in range(FC):
                    p.dma_start(W1[:, :, FF + c], A["L1_ffn_b1"][:, c * P:(c + 1) * P].rearrange("e p -> p e"))\
                        .then_inc(late_loaded, 16)
            p.dma_start(wr[:, :], A["L1_ffn_Wr"]).then_inc(late_loaded, 16)
            p.dma_start(br[:, :], A["L1_ffn_br"].partition_broadcast(NG)).then_inc(late_loaded, 16)
            p.dma_start(B2[:, :], A["L1_ffn_b2"]).then_inc(late_loaded, 16)
            p.dma_start(gamma[:, :], A["L1_ffn_gamma"].partition_broadcast(P)).then_inc(late_loaded, 16)
            p.dma_start(beta[:, :], A["L1_ffn_beta"].partition_broadcast(P)).then_inc(late_loaded, 16)

            def body(i, i0):
                if live("attn1", i0):
                    norm_root(at1["norm"], p, eps, minus_half, i - 1)
                if live("attn0", i0, -1):
                    attn_pool_residual(at0, p, x, i + 1)
                if live("route", i0):
                    norm_root(rn, p, eps, minus_half, i + 1)
                if live("attn1", i0, -1):
                    attn_pool_residual(at1, p, x, i - 2)
                if live("pool", i0):
                    g = i - 2
                    norm_root(pn, p, eps, minus_half, g)
                    norm_shift(pn, p, minus_one, g)
                    p.tensor_copy(rstd3[:, bass.ds(g * GG, GG)], pn["rstd"][:, :])
                    p.wait_ge(pn["shift_step"], 2 * g + 2)
                    p.tensor_copy(shift3[:, bass.ds(g * GG, GG)], pn["shift"][:, :]).then_inc(moments_ready, 1)
                if live("norm0", i0):
                    norm_root(at0["norm"], p, eps, minus_half, i + 3)
                    norm_shift(at0["norm"], p, minus_one, i + 3)

            rounds(p, body)

            p.wait_ge(late_loaded, LATE)

            def group(g, g0, par):
                need(p, fin_ready, g - 1)
                p.tensor_tensor(tiles(xb[par][:, :]), tiles(x[:, cols(g)]),
                                beta[:, :].unsqueeze(1).broadcast_to([P, GG, P]), ALU.add).then_inc(xb_ready, 1)
                if g0 > 0:
                    norm_root(fn, p, eps, minus_half, g - 1)
                    norm_shift(fn, p, minus_one, g - 1)
                p.wait_ge(b2b_loaded, 16 * g + 16)
                p.wait_ge(res_normed, g + 1)
                p.tensor_tensor(res[:, :], res[:, :], b2b[par][:, :], ALU.add).then_inc(res_ready, 1)
                if g0 > 0:
                    finish(g - 1, 1 - par)

            def finish(g, par):
                p.wait_ge(fn["xn_ready"], g + 1)
                p.tensor_tensor(tiles(sm[par][:, :]), tiles(sm[par][:, :]),
                                gamma[:, :].unsqueeze(1).broadcast_to([P, GG, P]), ALU.mult)\
                    .then_inc(scaled_ready, 1)
                p.wait_ge(scaled_ready, g + 1)
                p.wait_ge(xb_ready, g + 1)
                need(p, stored, 16 * (g - 1))
                p.tensor_tensor(fin[par][:, :], sm[par][:, :], xb[par][:, :], ALU.add).then_inc(fin_ready, 1)

            for g in range(4):
                group(g, g, g % 2)
            with p.Fori(4, N - 1, 2) as g:
                group(g, 4, 0)
                group(g + 1, 5, 1)
            norm_root(fn, p, eps, minus_half, N - 1)
            norm_shift(fn, p, minus_one, N - 1)
            finish(N - 1, 1)

        @block.scalar
        def _(a):
            with nc.allow_non_contiguous_dma(reason="bias columns, once"):
                a.dma_start(at0["a"][:, :], A["L0_gnn_a"].rearrange("(t p) -> p t", p=P)).then_inc(early_loaded, 16)
                a.dma_start(at1["a"][:, :], A["L1_gnn_a"].rearrange("(t p) a -> p (t a)", p=P))\
                    .then_inc(early_loaded, 16)
                a.dma_start(h1[:, :, :].rearrange("p a f -> p (a f)")[:, 0:E0 * P],
                            A["L0_ffn_expert_w1"].rearrange("e d h -> d e h")).then_inc(early_loaded, 16)
                a.dma_start(h2[:, 0, 0:RH], A["L0_ffn_router_w1"]).then_inc(early_loaded, 16)
                a.dma_start(rb1[:, :], A["L0_ffn_router_b1"].unsqueeze(1)).then_inc(small_loaded, 16)
                a.dma_start(rw2[0:RH, :], A["L0_ffn_router_w2"]).then_inc(small_loaded, 16)
                a.dma_start(rw2[RH:RH + 1, :], A["L0_ffn_router_b2"].unsqueeze(0)).then_inc(small_loaded, 16)
                a.dma_start(b1[:, :], A["L0_ffn_expert_b1"].rearrange("e p -> p e")).then_inc(small_loaded, 16)
                a.dma_start(b2[:, :], A["L0_ffn_expert_b2"].rearrange("e p -> p e")).then_inc(small_loaded, 16)
                for q in range(9):
                    a.dma_start(b3[q * E0:(q + 1) * E0, :], A["L0_ffn_expert_b3"]).then_inc(small_loaded, 16)
                a.dma_start(w2[:, :, :], A["L0_ffn_expert_w2"].rearrange("e d h -> d e h"))\
                    .then_inc(small_loaded, 16)
                a.dma_start(w3[:, :, :], A["L0_ffn_expert_w3"].rearrange("e d h -> d e h"))\
                    .then_inc(small_loaded, 16)

            def relu2(n, e):
                a.wait_ge(l2_done, n + 1)
                need(a, h2w_ready, n - 1)
                a.activation(h2[:, e % 2, :], b_h2[:, :], ACT.Relu, bias=b2[:, e:e + 1]).then_inc(h2_ready, 1)

            def relu1(n, e):
                a.wait_ge(l1_done, n + 1)
                a.activation(h1[:, e % 2, :], b_h1[:, :], ACT.Relu, bias=b1[:, e:e + 1]).then_inc(h1_ready, 1)

            def x_tile(g):
                return lambda t: x[:, bass.ds(g * GW + t * P, P)]

            def buf_tile(buf):
                return lambda t: buf[:, t * P:(t + 1) * P]

            a.wait_ge(small_loaded, SMALL)
            a.wait_ge(split_step, 12)

            def body(i, i0):
                run = live("experts", i0)
                for s in range(SLOTS):
                    n = i * E0 + s
                    if s == 0:
                        if live("attn1", i0, -1):
                            attn_act_prT(at1, a, i - 2)
                        if live("attn0", i0):
                            attn_act_xnT(at0, a, i + 2)
                    if s == 1 and live("attn0", i0):
                        attn_act_wh(at0, a, i + 2)
                    if s == 2 and live("attn1", i0):
                        attn_act_xnT(at1, a, i - 1)
                    if s == 3:
                        if live("attn1", i0):
                            attn_act_wh(at1, a, i - 1)
                    if s == 4 and live("attn0", i0):
                        attn_act_prT(at0, a, i + 2)
                    if s == 5 and live("pool", i0):
                        g = i - 2
                        a.wait_ge(p_xnT_done, g + 1)
                        a.activation(xnT3[:, cols(g)], b_misc[:, :], ACT.Copy).then_inc(xnT3_ready, 1)
                    if run:
                        relu2(n, s)
                    if s == 2 and live("route", i0):
                        g = i + 1
                        a.wait_ge(r_xnT_done, g + 1)
                        need(a, l1_done, (g - 1) * E0)
                        a.activation(xnTh[:, (i0 + 1) % 2, :], b_misc[:, :], ACT.Copy).then_inc(xnTh_ready, 1)
                    if s == 3 and live("route", i0):
                        g = i + 1
                        a.wait_ge(rh_done, g + 1)
                        need(a, lg_done, g)
                        a.activation(rh[0:RH, :], b_misc[0:RH, :], ACT.Relu, bias=rb1[:, :]).then_inc(rh_ready, 1)
                    if run and s < SLOTS - 1:
                        relu1(n + 1, s + 1)
                    if s == SLOTS - 1 and live("experts", i0, 1):
                        relu1(n + 1, 0)
                    if s == 0 and live("attn0", i0, -1):
                        attn_act_elu(at0, a, i + 1)
                    if s == 1 and live("attn1", i0, -1):
                        attn_act_elu(at1, a, i - 2)
                    if s == 3 and live("attn0", i0):
                        attn_act_exp(at0, a, i + 2)
                    if s == 4:
                        if live("pool", i0):
                            need(a, msum_ready, i - 2)
                            norm_apply_act(pn, a, buf_tile(p_xn), x_tile(i - 2), i - 2)
                        if live("route", i0):
                            a.wait_ge(route_step, ROUTE * (i + 1) + 2)
                            a.activation(pe0[:, :, :], lgd[:, :, :], ACT.Exp).then_inc(pe0_ready, 1)
                    if s == 5:
                        if live("attn1", i0):
                            attn_act_exp(at1, a, i - 1)
                        if live("norm0", i0):
                            need(a, at0["xnT_done"], i + 3)
                            norm_apply_act(at0["norm"], a, buf_tile(at0["xn"]), x_tile(i + 3), i + 3)
                        if live("route", i0):
                            a.wait_ge(route_step, ROUTE * (i + 1) + 7)
                            a.activation(pq[:, :, :], pd[:, :, :], ACT.Exp).then_inc(pq_ready, 1)

            rounds(a, body)

            for at, dst, src in ((3, hd[:, 3, :], hd[:, 1, :]), (12, hd[:, 8, :], hd[:, 7, :]),
                                 (19, hd[:, 11, 0:2], hd[:, 10, 0:2])):
                a.wait_ge(head_dve, at)
                a.activation(dst, src, ACT.Exp).then_inc(head_act, 1)

            def gelus(m, wpar):
                par = wpar % 2
                a.wait_ge(up_done, m + 1)
                need(a, down_done, m - 1)
                for k in range(2):
                    for c in range(FC):
                        s = slice((FC * k + c) * P, (FC * k + c + 1) * P)
                        last = a.activation(hid[par][:, s], bank[par][:, s], ACT.Gelu,
                                            bias=w1c[wpar][:, k, FF + c:FF + c + 1])
                last.then_inc(gelu_ready, 1)

            def group(g, g0, par):
                for t in range(GG):
                    gelus(GG * g + t, t)
                    if t == 1:
                        need(a, sum_ready, g)
                        for q in range(GG):
                            m = bass.ds(g * GG + q, 1)
                            last = a.activation(res[:, q * P:(q + 1) * P], x_tile(g)(q), ACT.Identity,
                                                bias=shift3[:, m], scale=rstd3[:, m])
                        last.then_inc(res_normed, 1)
                    if t == 2 and g0 > 0:
                        norm_apply_act(fn, a, buf_tile(sm[1 - par]), buf_tile(sm[1 - par]), g - 1)

            for g in range(4):
                group(g, g, g % 2)
            with a.Fori(4, N - 1, 2) as g:
                group(g, 4, 0)
                group(g + 1, 5, 1)
            norm_apply_act(fn, a, buf_tile(sm[1]), buf_tile(sm[1]), N - 1)

        @block.vector
        def _(v):
            v.wait_ge(early_loaded, EARLY)
            raw = h1[:, :, :].rearrange("p a f -> p (a f)")[:, 0:E0 * P]
            v.tensor_copy(w1h[:, :], raw).then_inc(split_step, 1)
            v.tensor_copy(rw1h[:, :], h2[:, 0, 0:RH]).then_inc(split_step, 1)
            v.wait_ge(split_step, 2)
            v.tensor_tensor(w1l[:, :], raw, w1h[:, :].bitcast(F32), ALU.subtract).then_inc(split_step, 1)
            v.tensor_tensor(rw1l[:, :], h2[:, 0, 0:RH], rw1h[:, :].bitcast(F32), ALU.subtract)\
                .then_inc(split_step, 1)
            for j, at in enumerate((at0, at1)):
                v.wait_ge(wT_done, j + 1)
                v.tensor_copy(at["wT"][:, :], at["bank"][:, 0:P]).then_inc(wT_ready, 1)
            for j, at in enumerate((at0, at1)):
                v.wait_ge(wa_done, 2)
                v.tensor_copy(at["wa"][:, :], b_misc[:, 2 * j:2 * j + 2]).then_inc(wa_ready, 1)
            v.wait_ge(wa_ready, 2)
            v.wait_ge(const_ready, 8)
            for at in (at0, at1):
                v.tensor_scalar(at["wa2"][:, :], ones[:, :], at["wa"][:, 1:2], None, ALU.mult).then_inc(wa_ready, 1)
            v.wait_ge(small_loaded, SMALL)
            v.wait_ge(const_step, 10)
            v.tensor_copy(b3a[:, 0, :], b3[:, :]).then_inc(split_step, 1)
            v.wait_ge(split_step, 5)
            v.tensor_tensor(b3r[:, 0, :], b3[:, :], b3a[:, 0, :], ALU.subtract).then_inc(split_step, 1)
            v.wait_ge(split_step, 6)
            v.tensor_copy(b3a[:, 1, :], b3r[:, 0, :]).then_inc(split_step, 1)
            v.wait_ge(split_step, 7)
            v.tensor_tensor(b3a[:, 2, :], b3r[:, 0, :], b3a[:, 1, :], ALU.subtract).then_inc(split_step, 1)
            v.wait_ge(split_step, 8)
            v.tensor_scalar(b3r[:, 0, :], b3a[:, 0, :], rowpart[:, 0:1], None, ALU.mult).then_inc(split_step, 1)
            v.wait_ge(split_step, 9)
            v.scalar_tensor_tensor(b3r[:, 1, :], b3a[:, 1, :], rowpart[:, 1:2], b3r[:, 0, :], ALU.mult, ALU.add)\
                .then_inc(split_step, 1)
            v.wait_ge(split_step, 10)
            v.scalar_tensor_tensor(b3p[:, :], b3a[:, 2, :], rowpart[:, 2:3], b3r[:, 1, :], ALU.mult, ALU.add)\
                .then_inc(split_step, 1)
            v.memset(rh[RH:RH + 1, :], 1.0).then_inc(split_step, 1)

            def x_tile(g):
                return lambda t: x[:, bass.ds(g * GW + t * P, P)]

            def buf_tile(buf):
                return lambda t: buf[:, t * P:(t + 1) * P]

            def make_mask(g, par):
                v.wait_ge(adj_loaded, 16 * g + 16)
                v.tensor_scalar(mask[:, cols(g)], adj_in[:, par, :], 0.0, MASKED, ALU.is_le, ALU.mult)\
                    .then_inc(mask_ready, 1)

            def weigh(n, e):
                v.wait_ge(h2_ready, n + 1)
                v.wait_ge(wb_done, n + 1)
                need(v, l3_done, n - 1)
                v.tensor_tensor(h2w[:, e % 2, :], h2[:, e % 2, :], b_wts[:, :], ALU.mult).then_inc(h2w_ready, 1)

            def route_first(g):
                base = ROUTE * g
                v.wait_ge(lg_done, g + 1)
                v.tensor_copy(lg[:, :, :], b_misc[:, 0:GG * E0].rearrange("p (t e) -> p t e", t=GG))\
                    .then_inc(lg_ready, 1)
                v.wait_ge(lg_ready, g + 1)
                v.tensor_reduce(lgmx[:, :], lg[:, :, :], AX, ALU.max).then_inc(route_step, 1)
                v.wait_ge(route_step, base + 1)
                v.tensor_tensor(lgd[:, :, :], lg[:, :, :], lgmx[:, :].unsqueeze(2).broadcast_to([P, GG, E0]),
                                ALU.subtract).then_inc(route_step, 1)

            def route_rank(g):
                base = ROUTE * g
                v.wait_ge(pe0_ready, g + 1)
                v.tensor_reduce(psum_[:, :], pe0[:, :, :], AX, ALU.add).then_inc(route_step, 1)
                v.wait_ge(route_step, base + 3)
                v.reciprocal(prc[:, :], psum_[:, :]).then_inc(route_step, 1)
                v.wait_ge(route_step, base + 4)
                v.tensor_tensor(prob[:, :, :], pe0[:, :, :], prc[:, :].unsqueeze(2).broadcast_to([P, GG, E0]),
                                ALU.mult).then_inc(route_step, 1)
                v.scalar_tensor_tensor(lifted[:, :, :], pe0[:, :, :], LIFT,
                                       prc[:, :].unsqueeze(2).broadcast_to([P, GG, E0]), ALU.mult, ALU.mult)\
                    .then_inc(route_step, 1)
                v.wait_ge(route_step, base + 5)
                v.tensor_tensor(pd[:, :, :], prob[:, :, :], prc[:, :].unsqueeze(2).broadcast_to([P, GG, E0]),
                                ALU.subtract).then_inc(route_step, 1)
                v.wait_ge(route_step, base + 6)
                mine = lifted[:, :, :].unsqueeze(3).broadcast_to([P, GG, E0, E0])
                other = lifted[:, :, :].unsqueeze(2).broadcast_to([P, GG, E0, E0])
                v.tensor_tensor(over[:, :, :, :], other, mine, ALU.subtract).then_inc(route_step, 1)
                lv = level[:, :, :].rearrange("p a b -> p (a b)").unsqueeze(1).broadcast_to([P, GG, E0 * E0])
                over3 = over[:, :, :, :].rearrange("p t a b -> p t (a b)")
                v.wait_ge(route_step, base + 8)
                v.tensor_tensor(over3, over3, lv, ALU.is_gt).then_inc(route_step, 1)
                v.wait_ge(route_step, base + 9)
                v.tensor_reduce(rank[:, :], over[:, :, :, :].rearrange("p t a b -> p (t a) b"), AX, ALU.add)\
                    .then_inc(route_step, 1)

            def route_weights(g):
                base = ROUTE * g
                v.wait_ge(pq_ready, g + 1)
                v.wait_ge(route_step, base + 10)
                v.scalar_tensor_tensor(pqs[:, :, :].rearrange("p t e -> p (t e)"), rank[:, :], 2.0,
                                       pq[:, :, :].rearrange("p t e -> p (t e)"), ALU.is_lt, ALU.mult)\
                    .then_inc(route_step, 1)
                v.wait_ge(route_step, base + 11)
                v.tensor_reduce(qsum[:, :], pqs[:, :, :], AX, ALU.add).then_inc(route_step, 1)
                v.wait_ge(route_step, base + 12)
                v.reciprocal(qrc[:, :], qsum[:, :]).then_inc(route_step, 1)
                v.wait_ge(route_step, base + 13)
                v.tensor_tensor(wgt[:, :, :], pqs[:, :, :], qrc[:, :].unsqueeze(2).broadcast_to([P, GG, E0]),
                                ALU.mult).then_inc(route_step, 1)
                v.wait_ge(route_step, base + 14)
                need(v, wpT_done, g)
                v.tensor_copy(wparts[:, :, :, 0, :], wgt[:, :, :].unsqueeze(2).broadcast_to([P, GG, 3, E0])).then_inc(route_step, 1)
                v.wait_ge(route_step, base + 15)
                v.tensor_tensor(wr1[:, :, :], wgt[:, :, :], wparts[:, :, 0, 0, :], ALU.subtract)\
                    .then_inc(route_step, 1)
                v.wait_ge(route_step, base + 16)
                v.tensor_copy(wparts[:, :, :, 1, :], wr1[:, :, :].unsqueeze(2).broadcast_to([P, GG, 3, E0])).then_inc(route_step, 1)
                v.wait_ge(route_step, base + 17)
                v.tensor_tensor(wparts[:, :, :, 2, :], wr1[:, :, :].unsqueeze(2).broadcast_to([P, GG, 3, E0]),
                                wparts[:, :, :, 1, :], ALU.subtract)\
                    .then_inc(route_step, 1)

            def measure(st, g, source_ready, value):
                settle(v, const_ready)
                if st is pn:
                    need(v, moments_ready, g)
                v.wait_ge(source_ready, value)
                norm_measure(st, v, x_tile(g), g)

            def body(i, i0):
                run = live("experts", i0)
                n = i * E0
                attn0, attn1, route, pool = (live(k, i0) for k in ("attn0", "attn1", "route", "pool"))
                if run:
                    v.wait_ge(wpT_done, i + 1)
                    need(v, wb_done, (i - 1) * E0)
                    v.tensor_copy(wpT[:, i0 % 2, :], b_misc[0:KW, 0:GW // 2].bitcast(BF16)).then_inc(wpT_ready, 1)
                if live("experts", i0, -1):
                    v.wait_ge(l3_done, i * E0)
                    v.tensor_tensor(x[:, cols(i - 1)], b_out[:, :], x[:, cols(i - 1)], ALU.add)\
                        .then_inc(x_experts_ready, 1)
                if attn1:
                    measure(at1["norm"], i - 1, x_experts_ready, i)
                if live("attn0", i0, -1):
                    attn_dve_elu(at0, v, i + 1)
                if live("attn1", i0, -1):
                    attn_dve_y(at1, v, i - 2)
                if run:
                    weigh(n, 0)
                if attn1:
                    need(v, at1["xnT_done"], i - 1)
                    norm_apply(at1["norm"], v, buf_tile(at1["xn"]), x_tile(i - 1), i - 1)
                if route:
                    measure(rn, i + 1, at0["x_ready"], i + 2)
                if attn0:
                    attn_dve_fi(at0, v, b_small, i + 2)
                if live("attn1", i0, -1):
                    attn_dve_elu(at1, v, i - 2)
                if route:
                    need(v, r_xnT_done, i + 1)
                    norm_apply(rn, v, buf_tile(r_xn), x_tile(i + 1), i + 1)
                if run:
                    weigh(n + 1, 1)
                if attn0:
                    attn_dve_scores(at0, v, i + 2)
                if route:
                    g = i + 1
                    par = (i0 + 1) % 2
                    v.wait_ge(xnTh_ready, g + 1)
                    v.tensor_tensor(xnTl[:, par, :], b_misc[:, :], xnTh[:, par, :].bitcast(F32),
                                    ALU.subtract).then_inc(xnTl_ready, 1)
                if run:
                    weigh(n + 2, 2)
                if attn1:
                    attn_dve_fi(at1, v, b_small, i - 1)
                if pool:
                    measure(pn, i - 2, at1["x_ready"], i - 1)
                if run:
                    weigh(n + 3, 3)
                if attn1:
                    attn_dve_scores(at1, v, i - 1)
                if route:
                    route_first(i + 1)
                if live("norm0", i0):
                    measure(at0["norm"], i + 3, x_loaded, 16 * (i + 3) + 16)
                    make_mask(i + 3, (i0 + 1) % 2)
                if attn0:
                    attn_dve_rsum(at0, v, i + 2)
                if run:
                    weigh(n + 4, 4)
                if attn0:
                    attn_dve_y(at0, v, i + 2)
                if route:
                    route_rank(i + 1)
                if pool:
                    g = i - 2
                    v.wait_ge(msum_done, g + 1)
                    v.tensor_copy(msum[:, bass.ds(g * GG, GG)], b_small[:, 0:GG]).then_inc(msum_ready, 1)
                if route:
                    route_weights(i + 1)
                if attn1:
                    attn_dve_rsum(at1, v, i - 1)
                if run:
                    weigh(n + 5, 5)

            rounds(v, body)

            count = [0]

            def step(ins):
                count[0] += 1
                ins.then_inc(head_dve, 1)
                v.wait_ge(head_dve, count[0])

            def h(j, w=E1):
                return hd[:, j, 0:w]

            def softmax(src, e, j):
                step(v.tensor_reduce(h(j, 1), src, AX, ALU.max))
                step(v.tensor_scalar(e, src, h(j, 1), None, ALU.subtract))

            def softmax_end(e, dst, j, nth):
                v.wait_ge(head_act, nth)
                step(v.tensor_reduce(h(j, 1), e, AX, ALU.add))
                step(v.reciprocal(h(j, 1), h(j, 1)))
                step(v.tensor_scalar(dst, e, h(j, 1), None, ALU.mult))

            v.wait_ge(late_loaded, LATE)
            v.wait_ge(head_pe, 1)
            step(v.scalar_tensor_tensor(h(0), b_misc[0:NG, 0:E1], 1.0 / P, br[:, :], ALU.mult, ALU.add))
            softmax(h(0), h(1), 2)
            softmax_end(h(3), h(4), 2, 1)
            v.wait_ge(head_pe, 2)
            step(v.tensor_scalar(h(5), b_misc[0:NG, 0:E1], float(P), None, ALU.mult))
            step(v.reciprocal(h(5), h(5)))
            step(v.tensor_scalar(h(5), h(5), CAPACITY, 1.0, ALU.mult, ALU.min))
            step(v.tensor_tensor(h(6), h(4), h(5), ALU.mult))
            softmax(h(6), h(7), 2)
            softmax_end(h(8), h(9), 2, 2)
            step(v.max(top8[:, :], h(9)))
            step(v.max_index(top8i[:, :], top8[:, :], h(9)))
            step(v.tensor_copy(pairs[:, 2:4], top8i[:, 0:2]))
            step(v.tensor_scalar(h(10, 2), top8[:, 0:2], top8[:, 0:1], None, ALU.subtract))
            softmax_end(h(11, 2), pairs[:, 0:2], 2, 3)
            step(v.tensor_scalar(h(0), iota8[:, :], pairs[:, 2:3], pairs[:, 0:1], ALU.is_equal, ALU.mult))
            step(v.tensor_scalar(h(1), iota8[:, :], pairs[:, 3:4], pairs[:, 1:2], ALU.is_equal, ALU.mult))
            step(v.tensor_tensor(h(2), h(0), h(1), ALU.add))
            for q in range(4):
                step(v.tensor_scalar(diag[:, q, :], ident[0:NG, 0:NG], pairs[:, q:q + 1], None, ALU.mult))
            v.wait_ge(head_pe, 3)
            v.tensor_copy(gidx[:, :], bank[0][:, 2 * NG:4 * NG]).then_inc(gidx_ready, 1)
            v.tensor_copy(gw[:, :], bank[0][:, 0:2 * NG]).then_inc(gw_ready, 1)
            v.wait_ge(head_pe, 4)
            step(v.tensor_copy(wdT[:, :], b_misc[0:E1, 0:NG]))
            v.wait_ge(head_pe, 5)
            step(v.tensor_copy(bias2[:, :], b_misc[0:NG, 0:P]))
            v.wait_ge(gidx_ready, 1)
            v.wait_ge(gw_ready, 1)

            def choose(m, par):
                experts = [v.value_load(gidx[0:1, bass.ds(m + k * NG, 1)], min_val=0, max_val=E1 - 1)
                           for k in range(2)]
                need(v, gelu_ready, m - 3)
                for k, e in enumerate(experts):
                    last = v.tensor_copy(w1c[par][:, k, :], W1[:, bass.ds(e, 1), :].rearrange("p a f -> p (a f)"))
                last.then_inc(w1c_ready, 1)
                need(v, down_done, m - 3)
                for k, e in enumerate(experts):
                    last = v.tensor_scalar(w2c[par][:, k * FF:(k + 1) * FF],
                                           W2[:, bass.ds(e, 1), :].rearrange("p a f -> p (a f)"),
                                           gw[:, bass.ds(m + k * NG, 1)], None, ALU.mult)
                last.then_inc(w2c_ready, 1)

            def tail_sum(g, par):
                v.wait_ge(down_done, GG * g + GG)
                v.wait_ge(res_ready, g + 1)
                need(v, scaled_ready, g - 1)
                need(v, fin_ready, g - 1)
                v.tensor_tensor(sm[par][:, :], bank[2 + par][:, :], res[:, :], ALU.add).then_inc(sum_ready, 1)
                settle(v, const_ready)
                v.wait_ge(sum_ready, g + 1)
                norm_measure(fn, v, buf_tile(sm[par]), g)

            def group(g, g0, par):
                for t in range(GG):
                    choose(GG * g + t, t)
                    if t == 2 and g0 > 0:
                        tail_sum(g - 1, 1 - par)

            for g in range(4):
                group(g, g, g % 2)
            with v.Fori(4, N - 1, 2) as g:
                group(g, 4, 0)
                group(g + 1, 5, 1)
            tail_sum(N - 1, 1)

        @block.tensor
        def _(pe):
            pe.wait_ge(early_loaded, EARLY)
            pe.wait_ge(const_ready, 8)
            for at in (at0, at1):
                pe.transpose(at["bank"][:, 0:P], at["w"][:, :], ident[:, :]).then_inc(wT_done, 1)
            pe.wait_ge(wT_ready, 2)
            for j, at in enumerate((at0, at1)):
                pe.matmul(b_misc[:, 2 * j:2 * j + 2], at["wT"][:, :], at["a"][:, :], start=True, stop=True)\
                    .then_inc(wa_done, 1)
            pe.wait_ge(wa_ready, 4)
            pe.wait_ge(small_loaded, SMALL)
            pe.wait_ge(split_step, 12)
            pe.wait_ge(const_step, 7)

            def layer1(n, g, par, e):
                ws = slice(e * P, (e + 1) * P)
                pe.matmul(b_h1[:, :], w1h[:, ws], xnTh[:, par, :], start=True, stop=False)
                pe.matmul(b_h1[:, :], w1l[:, ws], xnTh[:, par, :], start=False, stop=False)
                pe.matmul(b_h1[:, :], w1h[:, ws], xnTl[:, par, :], start=False, stop=True)\
                    .then_inc(l1_done, 1)

            def layer2(n, e):
                pe.wait_ge(h1_ready, n + 1)
                need(pe, h2_ready, n)
                pe.matmul(b_h2[:, :], w2[:, e, :], h1[:, e % 2, :], start=True, stop=True).then_inc(l2_done, 1)

            def spread_weights(n, par, e):
                need(pe, h2w_ready, n)
                pe.matmul(b_wts[:, :], pick[:, e, :], wpT[:, par, :], start=True, stop=True).then_inc(wb_done, 1)

            def bias3(g, par):
                need(pe, x_experts_ready, g)
                for t in range(GG):
                    s = slice(t * P, (t + 1) * P)
                    pe.matmul(b_out[:, s], wpT[:, par, s], b3p[:, :], start=(t == 0), stop=False,
                              skip_group_check=True)

            def layer3(n, e):
                pe.wait_ge(h2w_ready, n + 1)
                for t in range(GG):
                    s = slice(t * P, (t + 1) * P)
                    last = pe.matmul(b_out[:, s], h2w[:, e % 2, s], w3[:, e, :], start=False,
                                     stop=(e == E0 - 1), skip_group_check=True)
                last.then_inc(l3_done, 1)

            def weights_transpose(i):
                for t in range(GG):
                    last = pe.transpose(b_misc[:, :].bitcast(BF16)[0:KW, t * P:(t + 1) * P],
                                        wparts[:, t, :, :, :].rearrange("p a b e -> p (a b e)"), identb[:, :])
                last.then_inc(wpT_done, 1)

            def route_transpose(i, i0):
                pe.wait_ge(rn["xn_ready"], i + 2)
                need(pe, wpT_ready, newest(i, i0, "experts"))
                need(pe, xnT3_ready, newest(i - 1, i0 - 1, "pool"))
                for t in range(GG):
                    q = slice(t * P, (t + 1) * P)
                    last = pe.transpose(b_misc[:, q], r_xn[:, q], ident[:, :])
                last.then_inc(r_xnT_done, 1)

            def route_hidden(g, par):
                pe.wait_ge(xnTh_ready, g + 1)
                pe.wait_ge(xnTl_ready, g + 1)
                pe.matmul(b_misc[0:RH, :], rw1h[:, :], xnTh[:, par, :], start=True, stop=False)
                pe.matmul(b_misc[0:RH, :], rw1l[:, :], xnTh[:, par, :], start=False, stop=False)
                pe.matmul(b_misc[0:RH, :], rw1h[:, :], xnTl[:, par, :], start=False, stop=True)\
                    .then_inc(rh_done, 1)

            def route_logits(g):
                pe.wait_ge(rh_ready, g + 1)
                for t in range(GG):
                    last = pe.matmul(b_misc[:, t * E0:(t + 1) * E0], rh[:, t * P:(t + 1) * P], rw2[:, :],
                                     start=True, stop=True)
                last.then_inc(lg_done, 1)

            def pool_transpose(i, i0):
                g = i - 2
                pe.wait_ge(pn["xn_ready"], g + 1)
                need(pe, lg_ready, newest(i, i0, "route"))
                need(pe, wpT_ready, newest(i, i0, "experts"))
                need(pe, xnT3_ready, g)
                for t in range(GG):
                    q = slice(t * P, (t + 1) * P)
                    last = pe.transpose(b_misc[:, q], p_xn[:, q], ident[:, :])
                last.then_inc(p_xnT_done, 1)
                need(pe, at0["fi_ready"], newest(i, i0, "attn0"))
                need(pe, at1["fi_ready"], newest(i, i0, "attn1"))
                need(pe, msum_ready, g)
                for t in range(GG):
                    last = pe.matmul(b_small[:, t:t + 1], p_xn[:, t * P:(t + 1) * P], ones[:, 0:1],
                                     start=True, stop=True)
                last.then_inc(msum_done, 1)

            def body(i, i0):
                run = live("experts", i0)
                attn0, attn1, route, pool = (live(k, i0) for k in ("attn0", "attn1", "route", "pool"))
                par = i0 % 2
                n = i * E0
                if run:
                    layer2(n, 0)
                if run:
                    pe.wait_ge(route_step, ROUTE * (i + 1))
                    need(pe, xnT3_ready, newest(i - 1, i0 - 1, "pool"))
                if live("experts", i0, -1):
                    layer3(n - 1, E0 - 1)
                if run:
                    weights_transpose(i)
                    layer1(n + 1, i, par, 1)
                if live("attn1", i0, -1):
                    attn_pe_aggregate(at1, pe, i - 2)
                if attn0:
                    need(pe, msum_ready, newest(i - 1, i0 - 1, "pool"))
                    need(pe, at1["fi_ready"], newest(i - 1, i0 - 1, "attn1"))
                    attn_pe_project(at0, pe, b_small, i + 2)
                if run:
                    pe.wait_ge(wpT_ready, i + 1)
                    spread_weights(n, par, 0)
                    bias3(i, par)
                    layer2(n + 1, 1)
                    layer1(n + 2, i, par, 2)
                if attn0:
                    pe.wait_ge(mask_ready, i + 3)
                    attn_pe_scores(at0, pe, identb, mask, i + 2)
                if attn1:
                    attn_pe_transpose_xn(at1, pe, ident, i - 1)
                if run:
                    layer3(n, 0)
                    spread_weights(n + 1, par, 1)
                if run:
                    layer2(n + 2, 2)
                if route:
                    route_transpose(i, i0)
                if run:
                    layer1(n + 3, i, par, 3)
                if attn1:
                    need(pe, at0["fi_ready"], newest(i, i0, "attn0"))
                    need(pe, msum_ready, newest(i - 1, i0 - 1, "pool"))
                    attn_pe_project(at1, pe, b_small, i - 1)
                if run:
                    layer3(n + 1, 1)
                    spread_weights(n + 2, par, 2)
                if route:
                    route_hidden(i + 1, 1 - par)
                if run:
                    layer2(n + 3, 3)
                    layer1(n + 4, i, par, 4)
                if attn1:
                    attn_pe_scores(at1, pe, identb, mask, i - 1)
                if route:
                    route_logits(i + 1)
                if run:
                    layer3(n + 2, 2)
                    spread_weights(n + 3, par, 3)
                if attn0:
                    attn_pe_transpose_probs(at0, pe, ident, i + 2)
                if run:
                    layer2(n + 4, 4)
                    layer1(n + 5, i, par, 5)
                if attn0:
                    attn_pe_aggregate(at0, pe, i + 2)
                if run:
                    layer3(n + 3, 3)
                    spread_weights(n + 4, par, 4)
                if pool:
                    pool_transpose(i, i0)
                if run:
                    layer2(n + 5, 5)
                if live("experts", i0, 1):
                    pe.wait_ge(xnTl_ready, i + 2)
                    layer1(n + 6, i + 1, 1 - par, 0)
                if run:
                    layer3(n + 4, 4)
                    spread_weights(n + 5, par, 5)
                if attn1:
                    attn_pe_transpose_probs(at1, pe, ident, i - 1)
                if live("norm0", i0):
                    attn_pe_transpose_xn(at0, pe, ident, i + 3)

            rounds(pe, body)

            pe.wait_ge(late_loaded, LATE)
            pe.wait_ge(xnT3_ready, N)
            pe.wait_ge(msum_ready, N)
            pe.matmul(b_misc[0:NG, 0:E1], msum[:, :], wr[:, :], start=True, stop=True).then_inc(head_pe, 1)
            pe.wait_ge(head_dve, 6)
            pe.matmul(b_misc[0:NG, 0:E1], ones[0:NG, 0:NG], hd[:, 4, :], start=True, stop=True)\
                .then_inc(head_pe, 1)
            pe.wait_ge(head_dve, 29)
            pe.matmul(bank[0][:, 0:4 * NG], ones[0:NG, :], diag[:, :, :].rearrange("p a b -> p (a b)"),
                      start=True, stop=True).then_inc(head_pe, 1)
            pe.transpose(b_misc[0:E1, 0:NG], hd[:, 2, :], ident[0:NG, 0:NG]).then_inc(head_pe, 1)
            pe.wait_ge(head_dve, 30)
            pe.matmul(b_misc[0:NG, 0:P], wdT[:, :], B2[:, :], start=True, stop=True).then_inc(head_pe, 1)
            pe.wait_ge(gw_ready, 1)

            def up(m, wpar):
                par = wpar % 2
                pe.wait_ge(w1c_ready, m + 1)
                need(pe, gelu_ready, m - 1)
                for k in range(2):
                    for c in range(FC):
                        j = FC * k + c
                        last = pe.matmul(bank[par][:, j * P:(j + 1) * P], w1c[wpar][:, k, c * P:(c + 1) * P],
                                         xnT3[:, bass.ds(m * P, P)], start=True, stop=True)
                last.then_inc(up_done, 1)

            def down(m, gpar, t):
                par = t % 2
                pe.wait_ge(gelu_ready, m + 1)
                pe.wait_ge(w2c_ready, m + 1)
                for j in range(2 * FC):
                    last = pe.matmul(bank[2 + gpar][:, t * P:(t + 1) * P], hid[par][:, j * P:(j + 1) * P],
                                     w2c[t][:, j * P:(j + 1) * P], start=(j == 0), stop=(j == 2 * FC - 1))
                last.then_inc(down_done, 1)

            def group(g, g0, gpar):
                for t in range(GG):
                    up(GG * g + t, t)
                    if t == 0 and g0 > 0:
                        down(GG * g - 1, 1 - gpar, GG - 1)
                    if t == 1:
                        need(pe, sum_ready, g - 1)
                    if t > 0:
                        down(GG * g + t - 1, gpar, t - 1)

            for g in range(4):
                group(g, g, g % 2)
            with pe.Fori(4, N - 1, 2) as g:
                group(g, 4, 0)
                group(g + 1, 5, 1)
            down(NG - 1, 1, GG - 1)


_INS = ["x", "adj", "L0_gnn_W", "L0_gnn_a", "L0_ffn_router_w1", "L0_ffn_router_b1", "L0_ffn_router_w2",
        "L0_ffn_router_b2", "L0_ffn_expert_w1", "L0_ffn_expert_b1", "L0_ffn_expert_w2", "L0_ffn_expert_b2",
        "L0_ffn_expert_w3", "L0_ffn_expert_b3", "L1_gnn_W", "L1_gnn_a", "L1_ffn_Wr", "L1_ffn_br",
        "L1_ffn_W1", "L1_ffn_b1", "L1_ffn_W2", "L1_ffn_b2", "L1_ffn_gamma", "L1_ffn_beta"]


def kernel(**inputs):
    import numpy as _np
    import concourse.bacc as _bacc
    from concourse.bass_utils import run_bass_kernel_spmd as _run

    nc = _bacc.Bacc("TRN2", target_bir_lowering=False, num_devices=1)
    arrays, args = {}, {}
    for name in _INS:
        a = _np.ascontiguousarray(inputs[name])
        arrays["in_" + name] = a
        args[name] = nc.dram_tensor("in_" + name, a.shape, mybir.dt.from_np(a.dtype), kind="ExternalInput").ap()
    out = nc.dram_tensor("out_0", (NG, P, P), F32, kind="ExternalOutput").ap()
    build(nc, args, out)
    r = _run(nc, [arrays], core_ids=[0])
    return r.results[0]["out_0"]
```

```python
import concourse.bass as bass
from concourse import mybir

F32 = mybir.dt.float32
F32R = mybir.dt.float32r
BF16 = mybir.dt.bfloat16
I32 = mybir.dt.int32
U32 = mybir.dt.uint32
ALU = mybir.AluOpType
ACT = mybir.ActivationFunctionType
AX = mybir.AxisListType.X

P = 128
NG = 64
GG = 4
N = NG // GG
GW = GG * P
E0 = 6
RH = 64
E1 = 8
FF = 256
FC = FF // P
SLOPE = 0.2
EPS = 1e-5
MASKED = -5.0e9
LIFT = 2.0 ** 120
JUST_BELOW = -1e-30
CAPACITY = float(-(-NG * P * 5 // (4 * E1)))
ROUTE = 18
AHEAD = 2
KW = 9 * E0
LEAD = {"norm0": 3, "attn0": 2, "route": 1, "experts": 0, "attn1": -1, "pool": -2}


def need(eng, sem, value):
    if not isinstance(value, int) or value > 0:
        eng.wait_ge(sem, value)


def settle(eng, sem, value=1):
    eng.wait_ge(sem, value)


def cols(g):
    return bass.ds(g * GW, GW)


def tiles(ap):
    return ap.rearrange("p (t d) -> p t d", t=GG)


def per_tile(ap):
    return ap.unsqueeze(2).broadcast_to([P, GG, P])


def norm_stage(nc, name):
    st = {}
    st["stats"] = nc.alloc_sbuf_tensor(name + "_stats", [P, GG, 6], F32)
    st["turn"] = nc.alloc_sbuf_tensor(name + "_turn", [P, 1], F32)
    st["mv"] = nc.alloc_sbuf_tensor(name + "_mean_var", [P, GG, 2], F32)
    st["vare"] = nc.alloc_sbuf_tensor(name + "_var_eps", [P, GG], F32)
    st["rstd"] = nc.alloc_sbuf_tensor(name + "_rstd", [P, GG], F32)
    st["stats_ready"] = nc.alloc_semaphore(name + "_stats_ready")
    st["var_ready"] = nc.alloc_semaphore(name + "_var_ready")
    st["vare_ready"] = nc.alloc_semaphore(name + "_vare_ready")
    st["shift"] = nc.alloc_sbuf_tensor(name + "_shift", [P, GG], F32)
    st["shift0"] = nc.alloc_sbuf_tensor(name + "_shift0", [P, GG], F32)
    st["rstd_ready"] = nc.alloc_semaphore(name + "_rstd_ready")
    st["shift_step"] = nc.alloc_semaphore(name + "_shift_step")
    st["xn_ready"] = nc.alloc_semaphore(name + "_xn_ready")
    return st


def norm_measure(st, v, src, g):
    for t in range(GG):
        last = v.bn_stats(st["stats"][:, t, :], src(t))
    last.then_inc(st["stats_ready"], 1)
    v.wait_ge(st["stats_ready"], g + 1)
    need(v, st["xn_ready"], g)
    v.tensor_copy(st["turn"][:, :], st["stats"][:, GG - 1, 0:1])
    for t in range(GG):
        last = v.bn_aggr(st["mv"][:, t, :], st["stats"][:, t, :])
    last.then_inc(st["var_ready"], 1)


def norm_root(st, p, eps, minus_half, g):
    p.wait_ge(st["var_ready"], g + 1)
    p.tensor_tensor(st["vare"][:, :], st["mv"][:, :, 1], eps[:, :], ALU.add).then_inc(st["vare_ready"], 1)
    p.wait_ge(st["vare_ready"], g + 1)
    need(p, st["xn_ready"], g)
    p.tensor_tensor(st["rstd"][:, :], st["vare"][:, :], minus_half[:, :], ALU.pow).then_inc(st["rstd_ready"], 1)


def norm_shift(st, p, minus_one, g):
    p.wait_ge(st["rstd_ready"], g + 1)
    p.tensor_tensor(st["shift0"][:, :], st["mv"][:, :, 0], st["rstd"][:, :], ALU.mult).then_inc(st["shift_step"], 1)
    p.wait_ge(st["shift_step"], 2 * g + 1)
    p.tensor_tensor(st["shift"][:, :], st["shift0"][:, :], minus_one[:, :], ALU.mult)\
        .then_inc(st["shift_step"], 1)


def norm_apply_act(st, a, dst, src, g):
    a.wait_ge(st["shift_step"], 2 * g + 2)
    for t in range(GG):
        last = a.activation(dst(t), src(t), ACT.Identity, bias=st["shift"][:, t:t + 1],
                            scale=st["rstd"][:, t:t + 1])
    last.then_inc(st["xn_ready"], 1)


def norm_apply(st, v, dst, src, g):
    v.wait_ge(st["rstd_ready"], g + 1)
    for t in range(GG):
        last = v.tensor_scalar(dst(t), src(t), st["mv"][:, t, 0:1], st["rstd"][:, t:t + 1],
                               ALU.subtract, ALU.mult)
    last.then_inc(st["xn_ready"], 1)


def attn_stage(nc, name, bank):
    st = {}
    def sb(what, cols=GW, dt=F32):
        return nc.alloc_sbuf_tensor(name + "_" + what, [P, cols], dt)

    def sem(what):
        return nc.alloc_semaphore(name + "_" + what)

    st["norm"] = norm_stage(nc, name)
    st["bank"] = bank
    st["w"] = sb("w", P)
    st["wT"] = sb("wT", P)
    st["a"] = sb("a", 2)
    st["wa"] = sb("wa", 2)
    st["wa1"] = sb("wa1", P)
    st["wa2"] = sb("wa2", P)
    st["xn"] = sb("xn")
    st["xnT"] = sb("xnT")
    st["wh"] = sb("wh")
    st["z"] = sb("z")
    st["lk"] = sb("lk")
    st["pr"] = sb("pr")
    st["prT"] = sb("prT")
    st["mx"] = sb("mx", GG)
    st["nm"] = sb("nm", GG)
    st["sums"] = sb("sums", GG)
    st["rsum"] = sb("rsum", GG)
    st["xnT_done"] = sem("xnT_done")
    st["xnT_ready"] = sem("xnT_ready")
    st["wh_done"] = sem("wh_done")
    st["wh_ready"] = sem("wh_ready")
    st["z_done"] = sem("z_done")
    st["mx_ready"] = sem("mx_ready")
    st["z_ready"] = sem("z_ready")
    st["nm_ready"] = sem("nm_ready")
    st["lk_ready"] = sem("lk_ready")
    st["pr_ready"] = sem("pr_ready")
    st["prT_done"] = sem("prT_done")
    st["prT_ready"] = sem("prT_ready")
    st["rsum_ready"] = sem("rsum_ready")
    st["agg_done"] = sem("agg_done")
    st["y_ready"] = sem("y_ready")
    st["yneg_ready"] = sem("yneg_ready")
    st["yexp_ready"] = sem("yexp_ready")
    st["elu_ready"] = sem("elu_ready")
    st["x_ready"] = sem("x_ready")
    return st


def attn_pe_transpose_xn(st, pe, ident, g):
    pe.wait_ge(st["norm"]["xn_ready"], g + 1)
    need(pe, st["y_ready"], g)
    for t in range(GG):
        last = pe.transpose(st["bank"][:, t * P:(t + 1) * P], st["xn"][:, t * P:(t + 1) * P], ident[:, :])
    last.then_inc(st["xnT_done"], 1)


def attn_pe_project(st, pe, g):
    pe.wait_ge(st["xnT_ready"], g + 1)
    for t in range(GG):
        last = pe.matmul(st["bank"][:, t * P:(t + 1) * P], st["xnT"][:, t * P:(t + 1) * P], st["w"][:, :],
                         start=True, stop=True)
    last.then_inc(st["wh_done"], 1)


def attn_pe_scores(st, pe, identb, mask, g):
    pe.wait_ge(st["wh_ready"], g + 1)
    pe.matmul(st["bank"][:, :], st["wa2"][:, :], st["xnT"][:, :], start=True, stop=False, skip_group_check=True)
    for t in range(GG):
        s = slice(t * P, (t + 1) * P)
        pe.matmul(st["bank"][:, s], st["xnT"][:, s], st["wa1"][:, :], start=False, stop=False,
                  skip_group_check=True)
    pe.matmul(st["bank"][:, :], identb[:, :], mask[:, cols(g)], start=False, stop=True, skip_group_check=True)\
        .then_inc(st["z_done"], 1)


def attn_pe_transpose_probs(st, pe, ident, g):
    pe.wait_ge(st["pr_ready"], g + 1)
    pe.wait_ge(st["z_ready"], g + 1)
    for t in range(GG):
        last = pe.transpose(st["bank"][:, t * P:(t + 1) * P], st["pr"][:, t * P:(t + 1) * P], ident[:, :])
    last.then_inc(st["prT_done"], 1)


def attn_pe_aggregate(st, pe, g):
    pe.wait_ge(st["prT_ready"], g + 1)
    for t in range(GG):
        s = slice(t * P, (t + 1) * P)
        last = pe.matmul(st["bank"][:, s], st["prT"][:, s], st["wh"][:, s], start=True, stop=True)
    last.then_inc(st["agg_done"], 1)

def attn_act_xnT(st, a, g):
    a.wait_ge(st["xnT_done"], g + 1)
    need(a, st["z_done"], g)
    a.activation(st["xnT"][:, :], st["bank"][:, :], ACT.Copy).then_inc(st["xnT_ready"], 1)


def attn_act_wh(st, a, g):
    a.wait_ge(st["wh_done"], g + 1)
    need(a, st["agg_done"], g)
    a.activation(st["wh"][:, :], st["bank"][:, :], ACT.Copy).then_inc(st["wh_ready"], 1)


def attn_act_z(st, a, g):
    a.wait_ge(st["z_done"], g + 1)
    need(a, st["elu_ready"], g)
    a.activation(st["z"][:, :], st["bank"][:, :], ACT.Copy).then_inc(st["z_ready"], 1)


def attn_act_exp(st, a, g):
    a.wait_ge(st["lk_ready"], g + 1)
    a.wait_ge(st["nm_ready"], g + 1)
    need(a, st["elu_ready"], g)
    for t in range(GG):
        s = slice(t * P, (t + 1) * P)
        last = a.activation(st["pr"][:, s], st["lk"][:, s], ACT.Exp, bias=st["nm"][:, t:t + 1],
                            accum_out=st["sums"][:, t:t + 1])
    last.then_inc(st["pr_ready"], 1)


def attn_act_prT(st, a, g):
    a.wait_ge(st["prT_done"], g + 1)
    need(a, st["x_ready"], g)
    a.activation(st["prT"][:, :], st["bank"][:, :], ACT.Copy).then_inc(st["prT_ready"], 1)


def attn_act_elu(st, a, g):
    a.wait_ge(st["y_ready"], g + 1)
    a.activation(st["lk"][:, :], st["z"][:, :], ACT.Exp).then_inc(st["yexp_ready"], 1)
    a.wait_ge(st["yexp_ready"], g + 1)
    a.activation(st["pr"][:, :], st["lk"][:, :], ACT.Relu, bias=1.0, scale=-1.0).then_inc(st["yneg_ready"], 1)

def attn_dve_scores(st, v, g):
    v.wait_ge(st["z_ready"], g + 1)
    v.scalar_tensor_tensor(st["lk"][:, :], st["z"][:, :], SLOPE, st["z"][:, :], ALU.mult, ALU.max)\
        .then_inc(st["lk_ready"], 1)
    v.wait_ge(st["lk_ready"], g + 1)
    v.tensor_reduce(st["mx"][:, :], tiles(st["lk"][:, :]), AX, ALU.max).then_inc(st["mx_ready"], 1)
    v.wait_ge(st["mx_ready"], g + 1)
    v.tensor_scalar(st["nm"][:, :], st["mx"][:, :], -1.0, None, ALU.mult).then_inc(st["nm_ready"], 1)


def attn_dve_rsum(st, v, g):
    v.wait_ge(st["pr_ready"], g + 1)
    v.reciprocal(st["rsum"][:, :], st["sums"][:, :]).then_inc(st["rsum_ready"], 1)


def attn_dve_y(st, v, g):
    v.wait_ge(st["agg_done"], g + 1)
    v.wait_ge(st["rsum_ready"], g + 1)
    v.tensor_tensor(tiles(st["z"][:, :]), tiles(st["bank"][:, :]), per_tile(st["rsum"][:, :]), ALU.mult)\
        .then_inc(st["y_ready"], 1)


def attn_dve_elu(st, v, g):
    v.wait_ge(st["yneg_ready"], g + 1)
    v.scalar_tensor_tensor(st["prT"][:, :], st["pr"][:, :], -1.0, st["z"][:, :], ALU.mult, ALU.max)\
        .then_inc(st["elu_ready"], 1)

def attn_pool_residual(st, p, x, g):
    p.wait_ge(st["elu_ready"], g + 1)
    p.tensor_tensor(x[:, cols(g)], x[:, cols(g)], st["prT"][:, :], ALU.add).then_inc(st["x_ready"], 1)


def build(nc, A, out):
    def sb(name, shape, dt=F32):
        return nc.alloc_sbuf_tensor(name, shape, dt)

    def sem(name):
        return nc.alloc_semaphore(name)

    bank = [nc.alloc_psum_tensor("bank%d" % b, [P, GW], F32) for b in range(8)]
    b_h2, b_h1, b_out, b_wts, b_at0, b_spare, b_at1, b_misc = bank

    const_ready = sem("const_ready")

    x = sb("x", [P, NG * P])
    shift3 = sb("shift3", [P, NG])
    rstd3 = sb("rstd3", [P, NG])
    xnT3 = sb("xnT3", [P, NG * P])
    mask = sb("mask", [P, NG * P], BF16)
    adj_in = sb("adj_in", [P, 2, GW], I32)
    ident = sb("ident", [P, P])
    identb = sb("identb", [P, P], BF16)
    ones = sb("ones", [P, P])
    minus_half = sb("minus_half", [P, GG])
    minus_one = sb("minus_one", [P, GG])
    eps = sb("eps", [P, GG])
    level = sb("level", [P, E0, E0])
    pick = sb("pick", [KW, E0, P], BF16)

    at0 = attn_stage(nc, "at0", b_at0)
    at1 = attn_stage(nc, "at1", b_at1)
    rn = norm_stage(nc, "route")
    pn = norm_stage(nc, "pool")
    r_xn = sb("r_xn", [P, GW])
    p_xn = sb("p_xn", [P, GW])
    xnTh = sb("xnTh", [P, 2, GW], F32R)
    xnTl = sb("xnTl", [P, 2, GW], F32R)
    rw1h = sb("rw1h", [P, RH], F32R)
    rw1l = sb("rw1l", [P, RH], F32R)
    rb1 = sb("rb1", [RH, 1])
    rh = sb("rh", [RH + 1, GW])
    rw2 = sb("rw2", [RH + 1, E0])
    w1h = sb("w1h", [P, E0 * P], F32R)
    w1l = sb("w1l", [P, E0 * P], F32R)
    rowpart = sb("rowpart", [KW, 3])
    w2 = sb("w2", [P, E0, P])
    w3 = sb("w3", [P, E0, P])
    b1 = sb("b1", [P, E0])
    b2 = sb("b2", [P, E0])
    b3 = sb("b3", [KW, P])
    b3r = sb("b3r", [KW, 2, P])
    b3a = sb("b3a", [KW, 3, P], BF16)
    b3p = sb("b3p", [KW, P], BF16)
    h1 = sb("h1", [P, 2, GW])
    h2 = sb("h2", [P, 2, GW])
    h2w = sb("h2w", [P, 2, GW])
    lg = sb("lg", [P, GG, E0])
    lgmx = sb("lgmx", [P, GG])
    lgd = sb("lgd", [P, GG, E0])
    pe0 = sb("pe0", [P, GG, E0])
    psum_ = sb("p_sum", [P, GG])
    prc = sb("p_rcp", [P, GG])
    prob = sb("prob", [P, GG, E0])
    lifted = sb("lifted", [P, GG, E0])
    over = sb("over", [P, GG, E0, E0])
    rank = sb("rank", [P, GG * E0])
    pd = sb("pd", [P, GG, E0])
    pq = sb("pq", [P, GG, E0])
    pqs = sb("pqs", [P, GG, E0])
    qsum = sb("qsum", [P, GG])
    qrc = sb("qrc", [P, GG])
    wgt = sb("wgt", [P, GG, E0])
    wr1 = sb("wr1", [P, GG, E0])
    wparts = sb("wparts", [P, GG, 3, 3, E0], BF16)
    wpT = sb("wpT", [KW, 2, GW], BF16)

    W1 = sb("W1", [P, E1, FF + FC])
    W2 = sb("W2", [P, E1, FF])
    msum = sb("msum", [P, NG])
    wr = sb("wr", [P, E1])
    br = sb("br", [NG, E1])
    B2 = sb("B2", [E1, P])
    gamma = sb("gamma", [P, P])
    beta = sb("beta", [P, P])
    iota8 = sb("iota8", [NG, E1])
    hd = sb("hd", [NG, 12, E1])
    top8 = sb("top8", [NG, 8])
    top8i = sb("top8i", [NG, 8], U32)
    pairs = sb("pairs", [NG, 4])
    diag = sb("diag", [NG, 4, NG])
    gw = sb("gw", [P, 2 * NG])
    gidx = sb("gidx", [P, 2 * (NG + AHEAD)], I32)
    wdT = sb("wdT", [E1, NG])
    bias2 = sb("bias2", [NG, P])
    fn = norm_stage(nc, "final")

    bias2_dram = nc.dram_tensor("bias2_scratch", (NG, P), F32).ap()

    def flat(buf):
        return buf[:, :, :].rearrange("p a f -> p (a f)")[:, 0:2 * (FF + FC)].rearrange("p (k f) -> p k f", k=2)

    w1c = [flat(h1), flat(h2), flat(h2w), sb("w1c", [P, 2, FF + FC])]
    w2c = [at0["wh"], at0["z"], at0["xnT"], r_xn]
    hid = [at0["lk"], at0["pr"], p_xn, w2[:, 0:GG, :].rearrange("p a d -> p (a d)")]
    up_bank = [bank[0], bank[1], bank[4], bank[5]]
    b2b = [at0["prT"], at0["xn"]]
    res = at1["xn"]
    xb = [at1["xnT"], at1["wh"]]
    sm = [at1["z"], at1["lk"]]
    fin = [at1["pr"], at1["prT"]]

    x_loaded = sem("x_loaded")
    adj_loaded = sem("adj_loaded")
    small_loaded = sem("small_loaded")
    early_loaded = sem("early_loaded")
    late_loaded = sem("late_loaded")
    const_step = sem("const_step")
    wT_done = sem("wT_done")
    wT_ready = sem("wT_ready")
    wa_done = sem("wa_done")
    wa_ready = sem("wa_ready")
    split_step = sem("split_step")
    mask_ready = sem("mask_ready")
    r_xnT_done = sem("r_xnT_done")
    xnTh_ready = sem("xnTh_ready")
    xnTl_ready = sem("xnTl_ready")
    rh_done = sem("rh_done")
    rh_ready = sem("rh_ready")
    lg_done = sem("lg_done")
    lg_ready = sem("lg_ready")
    route_step = sem("route_step")
    pe0_ready = sem("pe0_ready")
    pq_ready = sem("pq_ready")
    wpT_done = sem("wpT_done")
    wpT_ready = sem("wpT_ready")
    l1_done = sem("l1_done")
    l2_done = sem("l2_done")
    l3_done = sem("l3_done")
    h1_ready = sem("h1_ready")
    h2_ready = sem("h2_ready")
    wb_done = sem("wb_done")
    h2w_ready = sem("h2w_ready")
    x_experts_ready = sem("x_experts_ready")
    p_xnT_done = sem("p_xnT_done")
    xnT3_ready = sem("xnT3_ready")
    moments_ready = sem("moments_ready")
    res_normed = sem("res_normed")

    head_pe = sem("head_pe")
    head_act = sem("head_act")
    head_dve = sem("head_dve")
    head_diag = sem("head_diag")
    gw_ready = sem("gw_ready")
    gidx_ready = sem("gidx_ready")
    bias2_stored = sem("bias2_stored")
    b2b_loaded = sem("b2b_loaded")
    w1c_ready = sem("w1c_ready")
    w2c_ready = sem("w2c_ready")
    up_done = sem("up_done")
    gelu_ready = sem("gelu_ready")
    down_done = sem("down_done")
    res_ready = sem("res_ready")
    xb_ready = sem("xb_ready")
    sum_ready = sem("sum_ready")
    scaled_ready = sem("scaled_ready")
    fin_ready = sem("fin_ready")
    stored = sem("stored")

    EARLY = 16 * 6
    SMALL = 16 * 16
    LATE = 16 * 10

    def rounds(eng, body):
        for i in range(-3, 3):
            body(i, i)
        with eng.Fori(3, N - 4, 2) as i:
            body(i, 3)
            body(i + 1, 4)
        for i in range(N - 3, N + 2):
            body(i, i)

    def live(stage, i0, shift=0):
        return 0 <= i0 + LEAD[stage] + shift < N

    def newest(i, i0, stage):
        lead = LEAD[stage] + 1
        if isinstance(i, int):
            return max(0, min(i + lead, N))
        return i + lead

    with nc.Block() as block:

        @block.sync
        def _(sp):
            xg = A["x"].rearrange("(g t) p d -> g p t d", t=GG)
            ag = A["adj"].rearrange("(g t) p d -> g p t d", t=GG)

            def load(g, par):
                settle(sp, const_ready)
                need(sp, x_loaded, 16 * g)
                sp.dma_start(tiles(x[:, cols(g)]), xg[g] if isinstance(g, int) else
                             xg[bass.ds(g, 1)].rearrange("a p t d -> p (a t) d")).then_inc(x_loaded, 16)
                settle(sp, const_ready)
                need(sp, adj_loaded, 16 * g)
                need(sp, mask_ready, g - 1)
                sp.dma_start(tiles(adj_in[:, par, :]), ag[g] if isinstance(g, int) else
                             ag[bass.ds(g, 1)].rearrange("a p t d -> p (a t) d")).then_inc(adj_loaded, 16)

            load(0, 0)
            sp.dma_start(at0["w"][:, :], A["L0_gnn_W"]).then_inc(early_loaded, 16)
            sp.dma_start(at1["w"][:, :], A["L1_gnn_W"]).then_inc(early_loaded, 16)
            load(1, 1)
            with sp.Fori(2, N - 1, 2) as g:
                load(g, 0)
                load(g + 1, 1)

            sp.wait_ge(head_dve, 27)
            sp.dma_start(bias2_dram, bias2[:, :]).then_inc(bias2_stored, 16)
            sp.wait_ge(bias2_stored, 16)
            b2g = bias2_dram.rearrange("(g t) d -> g (t d)", t=GG)
            outg = out.rearrange("(g t) p d -> g p t d", t=GG)

            def load_bias(g, par):
                settle(sp, const_ready)
                need(sp, res_ready, g - 1)
                need(sp, b2b_loaded, 16 * g)
                row = b2g[g] if isinstance(g, int) else b2g[bass.ds(g, 1)].rearrange("a d -> (a d)")
                sp.dma_start(b2b[par][:, :], row.partition_broadcast(P)).then_inc(b2b_loaded, 16)

            def store(g, par):
                settle(sp, const_ready)
                sp.wait_ge(fin_ready, g + 1)
                need(sp, stored, 16 * g)
                dst = outg[g] if isinstance(g, int) else outg[bass.ds(g, 1)].rearrange("a p t d -> p (a t) d")
                sp.dma_start(dst, tiles(fin[par][:, :])).then_inc(stored, 16)

            load_bias(0, 0)
            load_bias(1, 1)
            for g in range(2, 4):
                store(g - 2, g % 2)
                load_bias(g, g % 2)
            with sp.Fori(4, N - 1, 2) as g:
                store(g - 2, 0)
                load_bias(g, 0)
                store(g - 1, 1)
                load_bias(g + 1, 1)
            store(N - 2, 0)
            store(N - 1, 1)
            sp.wait_ge(stored, 16 * N)

        @block.gpsimd
        def _(p):
            p.memset(minus_half[:, :], -0.5).then_inc(const_ready, 1)
            p.memset(eps[:, :], EPS).then_inc(const_ready, 1)
            p.memset(minus_one[:, :], -1.0).then_inc(const_ready, 1)
            p.memset(ones[:, :], 1.0).then_inc(const_ready, 1)
            p.memset(ident[:, :], 0.0).then_inc(const_step, 1)
            p.memset(identb[:, :], 0.0).then_inc(const_step, 1)
            p.memset(level[:, :, :], JUST_BELOW).then_inc(const_step, 1)
            p.memset(pick[:, :, :], 0.0).then_inc(const_step, 1)
            p.iota(iota8[:, :], pattern=[[1, E1]], base=0, channel_multiplier=0,
                   allow_small_or_imprecise_dtypes=True).then_inc(const_ready, 1)
            p.wait_ge(const_step, 4)
            for m in (ident, identb):
                p.affine_select(out=m[:, :], in_=m[:, :], compare_op=ALU.not_equal, fill=1.0, base=0,
                                pattern=[[-1, P]], channel_multiplier=1).then_inc(const_ready, 1)
            p.affine_select(out=level[:, :, :], in_=level[:, :, :], compare_op=ALU.is_gt, fill=0.0, base=0,
                            pattern=[[1, E0], [-1, E0]], channel_multiplier=0).then_inc(const_ready, 1)
            for q in range(3):
                p.wait_ge(const_step, 4 + q)
                p.affine_select(out=pick[:, :, :], in_=pick[:, :, :], compare_op=ALU.not_equal, fill=1.0,
                                base=-q * E0, pattern=[[-1, E0], [0, P]], channel_multiplier=1)\
                    .then_inc(const_step, 1)
            p.wait_ge(const_ready, 8)
            p.memset(rowpart[:, :], 1.0).then_inc(const_step, 1)
            p.wait_ge(const_step, 8)
            p.affine_select(out=rowpart[:, :], in_=rowpart[:, :], compare_op=ALU.is_ge, fill=0.0, base=0,
                            pattern=[[-3 * E0, 3]], channel_multiplier=1).then_inc(const_step, 1)
            p.wait_ge(const_step, 9)
            p.affine_select(out=rowpart[:, :], in_=rowpart[:, :], compare_op=ALU.is_ge, fill=0.0,
                            base=3 * E0 - 1, pattern=[[3 * E0, 3]], channel_multiplier=-1)\
                .then_inc(const_step, 1)
            def load_late():
                w2d = A["L1_ffn_W2"].rearrange("e (c f) d -> f e c d", c=FC)
                p.dma_start(W1[:, :, 0:FF], A["L1_ffn_W1"].rearrange("e d f -> d e f")).then_inc(late_loaded, 16)
                for c in range(FC):
                    p.dma_start(W2[:, :, c * P:(c + 1) * P], w2d[:, :, c, :]).then_inc(late_loaded, 16)
                with nc.allow_non_contiguous_dma(reason="bias columns, once"):
                    for c in range(FC):
                        p.dma_start(W1[:, :, FF + c], A["L1_ffn_b1"][:, c * P:(c + 1) * P].rearrange("e p -> p e"))\
                            .then_inc(late_loaded, 16)
                p.dma_start(wr[:, :], A["L1_ffn_Wr"]).then_inc(late_loaded, 16)
                p.dma_start(br[:, :], A["L1_ffn_br"].partition_broadcast(NG)).then_inc(late_loaded, 16)
                p.dma_start(B2[:, :], A["L1_ffn_b2"]).then_inc(late_loaded, 16)
                p.dma_start(gamma[:, :], A["L1_ffn_gamma"].partition_broadcast(P)).then_inc(late_loaded, 16)
                p.dma_start(beta[:, :], A["L1_ffn_beta"].partition_broadcast(P)).then_inc(late_loaded, 16)

            def body(i, i0):
                if live("attn1", i0):
                    norm_root(at1["norm"], p, eps, minus_half, i - 1)
                if live("attn0", i0, -1):
                    attn_pool_residual(at0, p, x, i + 1)
                if live("route", i0):
                    norm_root(rn, p, eps, minus_half, i + 1)
                if live("norm0", i0):
                    norm_root(at0["norm"], p, eps, minus_half, i + 3)
                    norm_shift(at0["norm"], p, minus_one, i + 3)
                if live("attn1", i0, -1):
                    attn_pool_residual(at1, p, x, i - 2)
                if live("pool", i0):
                    g = i - 2
                    norm_root(pn, p, eps, minus_half, g)
                    norm_shift(pn, p, minus_one, g)
                    p.tensor_copy(rstd3[:, bass.ds(g * GG, GG)], pn["rstd"][:, :])
                    p.wait_ge(pn["shift_step"], 2 * g + 2)
                    p.tensor_copy(shift3[:, bass.ds(g * GG, GG)], pn["shift"][:, :]).then_inc(moments_ready, 1)
                if i0 == -LEAD["norm0"]:
                    load_late()

            rounds(p, body)

            p.wait_ge(late_loaded, LATE)

            def group(g, g0, par):
                if g0 > 1:
                    finish(g - 2, par)
                need(p, fin_ready, g - 1)
                p.tensor_tensor(tiles(xb[par][:, :]), tiles(x[:, cols(g)]),
                                beta[:, :].unsqueeze(1).broadcast_to([P, GG, P]), ALU.add).then_inc(xb_ready, 1)
                if g0 > 0:
                    norm_root(fn, p, eps, minus_half, g - 1)
                    norm_shift(fn, p, minus_one, g - 1)
                p.wait_ge(b2b_loaded, 16 * g + 16)
                p.wait_ge(res_normed, g + 1)
                p.tensor_tensor(res[:, :], res[:, :], b2b[par][:, :], ALU.add).then_inc(res_ready, 1)

            def finish(g, par):
                p.wait_ge(fn["xn_ready"], g + 1)
                p.tensor_tensor(tiles(sm[par][:, :]), tiles(sm[par][:, :]),
                                gamma[:, :].unsqueeze(1).broadcast_to([P, GG, P]), ALU.mult)\
                    .then_inc(scaled_ready, 1)
                p.wait_ge(scaled_ready, g + 1)
                p.wait_ge(xb_ready, g + 1)
                need(p, stored, 16 * (g - 1))
                p.tensor_tensor(fin[par][:, :], sm[par][:, :], xb[par][:, :], ALU.add).then_inc(fin_ready, 1)

            for g in range(4):
                group(g, g, g % 2)
            with p.Fori(4, N - 1, 2) as g:
                group(g, 4, 0)
                group(g + 1, 5, 1)
            finish(N - 2, 0)
            norm_root(fn, p, eps, minus_half, N - 1)
            finish(N - 1, 1)

        @block.scalar
        def _(a):
            with nc.allow_non_contiguous_dma(reason="bias columns, once"):
                a.dma_start(at0["a"][:, :], A["L0_gnn_a"].rearrange("(t p) -> p t", p=P)).then_inc(early_loaded, 16)
                a.dma_start(at1["a"][:, :], A["L1_gnn_a"].rearrange("(t p) a -> p (t a)", p=P))\
                    .then_inc(early_loaded, 16)
                a.dma_start(h1[:, :, :].rearrange("p a f -> p (a f)")[:, 0:E0 * P],
                            A["L0_ffn_expert_w1"].rearrange("e d h -> d e h")).then_inc(early_loaded, 16)
                a.dma_start(h2[:, 0, 0:RH], A["L0_ffn_router_w1"]).then_inc(early_loaded, 16)
                a.dma_start(rb1[:, :], A["L0_ffn_router_b1"].unsqueeze(1)).then_inc(small_loaded, 16)
                a.dma_start(rw2[0:RH, :], A["L0_ffn_router_w2"]).then_inc(small_loaded, 16)
                a.dma_start(rw2[RH:RH + 1, :], A["L0_ffn_router_b2"].unsqueeze(0)).then_inc(small_loaded, 16)
                a.dma_start(b1[:, :], A["L0_ffn_expert_b1"].rearrange("e p -> p e")).then_inc(small_loaded, 16)
                a.dma_start(b2[:, :], A["L0_ffn_expert_b2"].rearrange("e p -> p e")).then_inc(small_loaded, 16)
                for q in range(9):
                    a.dma_start(b3[q * E0:(q + 1) * E0, :], A["L0_ffn_expert_b3"]).then_inc(small_loaded, 16)
                a.dma_start(w2[:, :, :], A["L0_ffn_expert_w2"].rearrange("e d h -> d e h"))\
                    .then_inc(small_loaded, 16)
                a.dma_start(w3[:, :, :], A["L0_ffn_expert_w3"].rearrange("e d h -> d e h"))\
                    .then_inc(small_loaded, 16)

            def relu2(n, e):
                a.wait_ge(l2_done, n + 1)
                need(a, h2w_ready, n - 1)
                a.activation(h2[:, e % 2, :], b_h2[:, :], ACT.Relu, bias=b2[:, e:e + 1]).then_inc(h2_ready, 1)

            def relu1(n, e):
                a.wait_ge(l1_done, n + 1)
                a.activation(h1[:, e % 2, :], b_h1[:, :], ACT.Relu, bias=b1[:, e:e + 1]).then_inc(h1_ready, 1)

            def x_tile(g):
                return lambda t: x[:, bass.ds(g * GW + t * P, P)]

            def buf_tile(buf):
                return lambda t: buf[:, t * P:(t + 1) * P]

            def body(i, i0):
                run = live("experts", i0)
                if i0 == -LEAD["route"]:
                    a.wait_ge(small_loaded, SMALL)
                    a.wait_ge(split_step, 4)
                attn0, attn1, route, pool = (live(k, i0) for k in ("attn0", "attn1", "route", "pool"))
                n = i * E0
                if run:
                    relu2(n, 0)
                if live("attn1", i0, -1):
                    attn_act_prT(at1, a, i - 2)
                if attn0:
                    attn_act_xnT(at0, a, i + 2)
                if run:
                    relu1(n + 1, 1)
                if live("attn0", i0, -1):
                    attn_act_elu(at0, a, i + 1)
                if attn0:
                    attn_act_wh(at0, a, i + 2)
                if run:
                    relu2(n + 1, 1)
                    relu1(n + 2, 2)
                if live("attn1", i0, -1):
                    attn_act_elu(at1, a, i - 2)
                if run:
                    relu2(n + 2, 2)
                if attn0:
                    attn_act_z(at0, a, i + 2)
                if attn1:
                    attn_act_xnT(at1, a, i - 1)
                if run:
                    relu1(n + 3, 3)
                if route:
                    g = i + 1
                    a.wait_ge(r_xnT_done, g + 1)
                    need(a, l1_done, (g - 1) * E0)
                    a.activation(xnTh[:, (i0 + 1) % 2, :], b_misc[:, :], ACT.Copy).then_inc(xnTh_ready, 1)
                if attn0:
                    attn_act_exp(at0, a, i + 2)
                if attn1:
                    attn_act_wh(at1, a, i - 1)
                if run:
                    relu2(n + 3, 3)
                if run:
                    relu1(n + 4, 4)
                if live("norm0", i0):
                    need(a, at0["xnT_done"], i + 3)
                    norm_apply_act(at0["norm"], a, buf_tile(at0["xn"]), x_tile(i + 3), i + 3)
                if route:
                    g = i + 1
                    a.wait_ge(rh_done, g + 1)
                    need(a, lg_done, g)
                    a.activation(rh[0:RH, :], b_misc[0:RH, :], ACT.Relu, bias=rb1[:, :]).then_inc(rh_ready, 1)
                if attn0:
                    attn_act_prT(at0, a, i + 2)
                if run:
                    relu2(n + 4, 4)
                if attn1:
                    attn_act_z(at1, a, i - 1)
                if run:
                    relu1(n + 5, 5)
                if route:
                    a.wait_ge(route_step, ROUTE * (i + 1) + 2)
                    a.activation(pe0[:, :, :], lgd[:, :, :], ACT.Exp).then_inc(pe0_ready, 1)
                if pool:
                    need(a, p_xnT_done, i - 2)
                    norm_apply_act(pn, a, buf_tile(p_xn), x_tile(i - 2), i - 2)
                if run:
                    relu2(n + 5, 5)
                if live("experts", i0, 1):
                    relu1(n + 6, 0)
                if route:
                    a.wait_ge(route_step, ROUTE * (i + 1) + 7)
                    a.activation(pq[:, :, :], pd[:, :, :], ACT.Exp).then_inc(pq_ready, 1)
                if attn1:
                    attn_act_exp(at1, a, i - 1)
                if pool:
                    g = i - 2
                    a.wait_ge(p_xnT_done, g + 1)
                    for t in range(GG):
                        m = bass.ds(g * GG + t, 1)
                        last = a.activation(xnT3[:, bass.ds(g * GW + t * P, P)], b_misc[:, t * P:(t + 1) * P],
                                            ACT.Copy, accum_out=msum[:, m])
                    last.then_inc(xnT3_ready, 1)

            rounds(a, body)

            for at, dst, src in ((3, hd[:, 3, :], hd[:, 1, :]), (12, hd[:, 8, :], hd[:, 7, :]),
                                 (19, hd[:, 11, 0:2], hd[:, 10, 0:2])):
                a.wait_ge(head_dve, at)
                a.activation(dst, src, ACT.Exp).then_inc(head_act, 1)

            def gelus(m, t):
                a.wait_ge(up_done, m + 1)
                need(a, down_done, m - 3)
                for k in range(2):
                    for c in range(FC):
                        s = slice((FC * k + c) * P, (FC * k + c + 1) * P)
                        last = a.activation(hid[t][:, s], up_bank[t][:, s], ACT.Gelu,
                                            bias=w1c[t][:, k, FF + c:FF + c + 1])
                last.then_inc(gelu_ready, 1)

            def group(g, g0, par):
                for t in range(GG):
                    gelus(GG * g + t, t)
                    if t == 3:
                        need(a, sum_ready, g)
                        for q in range(GG):
                            m = bass.ds(g * GG + q, 1)
                            last = a.activation(res[:, q * P:(q + 1) * P], x_tile(g)(q), ACT.Identity,
                                                bias=shift3[:, m], scale=rstd3[:, m])
                        last.then_inc(res_normed, 1)
                    if t == 1 and g0 > 1:
                        norm_apply_act(fn, a, buf_tile(sm[par]), buf_tile(sm[par]), g - 2)

            for g in range(4):
                group(g, g, g % 2)
            with a.Fori(4, N - 1, 2) as g:
                group(g, 4, 0)
                group(g + 1, 5, 1)
            norm_apply_act(fn, a, buf_tile(sm[0]), buf_tile(sm[0]), N - 2)

        @block.vector
        def _(v):
            for j, at in enumerate((at0, at1)):
                v.wait_ge(wT_done, j + 1)
                v.tensor_copy(at["wT"][:, :], at["bank"][:, 0:P]).then_inc(wT_ready, 1)
            for j, at in enumerate((at0, at1)):
                v.wait_ge(wa_done, 2)
                v.tensor_copy(at["wa"][:, :], b_misc[:, 2 * j:2 * j + 2]).then_inc(wa_ready, 1)
            v.wait_ge(wa_ready, 2)
            v.wait_ge(const_ready, 8)
            for at in (at0, at1):
                v.tensor_scalar(at["wa1"][:, :], ones[:, :], at["wa"][:, 0:1], None, ALU.mult)
                v.tensor_scalar(at["wa2"][:, :], ones[:, :], at["wa"][:, 1:2], None, ALU.mult).then_inc(wa_ready, 1)
            def split_w1():
                v.wait_ge(early_loaded, EARLY)
                raw = h1[:, :, :].rearrange("p a f -> p (a f)")[:, 0:E0 * P]
                v.tensor_copy(w1h[:, :], raw).then_inc(split_step, 1)
                v.tensor_copy(rw1h[:, :], h2[:, 0, 0:RH]).then_inc(split_step, 1)
                v.wait_ge(split_step, 2)
                v.tensor_tensor(w1l[:, :], raw, w1h[:, :].bitcast(F32), ALU.subtract).then_inc(split_step, 1)
                v.tensor_tensor(rw1l[:, :], h2[:, 0, 0:RH], rw1h[:, :].bitcast(F32), ALU.subtract)\
                    .then_inc(split_step, 1)

            def split_b3():
                v.wait_ge(small_loaded, SMALL)
                v.wait_ge(const_step, 10)
                v.tensor_copy(b3a[:, 0, :], b3[:, :]).then_inc(split_step, 1)
                v.wait_ge(split_step, 5)
                v.tensor_tensor(b3r[:, 0, :], b3[:, :], b3a[:, 0, :], ALU.subtract).then_inc(split_step, 1)
                v.wait_ge(split_step, 6)
                v.tensor_copy(b3a[:, 1, :], b3r[:, 0, :]).then_inc(split_step, 1)
                v.wait_ge(split_step, 7)
                v.tensor_tensor(b3a[:, 2, :], b3r[:, 0, :], b3a[:, 1, :], ALU.subtract).then_inc(split_step, 1)
                v.wait_ge(split_step, 8)
                v.tensor_scalar(b3r[:, 0, :], b3a[:, 0, :], rowpart[:, 0:1], None, ALU.mult).then_inc(split_step, 1)
                v.wait_ge(split_step, 9)
                v.scalar_tensor_tensor(b3r[:, 1, :], b3a[:, 1, :], rowpart[:, 1:2], b3r[:, 0, :], ALU.mult, ALU.add)\
                    .then_inc(split_step, 1)
                v.wait_ge(split_step, 10)
                v.scalar_tensor_tensor(b3p[:, :], b3a[:, 2, :], rowpart[:, 2:3], b3r[:, 1, :], ALU.mult, ALU.add)\
                    .then_inc(split_step, 1)
                v.memset(gidx[:, 2 * NG:], 0).then_inc(gidx_ready, 1)
                v.memset(rh[RH:RH + 1, :], 1.0).then_inc(split_step, 1)

            def x_tile(g):
                return lambda t: x[:, bass.ds(g * GW + t * P, P)]

            def buf_tile(buf):
                return lambda t: buf[:, t * P:(t + 1) * P]

            def make_mask(g, par):
                v.wait_ge(adj_loaded, 16 * g + 16)
                v.tensor_scalar(mask[:, cols(g)], adj_in[:, par, :], 0.0, MASKED, ALU.is_le, ALU.mult)\
                    .then_inc(mask_ready, 1)

            def weigh(n, e):
                v.wait_ge(h2_ready, n + 1)
                v.wait_ge(wb_done, n + 1)
                need(v, l3_done, n - 1)
                v.tensor_tensor(h2w[:, e % 2, :], h2[:, e % 2, :], b_wts[:, :], ALU.mult).then_inc(h2w_ready, 1)

            def route_first(g):
                base = ROUTE * g
                v.wait_ge(lg_done, g + 1)
                v.tensor_copy(lg[:, :, :], b_misc[:, 0:GG * E0].rearrange("p (t e) -> p t e", t=GG))\
                    .then_inc(lg_ready, 1)
                v.wait_ge(lg_ready, g + 1)
                v.tensor_reduce(lgmx[:, :], lg[:, :, :], AX, ALU.max).then_inc(route_step, 1)
                v.wait_ge(route_step, base + 1)
                v.tensor_tensor(lgd[:, :, :], lg[:, :, :], lgmx[:, :].unsqueeze(2).broadcast_to([P, GG, E0]),
                                ALU.subtract).then_inc(route_step, 1)

            def route_rank(g):
                base = ROUTE * g
                v.wait_ge(pe0_ready, g + 1)
                v.tensor_reduce(psum_[:, :], pe0[:, :, :], AX, ALU.add).then_inc(route_step, 1)
                v.wait_ge(route_step, base + 3)
                v.reciprocal(prc[:, :], psum_[:, :]).then_inc(route_step, 1)
                v.wait_ge(route_step, base + 4)
                v.tensor_tensor(prob[:, :, :], pe0[:, :, :], prc[:, :].unsqueeze(2).broadcast_to([P, GG, E0]),
                                ALU.mult).then_inc(route_step, 1)
                v.scalar_tensor_tensor(lifted[:, :, :], pe0[:, :, :], LIFT,
                                       prc[:, :].unsqueeze(2).broadcast_to([P, GG, E0]), ALU.mult, ALU.mult)\
                    .then_inc(route_step, 1)
                v.wait_ge(route_step, base + 5)
                v.tensor_tensor(pd[:, :, :], prob[:, :, :], prc[:, :].unsqueeze(2).broadcast_to([P, GG, E0]),
                                ALU.subtract).then_inc(route_step, 1)
                v.wait_ge(route_step, base + 6)
                mine = lifted[:, :, :].unsqueeze(3).broadcast_to([P, GG, E0, E0])
                other = lifted[:, :, :].unsqueeze(2).broadcast_to([P, GG, E0, E0])
                v.tensor_tensor(over[:, :, :, :], other, mine, ALU.subtract).then_inc(route_step, 1)
                lv = level[:, :, :].rearrange("p a b -> p (a b)").unsqueeze(1).broadcast_to([P, GG, E0 * E0])
                over3 = over[:, :, :, :].rearrange("p t a b -> p t (a b)")
                v.wait_ge(route_step, base + 8)
                v.tensor_tensor(over3, over3, lv, ALU.is_gt).then_inc(route_step, 1)
                v.wait_ge(route_step, base + 9)
                v.tensor_reduce(rank[:, :], over[:, :, :, :].rearrange("p t a b -> p (t a) b"), AX, ALU.add)\
                    .then_inc(route_step, 1)

            def route_weights(g):
                base = ROUTE * g
                v.wait_ge(pq_ready, g + 1)
                v.wait_ge(route_step, base + 10)
                v.scalar_tensor_tensor(pqs[:, :, :].rearrange("p t e -> p (t e)"), rank[:, :], 2.0,
                                       pq[:, :, :].rearrange("p t e -> p (t e)"), ALU.is_lt, ALU.mult)\
                    .then_inc(route_step, 1)
                v.wait_ge(route_step, base + 11)
                v.tensor_reduce(qsum[:, :], pqs[:, :, :], AX, ALU.add).then_inc(route_step, 1)
                v.wait_ge(route_step, base + 12)
                v.reciprocal(qrc[:, :], qsum[:, :]).then_inc(route_step, 1)
                v.wait_ge(route_step, base + 13)
                v.tensor_tensor(wgt[:, :, :], pqs[:, :, :], qrc[:, :].unsqueeze(2).broadcast_to([P, GG, E0]),
                                ALU.mult).then_inc(route_step, 1)
                v.wait_ge(route_step, base + 14)
                need(v, wpT_done, g)
                v.tensor_copy(wparts[:, :, :, 0, :], wgt[:, :, :].unsqueeze(2).broadcast_to([P, GG, 3, E0])).then_inc(route_step, 1)
                v.wait_ge(route_step, base + 15)
                v.tensor_tensor(wr1[:, :, :], wgt[:, :, :], wparts[:, :, 0, 0, :], ALU.subtract)\
                    .then_inc(route_step, 1)
                v.wait_ge(route_step, base + 16)
                v.tensor_copy(wparts[:, :, :, 1, :], wr1[:, :, :].unsqueeze(2).broadcast_to([P, GG, 3, E0])).then_inc(route_step, 1)
                v.wait_ge(route_step, base + 17)
                v.tensor_tensor(wparts[:, :, :, 2, :], wr1[:, :, :].unsqueeze(2).broadcast_to([P, GG, 3, E0]),
                                wparts[:, :, :, 1, :], ALU.subtract)\
                    .then_inc(route_step, 1)

            def measure(st, g, source_ready, value):
                settle(v, const_ready)
                if st is pn:
                    need(v, moments_ready, g)
                v.wait_ge(source_ready, value)
                need(v, st["var_ready"], g)
                norm_measure(st, v, x_tile(g), g)

            def body(i, i0):
                run = live("experts", i0)
                n = i * E0
                attn0, attn1, route, pool = (live(k, i0) for k in ("attn0", "attn1", "route", "pool"))
                if run:
                    v.wait_ge(wpT_done, i + 1)
                    need(v, wb_done, (i - 1) * E0)
                    v.tensor_copy(wpT[:, i0 % 2, :], b_misc[0:KW, 0:GW // 2].bitcast(BF16)).then_inc(wpT_ready, 1)
                if live("experts", i0, -1):
                    v.wait_ge(l3_done, i * E0)
                    v.tensor_tensor(x[:, cols(i - 1)], b_out[:, :], x[:, cols(i - 1)], ALU.add)\
                        .then_inc(x_experts_ready, 1)
                if attn1:
                    measure(at1["norm"], i - 1, x_experts_ready, i)
                if live("attn0", i0, -1):
                    attn_dve_elu(at0, v, i + 1)
                if live("attn1", i0, -1):
                    attn_dve_y(at1, v, i - 2)
                if run:
                    weigh(n, 0)
                if attn1:
                    need(v, at1["xnT_done"], i - 1)
                    norm_apply(at1["norm"], v, buf_tile(at1["xn"]), x_tile(i - 1), i - 1)
                if route:
                    measure(rn, i + 1, at0["x_ready"], i + 2)
                if live("norm0", i0):
                    measure(at0["norm"], i + 3, x_loaded, 16 * (i + 3) + 16)
                if route:
                    need(v, r_xnT_done, i + 1)
                    norm_apply(rn, v, buf_tile(r_xn), x_tile(i + 1), i + 1)
                if run:
                    weigh(n + 1, 1)
                if live("attn1", i0, -1):
                    attn_dve_elu(at1, v, i - 2)
                if attn0:
                    attn_dve_scores(at0, v, i + 2)
                if route:
                    g = i + 1
                    par = (i0 + 1) % 2
                    v.wait_ge(xnTh_ready, g + 1)
                    v.tensor_tensor(xnTl[:, par, :], b_misc[:, :], xnTh[:, par, :].bitcast(F32),
                                    ALU.subtract).then_inc(xnTl_ready, 1)
                if run:
                    weigh(n + 2, 2)
                if pool:
                    measure(pn, i - 2, at1["x_ready"], i - 1)
                if live("norm0", i0):
                    make_mask(i + 3, (i0 + 1) % 2)
                if i0 == -LEAD["norm0"]:
                    split_w1()
                if attn0:
                    attn_dve_rsum(at0, v, i + 2)
                if i0 == -LEAD["attn0"]:
                    split_b3()
                if run:
                    weigh(n + 3, 3)
                if route:
                    route_first(i + 1)
                if attn1:
                    attn_dve_scores(at1, v, i - 1)
                if run:
                    weigh(n + 4, 4)
                if route:
                    route_rank(i + 1)
                if attn0:
                    attn_dve_y(at0, v, i + 2)
                if run:
                    weigh(n + 5, 5)
                if route:
                    route_weights(i + 1)
                if attn1:
                    attn_dve_rsum(at1, v, i - 1)

            rounds(v, body)

            count = [0]

            def step(ins):
                count[0] += 1
                ins.then_inc(head_dve, 1)
                v.wait_ge(head_dve, count[0])

            def h(j, w=E1):
                return hd[:, j, 0:w]

            def softmax(src, e, j):
                step(v.tensor_reduce(h(j, 1), src, AX, ALU.max))
                step(v.tensor_scalar(e, src, h(j, 1), None, ALU.subtract))

            def softmax_end(e, dst, j, nth):
                v.wait_ge(head_act, nth)
                step(v.tensor_reduce(h(j, 1), e, AX, ALU.add))
                step(v.reciprocal(h(j, 1), h(j, 1)))
                step(v.tensor_scalar(dst, e, h(j, 1), None, ALU.mult))

            v.wait_ge(late_loaded, LATE)
            v.wait_ge(head_pe, 1)
            step(v.scalar_tensor_tensor(h(0), b_misc[0:NG, 0:E1], 1.0 / P, br[:, :], ALU.mult, ALU.add))
            softmax(h(0), h(1), 2)
            softmax_end(h(3), h(4), 2, 1)
            v.wait_ge(head_pe, 2)
            step(v.tensor_scalar(h(5), b_misc[0:NG, 0:E1], float(P), None, ALU.mult))
            step(v.reciprocal(h(5), h(5)))
            step(v.tensor_scalar(h(5), h(5), CAPACITY, 1.0, ALU.mult, ALU.min))
            step(v.tensor_tensor(h(6), h(4), h(5), ALU.mult))
            softmax(h(6), h(7), 2)
            softmax_end(h(8), h(9), 2, 2)
            step(v.max(top8[:, :], h(9)))
            step(v.max_index(top8i[:, :], top8[:, :], h(9)))
            step(v.tensor_copy(pairs[:, 2:4], top8i[:, 0:2]))
            step(v.tensor_scalar(h(10, 2), top8[:, 0:2], top8[:, 0:1], None, ALU.subtract))
            softmax_end(h(11, 2), pairs[:, 0:2], 2, 3)
            for q in range(4):
                v.tensor_scalar(diag[:, q, :], ident[0:NG, 0:NG], pairs[:, q:q + 1], None, ALU.mult)\
                    .then_inc(head_diag, 1)
            step(v.tensor_scalar(h(0), iota8[:, :], pairs[:, 2:3], pairs[:, 0:1], ALU.is_equal, ALU.mult))
            step(v.tensor_scalar(h(1), iota8[:, :], pairs[:, 3:4], pairs[:, 1:2], ALU.is_equal, ALU.mult))
            step(v.tensor_tensor(h(2), h(0), h(1), ALU.add))
            v.wait_ge(head_pe, 3)
            v.tensor_scalar(gidx[:, 0:2 * NG].rearrange("p (m k) -> p k m", k=2),
                            bank[0][:, 2 * NG:4 * NG].rearrange("p (k m) -> p k m", k=2),
                            float(E1 - 1), 0.0, ALU.min, ALU.max).then_inc(gidx_ready, 1)
            v.tensor_copy(gw[:, :], bank[0][:, 0:2 * NG]).then_inc(gw_ready, 1)
            v.wait_ge(head_pe, 4)
            step(v.tensor_copy(wdT[:, :], b_misc[0:E1, 0:NG]))
            v.wait_ge(gidx_ready, 2)
            v.wait_ge(gw_ready, 1)

            def chosen(first, count):
                return nc.values_load_multi_w_load_instructions(
                    gidx[0:1, bass.ds(first * 2, 2 * count)], engines=(mybir.EngineType.DVE,),
                    min_val=0, max_val=E1 - 1,
                    skip_runtime_bounds_check_because="clamped to these bounds where gidx is written")[1]

            def choose_w1(m, t, experts):
                need(v, gelu_ready, m - 3)
                for k, e in enumerate(experts):
                    last = v.tensor_copy(w1c[t][:, k, :], W1[:, bass.ds(e, 1), :].rearrange("p a f -> p (a f)"))
                last.then_inc(w1c_ready, 1)

            def choose_w2(m, t, experts):
                need(v, down_done, m - 3)
                for k, e in enumerate(experts):
                    last = v.tensor_scalar(w2c[t][:, k * FF:(k + 1) * FF],
                                           W2[:, bass.ds(e, 1), :].rearrange("p a f -> p (a f)"),
                                           gw[:, bass.ds(m + k * NG, 1)], None, ALU.mult)
                last.then_inc(w2c_ready, 1)

            def tail_sum(g, par):
                v.wait_ge(down_done, GG * g + GG)
                v.wait_ge(res_ready, g + 1)
                need(v, scaled_ready, g - 1)
                need(v, fin_ready, g - 1)
                v.tensor_tensor(sm[par][:, :], bank[2 + par][:, :], res[:, :], ALU.add).then_inc(sum_ready, 1)
                settle(v, const_ready)
                v.wait_ge(sum_ready, g + 1)
                norm_measure(fn, v, buf_tile(sm[par]), g)

            def group(g, g0, par):
                experts = chosen(GG * g, GG + AHEAD)
                for t in range(GG):
                    choose_w1(GG * g + t + AHEAD, (t + AHEAD) % GG, experts[2 * (t + AHEAD):2 * (t + AHEAD) + 2])
                    choose_w2(GG * g + t, t, experts[2 * t:2 * t + 2])
                    if t == GG - 1 and isinstance(g, int) and g == 0:
                        v.wait_ge(head_pe, 5)
                        step(v.tensor_copy(bias2[:, :], b_misc[0:NG, 0:P]))
                if g0 > 0:
                    tail_sum(g - 1, 1 - par)

            for m in range(AHEAD):
                choose_w1(m, m, chosen(m, 1))
            for g in range(4):
                group(g, g, g % 2)
            with v.Fori(4, N - 1, 2) as g:
                group(g, 4, 0)
                group(g + 1, 5, 1)
            tail_sum(N - 1, 1)
            norm_apply(fn, v, buf_tile(sm[1]), buf_tile(sm[1]), N - 1)

        @block.tensor
        def _(pe):
            pe.wait_ge(early_loaded, EARLY)
            pe.wait_ge(const_ready, 8)
            for at in (at0, at1):
                pe.transpose(at["bank"][:, 0:P], at["w"][:, :], ident[:, :]).then_inc(wT_done, 1)
            pe.wait_ge(wT_ready, 2)
            for j, at in enumerate((at0, at1)):
                pe.matmul(b_misc[:, 2 * j:2 * j + 2], at["wT"][:, :], at["a"][:, :], start=True, stop=True)\
                    .then_inc(wa_done, 1)
            pe.wait_ge(wa_ready, 4)

            def layer1(n, g, par, e):
                ws = slice(e * P, (e + 1) * P)
                pe.matmul(b_h1[:, :], w1h[:, ws], xnTh[:, par, :], start=True, stop=False)
                pe.matmul(b_h1[:, :], w1l[:, ws], xnTh[:, par, :], start=False, stop=False)
                pe.matmul(b_h1[:, :], w1h[:, ws], xnTl[:, par, :], start=False, stop=True)\
                    .then_inc(l1_done, 1)

            def layer2(n, e):
                pe.wait_ge(h1_ready, n + 1)
                need(pe, h2_ready, n)
                pe.matmul(b_h2[:, :], w2[:, e, :], h1[:, e % 2, :], start=True, stop=True).then_inc(l2_done, 1)

            def spread_weights(n, par, e):
                need(pe, h2w_ready, n)
                pe.matmul(b_wts[:, :], pick[:, e, :], wpT[:, par, :], start=True, stop=True).then_inc(wb_done, 1)

            def bias3(g, par):
                need(pe, x_experts_ready, g)
                for t in range(GG):
                    s = slice(t * P, (t + 1) * P)
                    pe.matmul(b_out[:, s], wpT[:, par, s], b3p[:, :], start=(t == 0), stop=False,
                              skip_group_check=True)

            def layer3(n, e):
                pe.wait_ge(h2w_ready, n + 1)
                for t in range(GG):
                    s = slice(t * P, (t + 1) * P)
                    last = pe.matmul(b_out[:, s], h2w[:, e % 2, s], w3[:, e, :], start=False,
                                     stop=(e == E0 - 1), skip_group_check=True)
                last.then_inc(l3_done, 1)

            def weights_transpose(i):
                for t in range(GG):
                    last = pe.transpose(b_misc[:, :].bitcast(BF16)[0:KW, t * P:(t + 1) * P],
                                        wparts[:, t, :, :, :].rearrange("p a b e -> p (a b e)"), identb[:, :])
                last.then_inc(wpT_done, 1)

            def route_transpose(i, i0):
                pe.wait_ge(rn["xn_ready"], i + 2)
                need(pe, wpT_ready, newest(i, i0, "experts"))
                need(pe, xnT3_ready, newest(i - 1, i0 - 1, "pool"))
                for t in range(GG):
                    q = slice(t * P, (t + 1) * P)
                    last = pe.transpose(b_misc[:, q], r_xn[:, q], ident[:, :])
                last.then_inc(r_xnT_done, 1)

            def route_hidden(g, par):
                pe.wait_ge(xnTh_ready, g + 1)
                pe.wait_ge(xnTl_ready, g + 1)
                pe.matmul(b_misc[0:RH, :], rw1h[:, :], xnTh[:, par, :], start=True, stop=False)
                pe.matmul(b_misc[0:RH, :], rw1l[:, :], xnTh[:, par, :], start=False, stop=False)
                pe.matmul(b_misc[0:RH, :], rw1h[:, :], xnTl[:, par, :], start=False, stop=True)\
                    .then_inc(rh_done, 1)

            def route_logits(g):
                pe.wait_ge(rh_ready, g + 1)
                for t in range(GG):
                    last = pe.matmul(b_misc[:, t * E0:(t + 1) * E0], rh[:, t * P:(t + 1) * P], rw2[:, :],
                                     start=True, stop=True)
                last.then_inc(lg_done, 1)

            def pool_transpose(i, i0):
                g = i - 2
                pe.wait_ge(pn["xn_ready"], g + 1)
                need(pe, lg_ready, newest(i, i0, "route"))
                need(pe, wpT_ready, newest(i, i0, "experts"))
                need(pe, xnT3_ready, g)
                for t in range(GG):
                    q = slice(t * P, (t + 1) * P)
                    last = pe.transpose(b_misc[:, q], p_xn[:, q], ident[:, :])
                last.then_inc(p_xnT_done, 1)

            def body(i, i0):
                run = live("experts", i0)
                attn0, attn1, route, pool = (live(k, i0) for k in ("attn0", "attn1", "route", "pool"))
                par = i0 % 2
                n = i * E0
                if i0 == -LEAD["route"]:
                    pe.wait_ge(small_loaded, SMALL)
                    pe.wait_ge(split_step, 12)
                    pe.wait_ge(const_step, 7)
                if run:
                    layer2(n, 0)
                if live("attn1", i0, -1):
                    attn_pe_transpose_probs(at1, pe, ident, i - 2)
                if attn0:
                    attn_pe_transpose_xn(at0, pe, ident, i + 2)
                if live("experts", i0, -1):
                    layer3(n - 1, E0 - 1)
                if run:
                    pe.wait_ge(route_step, ROUTE * (i + 1))
                    need(pe, xnT3_ready, newest(i - 1, i0 - 1, "pool"))
                    layer1(n + 1, i, par, 1)
                    weights_transpose(i)
                if live("attn1", i0, -1):
                    attn_pe_aggregate(at1, pe, i - 2)
                if attn0:
                    attn_pe_project(at0, pe, i + 2)
                if run:
                    layer2(n + 1, 1)
                    layer1(n + 2, i, par, 2)
                    pe.wait_ge(wpT_ready, i + 1)
                    spread_weights(n, par, 0)
                    bias3(i, par)
                if attn0:
                    pe.wait_ge(mask_ready, i + 3)
                    attn_pe_scores(at0, pe, identb, mask, i + 2)
                if run:
                    layer3(n, 0)
                    spread_weights(n + 1, par, 1)
                if attn1:
                    attn_pe_transpose_xn(at1, pe, ident, i - 1)
                if run:
                    layer2(n + 2, 2)
                    layer1(n + 3, i, par, 3)
                if route:
                    route_transpose(i, i0)
                if run:
                    layer3(n + 1, 1)
                    spread_weights(n + 2, par, 2)
                if attn1:
                    attn_pe_project(at1, pe, i - 1)
                if run:
                    layer2(n + 3, 3)
                    layer1(n + 4, i, par, 4)
                if route:
                    route_hidden(i + 1, 1 - par)
                if run:
                    layer3(n + 2, 2)
                    spread_weights(n + 3, par, 3)
                if attn1:
                    attn_pe_scores(at1, pe, identb, mask, i - 1)
                if attn0:
                    attn_pe_transpose_probs(at0, pe, ident, i + 2)
                if run:
                    layer2(n + 4, 4)
                    layer1(n + 5, i, par, 5)
                if route:
                    route_logits(i + 1)
                if run:
                    layer3(n + 3, 3)
                    spread_weights(n + 4, par, 4)
                if attn0:
                    attn_pe_aggregate(at0, pe, i + 2)
                if run:
                    layer2(n + 5, 5)
                if live("experts", i0, 1):
                    pe.wait_ge(xnTl_ready, i + 2)
                    layer1(n + 6, i + 1, 1 - par, 0)
                if run:
                    layer3(n + 4, 4)
                    spread_weights(n + 5, par, 5)
                if pool:
                    pool_transpose(i, i0)

            rounds(pe, body)

            pe.wait_ge(late_loaded, LATE)
            pe.wait_ge(xnT3_ready, N)
            pe.matmul(b_misc[0:NG, 0:E1], msum[:, :], wr[:, :], start=True, stop=True).then_inc(head_pe, 1)
            pe.wait_ge(head_dve, 6)
            pe.matmul(b_misc[0:NG, 0:E1], ones[0:NG, 0:NG], hd[:, 4, :], start=True, stop=True)\
                .then_inc(head_pe, 1)
            pe.wait_ge(head_diag, 4)
            pe.matmul(bank[0][:, 0:4 * NG], ones[0:NG, :], diag[:, :, :].rearrange("p a b -> p (a b)"),
                      start=True, stop=True).then_inc(head_pe, 1)
            pe.wait_ge(head_dve, 25)
            pe.transpose(b_misc[0:E1, 0:NG], hd[:, 2, :], ident[0:NG, 0:NG]).then_inc(head_pe, 1)
            pe.wait_ge(gw_ready, 1)

            def up(m, t):
                pe.wait_ge(w1c_ready, m + 1)
                need(pe, gelu_ready, m - 3)
                for k in range(2):
                    for c in range(FC):
                        j = FC * k + c
                        last = pe.matmul(up_bank[t][:, j * P:(j + 1) * P], w1c[t][:, k, c * P:(c + 1) * P],
                                         xnT3[:, bass.ds(m * P, P)], start=True, stop=True)
                last.then_inc(up_done, 1)

            def down(m, gpar, t):
                pe.wait_ge(gelu_ready, m + 1)
                pe.wait_ge(w2c_ready, m + 1)
                for j in range(2 * FC):
                    last = pe.matmul(bank[2 + gpar][:, t * P:(t + 1) * P], hid[t][:, j * P:(j + 1) * P],
                                     w2c[t][:, j * P:(j + 1) * P], start=(j == 0), stop=(j == 2 * FC - 1))
                last.then_inc(down_done, 1)

            def group(g, g0, gpar):
                for t in range(GG):
                    up(GG * g + t, t)
                    if t < 2 and g0 > 0:
                        down(GG * g + t - 2, 1 - gpar, t + 2)
                    if t == 2:
                        need(pe, sum_ready, g - 1)
                    if t >= 2:
                        down(GG * g + t - 2, gpar, t - 2)

            for g in range(4):
                group(g, g, g % 2)
                if g == 0:
                    pe.wait_ge(head_dve, 26)
                    pe.matmul(b_misc[0:NG, 0:P], wdT[:, :], B2[:, :], start=True, stop=True).then_inc(head_pe, 1)
            with pe.Fori(4, N - 1, 2) as g:
                group(g, 4, 0)
                group(g + 1, 5, 1)
            down(NG - 2, 1, GG - 2)
            down(NG - 1, 1, GG - 1)


_INS = ["x", "adj", "L0_gnn_W", "L0_gnn_a", "L0_ffn_router_w1", "L0_ffn_router_b1", "L0_ffn_router_w2",
        "L0_ffn_router_b2", "L0_ffn_expert_w1", "L0_ffn_expert_b1", "L0_ffn_expert_w2", "L0_ffn_expert_b2",
        "L0_ffn_expert_w3", "L0_ffn_expert_b3", "L1_gnn_W", "L1_gnn_a", "L1_ffn_Wr", "L1_ffn_br",
        "L1_ffn_W1", "L1_ffn_b1", "L1_ffn_W2", "L1_ffn_b2", "L1_ffn_gamma", "L1_ffn_beta"]


def kernel(**inputs):
    import numpy as _np
    import concourse.bacc as _bacc
    from concourse.bass_utils import run_bass_kernel_spmd as _run

    nc = _bacc.Bacc("TRN2", target_bir_lowering=False, num_devices=1)
    arrays, args = {}, {}
    for name in _INS:
        a = _np.ascontiguousarray(inputs[name])
        arrays["in_" + name] = a
        args[name] = nc.dram_tensor("in_" + name, a.shape, mybir.dt.from_np(a.dtype), kind="ExternalInput").ap()
    out = nc.dram_tensor("out_0", (NG, P, P), F32, kind="ExternalOutput").ap()
    build(nc, args, out)
    r = _run(nc, [arrays], core_ids=[0])
    return r.results[0]["out_0"]
```
